# Optimizing a Trainium2 kernel written in Bass

```python
import numpy as np
import jax
import jax.numpy as jnp

def _softmax(x, axis=-1):
    return jax.nn.softmax(x, axis=axis)

def _gelu(x):
    return jax.nn.gelu(x, approximate=True)

def _silu(x):
    return jax.nn.silu(x)

def _sigmoid(x):
    return jax.nn.sigmoid(x)

def _layernorm(x, axis=-1, eps=1e-05):
    m = jnp.mean(x, axis=axis, keepdims=True)
    v = jnp.var(x, axis=axis, keepdims=True)
    return (x - m) / jnp.sqrt(v + eps)

def _scatter_add(tgt, idx, src, axis=0):
    return tgt.at[idx].add(src)

def _segment_sum(src, seg, n):
    return jax.ops.segment_sum(src, seg, n)
kernel_name = 'mk_gnn_resnorm_d4_gnn_r32_3f945f'

def setup_inputs(seed: int=0):
    np.random.seed(seed)
    _w = jnp.asarray

    def _rec_inputs():
        import jax
        import jax.numpy as jnp
        _gk = jax.random.key(seed)
        x = -0.000202 + 1 * jax.random.normal(jax.random.fold_in(_gk, 1), (3125, 64), jnp.float32)
        src = jax.random.randint(jax.random.fold_in(_gk, 2), (50000,), 0, 3125, jnp.int32)
        dst = jnp.minimum((3125 * jax.random.uniform(jax.random.fold_in(_gk, 3), (50000,)) ** 2.0).astype(jnp.int32), 99999)
        _o = jnp.argsort(dst, stable=True)
        src = src[_o]
        dst = dst[_o]
        edge_attr_3 = 0.00117183 + 1.0004 * jax.random.normal(jax.random.fold_in(_gk, 12), (50000, 3), jnp.float32)
        edge_type_32 = jax.random.randint(jax.random.fold_in(_gk, 14), (50000,), 0, 32, jnp.int32)
        return (x, src, dst, edge_attr_3, edge_type_32)
    x, src, dst, edge_attr_3, edge_type_32 = _rec_inputs()

    def _L0_gnn_setup():
        import jax, jax.numpy as jnp
        import numpy as np
        N_NODES = 3125
        NUM_LAYERS = 2
        key = jax.random.key(seed)
        k1, k2 = jax.random.split(key)
        x = jax.random.normal(k1, (N_NODES, 64), dtype=jnp.float32)
        edge_index = jax.random.randint(k2, (2, 100000), 0, N_NODES, dtype=jnp.int64)
        alpha = jnp.full((NUM_LAYERS + 1,), 1.0 / (NUM_LAYERS + 1), dtype=jnp.float32)
        return {'x': x, 'edge_index': edge_index, 'alpha': alpha}
    _L0_gnn_all = _L0_gnn_setup()
    _L0_gnn_in = {k: v for k, v in _L0_gnn_all.items() if k in ('alpha',)}
    del _L0_gnn_all

    def _L1_gnn_setup():
        import jax, jax.numpy as jnp
        import numpy as np
        NUM_NODES = 50000
        NUM_EDGES = 25000
        EMBED = 64
        HEADS = 4
        NEG_SLOPE = 0.2

        def gat_conv(x, src, dst, W, a_src, a_dst, bias, heads, out_dim):
            n = x.shape[0]
            h = (x @ W).reshape(n, heads, out_dim)
            al_src = jnp.einsum('nhd,hd->nh', h, a_src)
            al_dst = jnp.einsum('nhd,hd->nh', h, a_dst)
            e = al_src[src] + al_dst[dst]
            e = jnp.where(e > 0, e, NEG_SLOPE * e)
            m = jax.ops.segment_max(e, dst, num_segments=n)
            m = jax.lax.stop_gradient(jnp.where(jnp.isfinite(m), m, 0.0))
            ex = jnp.exp(e - m[dst])
            denom = jax.ops.segment_sum(ex, dst, num_segments=n)
            alpha = ex / (denom[dst] + 1e-16)
            msg = h[src] * alpha[:, :, None]
            out = jax.ops.segment_sum(msg, dst, num_segments=n)
            return out.reshape(n, heads * out_dim) + bias
        key = jax.random.key(seed)
        ks = jax.random.split(key, 12)
        x = jax.random.normal(ks[0], (NUM_NODES, EMBED), dtype=jnp.float32)
        edge_index = jax.random.randint(ks[1], (2, NUM_EDGES), 0, NUM_NODES, dtype=jnp.int64)
        s1 = 1.0 / np.sqrt(EMBED)
        s2 = 1.0 / np.sqrt(EMBED * HEADS)
        W1 = jax.random.normal(ks[2], (EMBED, HEADS * EMBED), dtype=jnp.float32) * s1
        a_src1 = jax.random.normal(ks[3], (HEADS, EMBED), dtype=jnp.float32) * s1
        a_dst1 = jax.random.normal(ks[4], (HEADS, EMBED), dtype=jnp.float32) * s1
        b1 = jnp.zeros((HEADS * EMBED,), dtype=jnp.float32)
        W2 = jax.random.normal(ks[5], (HEADS * EMBED, EMBED), dtype=jnp.float32) * s2
        a_src2 = jax.random.normal(ks[6], (1, EMBED), dtype=jnp.float32) * s2
        a_dst2 = jax.random.normal(ks[7], (1, EMBED), dtype=jnp.float32) * s2
        b2 = jnp.zeros((EMBED,), dtype=jnp.float32)
        return {'x': x, 'edge_index': edge_index, 'W1': W1, 'a_src1': a_src1, 'a_dst1': a_dst1, 'b1': b1, 'W2': W2, 'a_src2': a_src2, 'a_dst2': a_dst2, 'b2': b2}
    _L1_gnn_all = _L1_gnn_setup()
    _L1_gnn_in = {k: v for k, v in _L1_gnn_all.items() if k in ('W1', 'a_src1', 'a_dst1', 'b1', 'W2', 'a_src2', 'a_dst2', 'b2')}
    del _L1_gnn_all

    def _L2_gnn_setup():
        import jax, jax.numpy as jnp
        import numpy as np
        N_NODES = 50000
        N_EDGES = 25000
        IN_F = 64
        OUT_F = 64
        N_REL = 32
        N_BASES = 30
        key = jax.random.key(seed)
        ks = jax.random.split(key, 6)
        x = jax.random.normal(ks[0], (N_NODES, IN_F), dtype=jnp.float32)
        edge_index = jax.random.randint(ks[1], (2, N_EDGES), 0, N_NODES, dtype=jnp.int64)
        edge_type = jax.random.randint(ks[2], (N_EDGES,), 0, N_REL, dtype=jnp.int64)
        basis = jax.random.normal(ks[3], (N_BASES, IN_F, OUT_F), dtype=jnp.float32) * 0.01
        coeff = jax.random.normal(ks[4], (N_REL, N_BASES), dtype=jnp.float32) * 0.01
        self_weight = jax.random.normal(ks[5], (IN_F, OUT_F), dtype=jnp.float32) * 0.01
        bias = jnp.zeros((OUT_F,), dtype=jnp.float32)
        return {'x': x, 'edge_index': edge_index, 'edge_type': edge_type, 'num_nodes': N_NODES, 'basis': basis, 'coeff': coeff, 'self_weight': self_weight, 'bias': bias}
    _L2_gnn_all = _L2_gnn_setup()
    _L2_gnn_in = {k: v for k, v in _L2_gnn_all.items() if k in ('basis', 'coeff', 'self_weight', 'bias')}
    del _L2_gnn_all

    def _L3_gnn_setup():
        import jax, jax.numpy as jnp
        import numpy as np
        M = 50000
        E = 25000
        C_IN = 64
        C_OUT = 64
        DIM = 3
        RADIUS = 1.0
        EPS = 1e-05

        def layer_norm(x, g, b):
            mu = jnp.mean(x, axis=-1, keepdims=True)
            var = jnp.mean((x - mu) ** 2, axis=-1, keepdims=True)
            return (x - mu) * jax.lax.rsqrt(var + EPS) * g + b
        key = jax.random.key(seed)
        ks = jax.random.split(key, 12)
        inv = 1.0 / np.sqrt(C_OUT)
        return {'source': jax.random.randint(ks[0], (E,), 0, M), 'target': jax.random.randint(ks[1], (E,), 0, M), 'features': jax.random.normal(ks[2], (M, C_IN), dtype=jnp.float32), 'hood_coords': jax.random.normal(ks[3], (E, DIM), dtype=jnp.float32), 'Wd1': jax.random.normal(ks[4], (DIM, C_OUT), dtype=jnp.float32) / np.sqrt(DIM), 'bd1': jnp.zeros((C_OUT,), jnp.float32), 'g1': jnp.ones((C_OUT,), jnp.float32), 'b1': jnp.zeros((C_OUT,), jnp.float32), 'Wd2': jax.random.normal(ks[5], (C_OUT, C_OUT), dtype=jnp.float32) * inv, 'bd2': jnp.zeros((C_OUT,), jnp.float32), 'g2': jnp.ones((C_OUT,), jnp.float32), 'b2': jnp.zeros((C_OUT,), jnp.float32), 'W1': jax.random.normal(ks[6], (C_IN, C_OUT), dtype=jnp.float32) / np.sqrt(C_IN), 'W2': jax.random.normal(ks[7], (C_IN, C_OUT), dtype=jnp.float32) / np.sqrt(C_IN), 'W3': jax.random.normal(ks[8], (C_IN, C_OUT), dtype=jnp.float32) / np.sqrt(C_IN)}
    _L3_gnn_all = _L3_gnn_setup()
    _L3_gnn_in = {k: v for k, v in _L3_gnn_all.items() if k in ('Wd1', 'bd1', 'g1', 'b1', 'Wd2', 'bd2', 'g2', 'b2', 'W1', 'W2', 'W3')}
    del _L3_gnn_all
    return {'x': x, 'src': src, 'dst': dst, 'edge_attr_3': edge_attr_3, 'edge_type_32': edge_type_32, 'L0_gnn_alpha': _L0_gnn_in['alpha'], 'L1_gnn_W1': _L1_gnn_in['W1'], 'L1_gnn_a_src1': _L1_gnn_in['a_src1'], 'L1_gnn_a_dst1': _L1_gnn_in['a_dst1'], 'L1_gnn_b1': _L1_gnn_in['b1'], 'L1_gnn_W2': _L1_gnn_in['W2'], 'L1_gnn_a_src2': _L1_gnn_in['a_src2'], 'L1_gnn_a_dst2': _L1_gnn_in['a_dst2'], 'L1_gnn_b2': _L1_gnn_in['b2'], 'L2_gnn_basis': _L2_gnn_in['basis'], 'L2_gnn_coeff': _L2_gnn_in['coeff'], 'L2_gnn_self_weight': _L2_gnn_in['self_weight'], 'L2_gnn_bias': _L2_gnn_in['bias'], 'L3_gnn_Wd1': _L3_gnn_in['Wd1'], 'L3_gnn_bd1': _L3_gnn_in['bd1'], 'L3_gnn_g1': _L3_gnn_in['g1'], 'L3_gnn_b1': _L3_gnn_in['b1'], 'L3_gnn_Wd2': _L3_gnn_in['Wd2'], 'L3_gnn_bd2': _L3_gnn_in['bd2'], 'L3_gnn_g2': _L3_gnn_in['g2'], 'L3_gnn_b2': _L3_gnn_in['b2'], 'L3_gnn_W1': _L3_gnn_in['W1'], 'L3_gnn_W2': _L3_gnn_in['W2'], 'L3_gnn_W3': _L3_gnn_in['W3']}

def reference(x, src, dst, edge_attr_3, edge_type_32, L0_gnn_alpha, L1_gnn_W1, L1_gnn_a_src1, L1_gnn_a_dst1, L1_gnn_b1, L1_gnn_W2, L1_gnn_a_src2, L1_gnn_a_dst2, L1_gnn_b2, L2_gnn_basis, L2_gnn_coeff, L2_gnn_self_weight, L2_gnn_bias, L3_gnn_Wd1, L3_gnn_bd1, L3_gnn_g1, L3_gnn_b1, L3_gnn_Wd2, L3_gnn_bd2, L3_gnn_g2, L3_gnn_b2, L3_gnn_W1, L3_gnn_W2, L3_gnn_W3):
    import jax
    import jax.numpy as jnp

    def _L0_gnn_ref(x, edge_index, alpha):
        import jax, jax.numpy as jnp
        import numpy as np
        N_NODES = 3125
        NUM_LAYERS = 2
        row, col = (edge_index[0], edge_index[1])
        n = x.shape[0]
        ew = jnp.ones(row.shape[0], dtype=x.dtype)
        deg = jax.ops.segment_sum(ew, col, num_segments=n)
        dis = jnp.where(deg > 0, jax.lax.rsqrt(jnp.maximum(deg, 1.0)), 0.0).astype(x.dtype)
        norm = dis[row] * ew * dis[col]
        out = x * alpha[0]
        for i in range(NUM_LAYERS):
            msg = x[row] * norm[:, None]
            x = jax.ops.segment_sum(msg, col, num_segments=n)
            out = out + x * alpha[i + 1]
        return out

    def _L1_gnn_ref(x, edge_index, W1, a_src1, a_dst1, b1, W2, a_src2, a_dst2, b2):
        import jax, jax.numpy as jnp
        import numpy as np
        NUM_NODES = 50000
        NUM_EDGES = 25000
        EMBED = 64
        HEADS = 4
        NEG_SLOPE = 0.2

        def gat_conv(x, src, dst, W, a_src, a_dst, bias, heads, out_dim):
            n = x.shape[0]
            h = (x @ W).reshape(n, heads, out_dim)
            al_src = jnp.einsum('nhd,hd->nh', h, a_src)
            al_dst = jnp.einsum('nhd,hd->nh', h, a_dst)
            e = al_src[src] + al_dst[dst]
            e = jnp.where(e > 0, e, NEG_SLOPE * e)
            m = jax.ops.segment_max(e, dst, num_segments=n)
            m = jax.lax.stop_gradient(jnp.where(jnp.isfinite(m), m, 0.0))
            ex = jnp.exp(e - m[dst])
            denom = jax.ops.segment_sum(ex, dst, num_segments=n)
            alpha = ex / (denom[dst] + 1e-16)
            msg = h[src] * alpha[:, :, None]
            out = jax.ops.segment_sum(msg, dst, num_segments=n)
            return out.reshape(n, heads * out_dim) + bias
        n = x.shape[0]
        loops = jnp.arange(n, dtype=edge_index.dtype)
        src = jnp.concatenate([edge_index[0], loops])
        dst = jnp.concatenate([edge_index[1], loops])
        h = gat_conv(x, src, dst, W1, a_src1, a_dst1, b1, HEADS, EMBED)
        h = jax.nn.relu(h)
        out = gat_conv(h, src, dst, W2, a_src2, a_dst2, b2, 1, EMBED)
        return out

    def _L2_gnn_ref(x, edge_index, edge_type, num_nodes, basis, coeff, self_weight, bias):
        import jax, jax.numpy as jnp
        import numpy as np
        N_NODES = 50000
        N_EDGES = 25000
        IN_F = 64
        OUT_F = 64
        N_REL = 32
        N_BASES = 30
        rel_weight = jnp.einsum('rb,bio->rio', coeff, basis)
        source_idx = edge_index[0]
        target_idx = edge_index[1]
        src_feats = x[source_idx]

        def body(out, rw_r):
            rw, r = rw_r
            mask = (edge_type == r).astype(jnp.float32)
            msg = src_feats @ rw * mask[:, None]
            return (out.at[target_idx].add(msg), None)
        out0 = jnp.zeros((num_nodes, rel_weight.shape[-1]), dtype=jnp.float32)
        out, _ = jax.lax.scan(body, out0, (rel_weight, jnp.arange(rel_weight.shape[0])))
        in_degree = jnp.zeros((num_nodes,), dtype=jnp.float32).at[target_idx].add(1.0)
        in_degree = jnp.maximum(in_degree, 1.0)
        out = out / in_degree[:, None]
        out = out + x @ self_weight + bias
        return out

    def _L3_gnn_ref(source, target, features, hood_coords, Wd1, bd1, g1, b1, Wd2, bd2, g2, b2, W1, W2, W3):
        import jax, jax.numpy as jnp
        import numpy as np
        M = 50000
        E = 25000
        C_IN = 64
        C_OUT = 64
        DIM = 3
        RADIUS = 1.0
        EPS = 1e-05

        def layer_norm(x, g, b):
            mu = jnp.mean(x, axis=-1, keepdims=True)
            var = jnp.mean((x - mu) ** 2, axis=-1, keepdims=True)
            return (x - mu) * jax.lax.rsqrt(var + EPS) * g + b
        m = features.shape[0]
        x = hood_coords / RADIUS
        d = jax.nn.gelu(layer_norm(x @ Wd1 + bd1, g1, b1), approximate=False)
        d = jax.nn.gelu(layer_norm(d @ Wd2 + bd2, g2, b2), approximate=False)
        w1 = features @ W1
        w2 = features @ W2
        w3 = features @ W3
        logits = w1[target] - w2[source] + d
        seg_max = jax.ops.segment_max(logits, target, num_segments=m)
        seg_max = jnp.where(jnp.isfinite(seg_max), seg_max, 0.0)
        e = jnp.exp(logits - seg_max[target])
        denom = jax.ops.segment_sum(e, target, num_segments=m)
        a = e / denom[target]
        out = jax.ops.segment_sum(a * (w3[source] + d), target, num_segments=m)
        return out
    edge_index = jnp.stack([src, dst])
    x = _layernorm(x + _L0_gnn_ref(x, edge_index, L0_gnn_alpha), axis=-1)
    x = _layernorm(x + _L1_gnn_ref(x, edge_index, L1_gnn_W1, L1_gnn_a_src1, L1_gnn_a_dst1, L1_gnn_b1, L1_gnn_W2, L1_gnn_a_src2, L1_gnn_a_dst2, L1_gnn_b2), axis=-1)
    x = _layernorm(x + _L2_gnn_ref(x, edge_index, edge_type_32, 3125, L2_gnn_basis, L2_gnn_coeff, L2_gnn_self_weight, L2_gnn_bias), axis=-1)
    x = _layernorm(x + _L3_gnn_ref(src, dst, x, edge_attr_3, L3_gnn_Wd1, L3_gnn_bd1, L3_gnn_g1, L3_gnn_b1, L3_gnn_Wd2, L3_gnn_bd2, L3_gnn_g2, L3_gnn_b2, L3_gnn_W1, L3_gnn_W2, L3_gnn_W3), axis=-1)
    return x

_drawn_inputs = setup_inputs


def setup_inputs(seed=0):
    import zlib

    import numpy as np

    out = dict(_drawn_inputs(seed))
    spreads = {'L0_gnn_alpha': (0.3333333432674408, 0.6),
     'L1_gnn_b1': (0.0, 0.1),
     'L1_gnn_b2': (0.0, 0.1),
     'L2_gnn_bias': (0.0, 0.1),
     'L3_gnn_bd1': (0.0, 0.1),
     'L3_gnn_g1': (1.0, 0.2),
     'L3_gnn_b1': (0.0, 0.1),
     'L3_gnn_bd2': (0.0, 0.1),
     'L3_gnn_g2': (1.0, 0.2),
     'L3_gnn_b2': (0.0, 0.1)}
    factors = {'L1_gnn_a_dst1': 4.504,
     'L1_gnn_a_src2': 8.0,
     'L1_gnn_a_dst2': 23.572,
     'L2_gnn_basis': 8.0,
     'L2_gnn_coeff': 8.0,
     'L3_gnn_W1': 64.0}
    for name, (base, spread) in spreads.items():
        noise = np.random.default_rng([zlib.crc32(name.encode()), seed]).standard_normal(out[name].shape)
        drawn = base * np.exp(spread * noise) if base else spread * noise
        out[name] = jnp.asarray(drawn.astype(out[name].dtype))
    for name, factor in factors.items():
        out[name] = (out[name] * factor).astype(out[name].dtype)
    return out
```

```python
import concourse.bass as bass
from concourse import mybir
from contextlib import ExitStack, contextmanager

FP32 = mybir.dt.float32
I32 = mybir.dt.int32
ALU = mybir.AluOpType
ACT = mybir.ActivationFunctionType
AX = mybir.AxisListType

P = 128
N = 3125
F = 64
E = 50000
REL = 32
NBASE = 30
HEADS = 4
NB = -(-N // P)
NFULL = N // P
NREM = N - NFULL * P
T = -(-E // P)
TG = -(-T // P)
SLOTS = -(-(T + NB - 1) // 16) * 16
SG = SLOTS // 4
CH = 4
CW = CH * P
ITERS = SLOTS // (2 * CH)
BANK = 512
BIG = 1.0e30
EPS = 1.0e-5


class Link:

    def __init__(self, eng, sem, per=0):
        self.eng, self.sem, self.per, self.base, self.n = eng, sem, per, 0, 0

    def turn(self, it):
        self.base, self.n = it * self.per, 0

    def __call__(self, ins):
        self.n += 1
        ins.then_inc(self.sem, 1)
        self.eng.wait_ge(self.sem, self.base + self.n)


@contextmanager
def semaphore(nc, name):
    yield nc.alloc_semaphore(name=name)


class Space:
    pass


def bcast_rows(ap, parts):
    return ap.rearrange("(o n) -> o n", o=1).broadcast_to([parts, ap.shape[0]])


def node_rows(tab):
    return tab.rearrange("(b p) c -> p b c", p=P)


def build_slots(nc, K, dst, src, edge_type, edge_attr):
    ctx = ExitStack()
    with ctx:
        def sb(name, shape, dt=FP32):
            return ctx.enter_context(nc.sbuf_tensor(name, shape, dt))

        def sem(name):
            return ctx.enter_context(semaphore(nc, name))

        NARR = 5
        dst_i, prev_i, next_i, src_i, typ_i = (sb(n, [P, TG, P], I32) for n in
                                               ("dst_i", "prev_i", "next_i", "src_i", "typ_i"))
        raw = sb("raw", [P, TG, NARR, P])
        att = sb("att", [P, TG, 3 * P])
        thr = sb("thr", [P, NB - 1])
        cmp0 = sb("cmp0", [P, TG, NB - 1])
        cmp1 = sb("cmp1", [P, TG, NB - 1])
        bmin, bmax, dmax, live, cnt, cum, cumex, bmc = (sb(n, [P, TG]) for n in
                                                       ("bmin", "bmax", "dmax", "live", "cnt", "cum", "cumex", "bmc"))
        bmcb = sb("bmcb", [P, TG, P])
        tri = sb("tri", [P, P])
        ones = sb("ones_sq", [P, P])
        iota_s = sb("iota_s", [P, SLOTS])
        iota_g = sb("iota_g", [P, 4])
        own = sb("own", [P, TG, SLOTS])
        ge = sb("ge", [P, SLOTS])
        blk = sb("blk", [P, SLOTS])
        tmp = sb("tmp", [P, SLOTS])
        tmp2 = sb("tmp2", [P, SLOTS])
        rows = sb("rows", [P, 4, 2, P])
        arows = sb("arows", [P, 4, 3, P])
        bcol = sb("bcol", [P, 4])

        pads = sem("pads")
        loads = sem("edge_loads")
        iotas = sem("iotas")
        tri0 = sem("tri0")
        dve = sem("slot_dve")
        counted = sem("tiles_counted")
        cum_ready = sem("cum_ready")
        own_ready = sem("own_ready")
        slots_ready = sem("slots_ready")
        rows_ready = sem("rows_ready")
        rows_taken = sem("rows_taken")
        rows_out = sem("rows_out")
        ident0 = sem("ident0")

        block = ctx.enter_context(nc.Block())
        G3 = TG - 1
        full = T - 1 - G3 * P
        last = E - (T - 1) * P

        @block.gpsimd
        def _(pool):
            for t, v in ((dst_i, -1), (prev_i, -5), (next_i, -1), (src_i, 0), (typ_i, 0)):
                pool.memset(t[:, :, :], v).then_inc(pads, 1)
            pool.memset(att[:, :, :], 0.0).then_inc(pads, 1)
            pool.iota(thr[:, :], pattern=[[P, NB - 1]], base=P, channel_multiplier=0,
                      allow_small_or_imprecise_dtypes=True).then_inc(iotas, 1)
            pool.iota(iota_s[:, :], pattern=[[1, SLOTS]], base=0, channel_multiplier=0,
                      allow_small_or_imprecise_dtypes=True).then_inc(iotas, 1)
            pool.iota(iota_g[:, :], pattern=[[SG, 4]], base=0, channel_multiplier=1,
                      allow_small_or_imprecise_dtypes=True).then_inc(iotas, 1)
            pool.iota(K.iota_row[:, :], pattern=[[1, P]], base=0, channel_multiplier=0,
                      allow_small_or_imprecise_dtypes=True).then_inc(iotas, 1)
            pool.iota(K.iota_part[:, :], pattern=[[0, 1]], base=0, channel_multiplier=1,
                      allow_small_or_imprecise_dtypes=True).then_inc(iotas, 1)
            pool.memset(tri[:, :], 1.0).then_inc(tri0, 1)
            pool.memset(ones[:, :], 1.0).then_inc(tri0, 1)
            pool.memset(K.ones[:, :], 1.0).then_inc(tri0, 1)
            pool.memset(K.zeros[:, :], 0.0).then_inc(tri0, 1)
            pool.memset(K.ident[:, :], 0.0).then_inc(ident0, 1)
            pool.wait_ge(tri0, 4)
            pool.affine_select(out=tri[:, :], in_=tri[:, :], compare_op=ALU.is_ge, fill=0.0, base=0,
                               pattern=[[1, P]], channel_multiplier=-1).then_inc(iotas, 1)
            pool.wait_ge(ident0, 1)
            pool.affine_select(out=K.ident[:, :], in_=K.ident[:, :], compare_op=ALU.not_equal, fill=1.0, base=0,
                               pattern=[[-1, P]], channel_multiplier=1).then_inc(iotas, 1)

        @block.sync
        def _(sp):
            sp.wait_ge(pads, 6)
            body = G3 * P * P
            for t, a in ((dst_i, dst), (src_i, src), (typ_i, edge_type)):
                sp.dma_start(t[:, 0:G3, :], a[0:body].rearrange("(g p e) -> p g e", p=P, e=P)).then_inc(loads, 16)
                sp.dma_start(t[0:full, G3, :], a[body:body + full * P].rearrange("(p e) -> p e", e=P)).then_inc(loads, 16)
                sp.dma_start(t[full:full + 1, G3, 0:last],
                             a[E - last:E].rearrange("(o e) -> o e", o=1)).then_inc(loads, 16)
            sp.dma_start(next_i[:, 0:G3, :], dst[1:body + 1].rearrange("(g p e) -> p g e", p=P, e=P)).then_inc(loads, 16)
            sp.dma_start(next_i[0:full, G3, :],
                         dst[body + 1:body + 1 + full * P].rearrange("(p e) -> p e", e=P)).then_inc(loads, 16)
            sp.dma_start(next_i[full:full + 1, G3, 0:last - 1],
                         dst[E - last + 1:E].rearrange("(o e) -> o e", o=1)).then_inc(loads, 16)
            sp.dma_start(prev_i[0:1, 0, 1:P], dst[0:P - 1].rearrange("(o e) -> o e", o=1)).then_inc(loads, 16)
            sp.dma_start(prev_i[1:P, 0, :], dst[P - 1:P * P - 1].rearrange("(p e) -> p e", e=P)).then_inc(loads, 16)
            sp.dma_start(prev_i[:, 1:G3, :], dst[P * P - 1:body - 1].rearrange("(g p e) -> p g e", p=P, e=P)).then_inc(loads, 16)
            sp.dma_start(prev_i[0:full, G3, :],
                         dst[body - 1:body - 1 + full * P].rearrange("(p e) -> p e", e=P)).then_inc(loads, 16)
            sp.dma_start(prev_i[full:full + 1, G3, 0:last],
                         dst[E - last - 1:E - 1].rearrange("(o e) -> o e", o=1)).then_inc(loads, 16)
            sp.dma_start(att[:, 0:G3, :],
                         edge_attr[0:body, :].rearrange("(g p e) a -> p g (e a)", p=P, e=P)).then_inc(loads, 16)
            sp.dma_start(att[0:full, G3, :],
                         edge_attr[body:body + full * P, :].rearrange("(p e) a -> p (e a)", e=P)).then_inc(loads, 16)
            sp.dma_start(att[full:full + 1, G3, 0:3 * last],
                         edge_attr[E - last:E, :].rearrange("(o e) a -> o (e a)", o=1)).then_inc(loads, 16)
            for sg in range(4):
                sp.wait_ge(rows_taken, 1 + sg)
                sp.dma_start(K.dl_rows[sg * SG:(sg + 1) * SG, :], rows[0:SG, sg, 0, :]).then_inc(rows_out, 16)
                sp.dma_start(K.pen_rows[sg * SG:(sg + 1) * SG, :], rows[0:SG, sg, 1, :]).then_inc(rows_out, 16)
                for a in range(3):
                    sp.dma_start(K.attr_rows[a, sg * SG:(sg + 1) * SG, :], arows[0:SG, sg, a, :]).then_inc(rows_out, 16)
            sp.wait_ge(rows_out, 16 * 5 * 4)

        @block.vector
        def _(v):
            link = Link(v, dve)
            v.wait_ge(loads, 16 * 20)
            v.wait_ge(iotas, 7)
            link(v.tensor_copy(raw[:, :, 0, :], dst_i[:, :, :]))
            link(v.tensor_tensor(raw[:, :, 1, :], dst_i[:, :, :], prev_i[:, :, :], ALU.is_equal))
            link(v.tensor_copy(raw[:, :, 2, :], src_i[:, :, :]))
            link(v.tensor_copy(raw[:, :, 3, :], typ_i[:, :, :]))
            link(v.tensor_tensor(raw[:, :, 4, :], dst_i[:, :, :], next_i[:, :, :], ALU.not_equal))
            link(v.tensor_tensor(cmp0[:, :, :], raw[:, :, 0, 0:1].broadcast_to([P, TG, NB - 1]),
                                 thr[:, :].unsqueeze(1).broadcast_to([P, TG, NB - 1]), ALU.is_ge))
            link(v.tensor_reduce(bmin[:, :], cmp0[:, :, :], AX.X, ALU.add))
            link(v.tensor_reduce(dmax[:, :], raw[:, :, 0, :], AX.X, ALU.max))
            link(v.tensor_tensor(cmp1[:, :, :], dmax[:, :].unsqueeze(2).broadcast_to([P, TG, NB - 1]),
                                 thr[:, :].unsqueeze(1).broadcast_to([P, TG, NB - 1]), ALU.is_ge))
            link(v.tensor_reduce(bmax[:, :], cmp1[:, :, :], AX.X, ALU.add))
            link(v.tensor_scalar(live[:, :], raw[:, :, 0, 0], 0.0, None, ALU.is_ge))
            link(v.scalar_tensor_tensor(out=cnt[:, :], in0=bmax[:, :], scalar=1.0, in1=bmin[:, :],
                                        op0=ALU.add, op1=ALU.subtract))
            link(v.tensor_tensor(cnt[:, :], cnt[:, :], live[:, :], ALU.mult))
            v.sem_inc(counted, 1)
            v.wait_ge(cum_ready, 1)
            link(v.tensor_copy(cum[:, :], K.ps[:, 0:TG]))
            link(v.tensor_tensor(cumex[:, :], cum[:, :], cnt[:, :], ALU.subtract))
            link(v.tensor_tensor(bmc[:, :], bmin[:, :], cumex[:, :], ALU.subtract))
            link(v.tensor_copy(bmcb[:, :, :], bmc[:, :].unsqueeze(2).broadcast_to([P, TG, P])))
            for g in range(TG):
                link(v.tensor_scalar(ge[:, :], iota_s[:, :], cum[:, g:g + 1], None, ALU.is_ge))
                link(v.scalar_tensor_tensor(out=own[:, g, :], in0=iota_s[:, :], scalar=cumex[:, g:g + 1],
                                            in1=ge[:, :], op0=ALU.is_ge, op1=ALU.subtract))
            v.sem_inc(own_ready, 1)
            v.wait_ge(slots_ready, 5)
            link(v.tensor_tensor(blk[:, :], K.ps[:, 4 * BANK:4 * BANK + SLOTS], iota_s[:, :], ALU.add))
            link(v.tensor_scalar(blk[:, :], blk[:, :], float(NB - 1), None, ALU.min))
            link(v.tensor_copy(K.blk_i[:, :], blk[:, :]))
            link(v.scalar_tensor_tensor(out=K.dl[:, :], in0=blk[:, :], scalar=-float(P),
                                        in1=K.ps[:, 0:SLOTS], op0=ALU.mult, op1=ALU.add))
            link(v.tensor_copy(K.src_idx[:, :], K.ps[:, BANK:BANK + SLOTS]))
            link(v.tensor_copy(tmp[:, :], K.ps[:, BANK:BANK + SLOTS]))
            link(v.scalar_tensor_tensor(out=tmp2[:, :], in0=tmp[:, :], scalar=float(REL),
                                        in1=K.ps[:, 2 * BANK:2 * BANK + SLOTS], op0=ALU.mult, op1=ALU.add))
            link(v.tensor_copy(K.rel_idx[:, :], tmp2[:, :]))
            link(v.scalar_tensor_tensor(out=tmp[:, :], in0=K.dl[:, :], scalar=1.0,
                                        in1=K.ps[:, 3 * BANK:3 * BANK + SLOTS], op0=ALU.add, op1=ALU.mult))
            link(v.tensor_scalar(K.dl_end[:, :], tmp[:, :], -1.0, None, ALU.add))
            for sg in range(4):
                v.wait_ge(rows_ready, sg + 1)
                o = 5 * BANK
                link(v.tensor_tensor(bcol[0:SG, sg:sg + 1], K.ps[0:SG, o + 2 * P:o + 2 * P + 1],
                                     iota_g[0:SG, sg:sg + 1], ALU.add))
                link(v.tensor_scalar(bcol[0:SG, sg:sg + 1], bcol[0:SG, sg:sg + 1], float(NB - 1), -float(P),
                                     ALU.min, ALU.mult))
                link(v.tensor_scalar(rows[0:SG, sg, 0, :], K.ps[0:SG, o:o + P], bcol[0:SG, sg:sg + 1], None, ALU.add))
                link(v.tensor_scalar(rows[0:SG, sg, 1, :], K.ps[0:SG, o + P:o + 2 * P], -1.0, BIG, ALU.add, ALU.mult))
                o = 6 * BANK
                link(v.tensor_copy(arows[0:SG, sg, :, :], K.ps[0:SG, o:o + 3 * P].rearrange("p (e a) -> p a e", a=3)))
                v.sem_inc(rows_taken, 1)

        @block.tensor
        def _(pe):
            pe.wait_ge(counted, 1)
            for g in range(TG):
                pe.matmul(K.ps[:, g:g + 1], tri[:, :], cnt[:, g:g + 1], start=True, stop=g == 0, skip_group_check=True)
                for h in range(g):
                    ins = pe.matmul(K.ps[:, g:g + 1], ones[:, :], cnt[:, h:h + 1], start=False, stop=h == g - 1,
                                    skip_group_check=True)
            ins.then_inc(cum_ready, 1)
            pe.wait_ge(own_ready, 1)
            for b, k in enumerate((0, 2, 3, 4, None)):
                for g in range(TG):
                    lhs = bmcb[:, g, :] if k is None else raw[:, g, k, :]
                    ins = pe.matmul(K.ps[:, b * BANK:b * BANK + SLOTS], lhs, own[:, g, :], start=g == 0, stop=g == TG - 1)
                ins.then_inc(slots_ready, 1)
            for sg in range(4):
                if sg:
                    pe.wait_ge(rows_taken, sg)
                part = own[:, :, sg * SG:(sg + 1) * SG]
                for g in range(TG):
                    pe.matmul(K.ps[0:SG, 5 * BANK:5 * BANK + 2 * P], part[:, g, :],
                              raw[:, g, 0:2, :].rearrange("p k e -> p (k e)"), start=g == 0, stop=g == TG - 1)
                for g in range(TG):
                    pe.matmul(K.ps[0:SG, 5 * BANK + 2 * P:5 * BANK + 2 * P + 1], part[:, g, :], bmc[:, g:g + 1],
                              start=False, stop=g == TG - 1, skip_group_check=True)
                for g in range(TG):
                    ins = pe.matmul(K.ps[0:SG, 6 * BANK:6 * BANK + 3 * P], part[:, g, :], att[:, g, :],
                                    start=g == 0, stop=g == TG - 1)
                ins.then_inc(rows_ready, 1)


def onehot(v, out, iota_row, dl_chunk):
    return v.tensor_tensor(out, iota_row.unsqueeze(1).broadcast_to([P, CH, P]),
                           dl_chunk.unsqueeze(2).broadcast_to([P, CH, P]), ALU.is_equal)


def clear_banks(pe, K, first, count):
    for b in range(first, first + count):
        ins = pe.matmul(K.ps[:, b * BANK:(b + 1) * BANK], K.zeros[:, 0:P], K.zeros[:, :], start=True, stop=False,
                        skip_group_check=True)
    return ins


def count_degrees(nc, K):
    ctx = ExitStack()
    with ctx:
        hot = [ctx.enter_context(nc.sbuf_tensor(f"hot{k}", [P, CH, P], FP32)) for k in range(2)]
        hot_ready = ctx.enter_context(semaphore(nc, "deg_hot_ready"))
        hot_free = ctx.enter_context(semaphore(nc, "deg_hot_free"))
        deg_link = ctx.enter_context(semaphore(nc, "deg_link"))
        root_ready = ctx.enter_context(semaphore(nc, "deg_root"))
        block = ctx.enter_context(nc.Block())

        @block.vector
        def _(v):
            with v.Fori(0, ITERS) as it:
                for k in range(2):
                    v.wait_ge(hot_free, it * 2 + k + 1)
                    onehot(v, hot[k][:, :, :], K.iota_row[:, :],
                           K.dl[:, bass.ds(it * (2 * CH) + k * CH, CH)]).then_inc(hot_ready, 1)
            link = Link(v, deg_link)
            v.wait_ge(hot_free, 2 + 2 * ITERS)
            link(v.tensor_copy(K.deg[:, :], K.ps[:, 0:NB]))
            link(v.tensor_scalar(K.deg1[:, :], K.deg[:, :], 1.0, None, ALU.max))
            link(v.tensor_scalar(K.has[:, :], K.deg[:, :], 0.0, None, ALU.is_gt))
            link(v.reciprocal(K.rdeg[:, :], K.deg1[:, :]))
            v.wait_ge(root_ready, 1)
            link(v.tensor_tensor(K.dis[:, :], K.dis[:, :], K.has[:, :], ALU.mult))

        @block.scalar
        def _(act):
            act.wait_ge(deg_link, 4)
            act.activation(K.dis[:, :], K.rdeg[:, :], ACT.Sqrt).then_inc(root_ready, 1)

        @block.tensor
        def _(pe):
            clear_banks(pe, K, 0, 1).then_inc(hot_free, 2)
            with pe.Fori(0, ITERS) as it:
                for k in range(2):
                    pe.wait_ge(hot_ready, it * 2 + k + 1)
                    for j in range(CH):
                        b = pe.value_load(K.blk_i[0:1, bass.ds(it * (2 * CH) + k * CH + j, 1)], min_val=0, max_val=NB - 1)
                        ins = pe.matmul(K.ps[:, bass.ds(b, 1)], hot[k][:, j, :], K.ones[:, 0:1], start=False, stop=False,
                                        skip_group_check=True)
                    ins.then_inc(hot_free, 1)


def gather_sum(nc, K, table, index, tag):
    ctx = ExitStack()
    with ctx:
        hot = [ctx.enter_context(nc.sbuf_tensor(f"{tag}_hot{k}", [P, CH, P], FP32)) for k in range(2)]
        ring = [ctx.enter_context(nc.sbuf_tensor(f"{tag}_ring{k}", [P, CH, F], FP32)) for k in range(2)]
        idx = [ctx.enter_context(nc.sbuf_tensor(f"{tag}_idx{k}", [P, CH], I32)) for k in range(2)]
        hot_ready = ctx.enter_context(semaphore(nc, f"{tag}_hot_ready"))
        idx_ready = ctx.enter_context(semaphore(nc, f"{tag}_idx_ready"))
        rows_in = [ctx.enter_context(semaphore(nc, f"{tag}_rows_in{k}")) for k in range(2)]
        chunk_free = ctx.enter_context(semaphore(nc, f"{tag}_chunk_free"))
        block = ctx.enter_context(nc.Block())

        @block.gpsimd
        def _(pool):
            with pool.Fori(0, ITERS) as it:
                for k in range(2):
                    pool.wait_ge(chunk_free, it * 2 + k + 1)
                    pool.tensor_copy(idx[k][:, :], index[:, bass.ds(it * (2 * CH) + k * CH, CH)]).then_inc(idx_ready, 1)
                    pool.wait_ge(idx_ready, it * 2 + k + 1)
                    pool.nop(nofuse=True)
                    for j in range(CH):
                        pool.indirect_dma_start(out=ring[k][:, j, :], out_offset=None, in_=table,
                                                in_offset=bass.IndirectOffsetOnAxis(ap=idx[k][:, j:j + 1], axis=0)
                                                ).then_inc(rows_in[k], 16)

        @block.vector
        def _(v):
            with v.Fori(0, ITERS) as it:
                for k in range(2):
                    v.wait_ge(chunk_free, it * 2 + k + 1)
                    onehot(v, hot[k][:, :, :], K.iota_row[:, :],
                           K.dl[:, bass.ds(it * (2 * CH) + k * CH, CH)]).then_inc(hot_ready, 1)

        @block.tensor
        def _(pe):
            clear_banks(pe, K, 0, 4).then_inc(chunk_free, 2)
            with pe.Fori(0, ITERS) as it:
                for k in range(2):
                    pe.wait_ge(hot_ready, it * 2 + k + 1)
                    pe.wait_ge(rows_in[k], it * (16 * CH) + 16 * CH)
                    for j in range(CH):
                        b = pe.value_load(K.blk_i[0:1, bass.ds(it * (2 * CH) + k * CH + j, 1)], min_val=0, max_val=NB - 1)
                        ins = pe.matmul(K.ps[:, bass.ds(b * F, F)], hot[k][:, j, :], ring[k][:, j, :],
                                        start=False, stop=False, skip_group_check=True)
                    ins.then_inc(chunk_free, 1)


def per_node(ap, width=F):
    return ap.unsqueeze(2).broadcast_to([P, NB, width])


def per_feature(ap):
    return ap.unsqueeze(1).broadcast_to([P, NB, F])


def sums(K):
    return K.ps[:, 0:NB * F].rearrange("p (b c) -> p b c", c=F)


def layernorm_steps(v, link, K, y, out, sq, mean, var, std_wanted, std_ready):
    link(v.tensor_reduce(mean, y, AX.X, ALU.add))
    link(v.tensor_scalar(mean, mean, -1.0 / F, None, ALU.mult))
    link(v.tensor_tensor(y, y, per_node(mean), ALU.add))
    link(v.tensor_tensor(sq, y, y, ALU.mult))
    link(v.tensor_reduce(var, sq, AX.X, ALU.add))
    link(v.tensor_scalar(var, var, 1.0 / F, EPS, ALU.mult, ALU.add))
    v.sem_inc(std_wanted, 1)
    v.wait_ge(std_ready, 1)
    link(v.reciprocal(var, var))
    link(v.tensor_tensor(out, y, per_node(var), ALU.mult))


def appnp(nc, K, x_in, alpha):
    ctx = ExitStack()
    with ctx:
        scaled = ctx.enter_context(nc.sbuf_tensor("scaled", [P, NB, F], FP32))
        total = ctx.enter_context(nc.sbuf_tensor("total", [P, NB, F], FP32))
        hop = ctx.enter_context(nc.sbuf_tensor("hop", [P, NB, F], FP32))
        al = ctx.enter_context(nc.sbuf_tensor("al", [P, 3], FP32))
        mean = ctx.enter_context(nc.sbuf_tensor("mean0", [P, NB], FP32))
        var = ctx.enter_context(nc.sbuf_tensor("var0", [P, NB], FP32))

        def prepare():
            c2 = ExitStack()
            with c2:
                x_loaded = c2.enter_context(semaphore(nc, "x_loaded"))
                x_pad = c2.enter_context(semaphore(nc, "x_pad"))
                made = c2.enter_context(semaphore(nc, "a_made"))
                stored = c2.enter_context(semaphore(nc, "a_stored"))
                block = c2.enter_context(nc.Block())

                @block.sync
                def _(sp):
                    sp.wait_ge(x_pad, 1)
                    sp.dma_start(K.x[:, 0:NFULL, :], node_rows(x_in[0:NFULL * P, :])).then_inc(x_loaded, 16)
                    sp.dma_start(K.x[0:NREM, NFULL, :], x_in[NFULL * P:N, :]).then_inc(x_loaded, 16)
                    sp.dma_start(al[:, :], bcast_rows(alpha, P)).then_inc(x_loaded, 16)
                    sp.wait_ge(made, 1)
                    sp.dma_start(node_rows(K.tab64), scaled[:, :, :]).then_inc(stored, 16)
                    sp.wait_ge(stored, 16)

                @block.vector
                def _(v):
                    v.memset(K.x[:, NFULL, :], 0.0).then_inc(x_pad, 1)
                    v.wait_ge(x_loaded, 48)
                    v.tensor_tensor(scaled[:, :, :], K.x[:, :, :], per_node(K.dis[:, :]), ALU.mult).then_inc(made, 1)

        def between(second):
            c2 = ExitStack()
            with c2:
                made = c2.enter_context(semaphore(nc, f"a_made{second}"))
                steps = c2.enter_context(semaphore(nc, f"a_steps{second}"))
                stored = c2.enter_context(semaphore(nc, f"a_stored{second}"))
                wanted = c2.enter_context(semaphore(nc, f"a_wanted{second}"))
                ready = c2.enter_context(semaphore(nc, f"a_ready{second}"))
                block = c2.enter_context(nc.Block())

                @block.vector
                def _(v):
                    link = Link(v, steps)
                    link(v.tensor_tensor(hop[:, :, :], sums(K), per_node(K.dis[:, :]), ALU.mult))
                    if not second:
                        v.tensor_tensor(scaled[:, :, :], hop[:, :, :], per_node(K.dis[:, :]), ALU.mult).then_inc(made, 1)
                        link(v.tensor_scalar(total[:, :, :], K.x[:, :, :], al[:, 0:1], None, ALU.mult))
                    link(v.scalar_tensor_tensor(out=total[:, :, :], in0=hop[:, :, :], scalar=al[:, 1 + second:2 + second],
                                                in1=total[:, :, :], op0=ALU.mult, op1=ALU.add))
                    if second:
                        link(v.tensor_tensor(total[:, :, :], total[:, :, :], K.x[:, :, :], ALU.add))
                        layernorm_steps(v, link, K, total[:, :, :], K.x[:, :, :], hop[:, :, :], mean[:, :], var[:, :],
                                        wanted, ready)

                if second:
                    @block.scalar
                    def _(act):
                        act.wait_ge(wanted, 1)
                        act.activation(var[:, :], var[:, :], ACT.Sqrt).then_inc(ready, 1)
                else:
                    @block.sync
                    def _(sp):
                        sp.wait_ge(made, 1)
                        sp.dma_start(node_rows(K.tab64), scaled[:, :, :]).then_inc(stored, 16)
                        sp.wait_ge(stored, 16)

        prepare()
        gather_sum(nc, K, K.tab64, K.src_idx, "hop1")
        between(0)
        gather_sum(nc, K, K.tab64, K.src_idx, "hop2")
        between(1)


def store_out(nc, K, out):
    with semaphore(nc, "out_stored") as stored, nc.Block() as block:
        @block.sync
        def _(sp):
            sp.dma_start(node_rows(out[0:NFULL * P, :]), K.x[:, 0:NFULL, :]).then_inc(stored, 16)
            sp.dma_start(out[NFULL * P:N, :], K.x[0:NREM, NFULL, :]).then_inc(stored, 16)
            sp.wait_ge(stored, 32)



def transpose_nodes(nc, K, nodes, out, tag):
    with semaphore(nc, f"{tag}_turned") as turned, semaphore(nc, f"{tag}_taken") as taken, nc.Block() as block:
        groups = [(q, min(q + 4, NB)) for q in range(0, NB, 4)]

        @block.tensor
        def _(pe):
            for i, (lo, hi) in enumerate(groups):
                for b in range(lo, hi):
                    o = i * BANK + (b - lo) * P
                    ins = pe.transpose(K.ps[0:F, o:o + P], nodes[:, b, :], K.ident[:, :])
                ins.then_inc(turned, 1)

        @block.vector
        def _(v):
            for i, (lo, hi) in enumerate(groups):
                v.wait_ge(turned, i + 1)
                v.tensor_copy(out[:, lo * P:hi * P], K.ps[0:F, i * BANK:i * BANK + (hi - lo) * P]).then_inc(taken, 1)
            v.wait_ge(taken, len(groups))


def project(nc, K, xT, w, cols, out, tag):
    per = BANK // cols
    groups = [(q, min(q + per, NB)) for q in range(0, NB, per)]
    with semaphore(nc, f"{tag}_made") as made, semaphore(nc, f"{tag}_copied") as copied, nc.Block() as block:
        @block.tensor
        def _(pe):
            for i, (lo, hi) in enumerate(groups):
                if i >= 8:
                    pe.wait_ge(copied, i - 7)
                for b in range(lo, hi):
                    o = (i % 8) * BANK + (b - lo) * cols
                    ins = pe.matmul(K.ps[:, o:o + cols], xT[:, b * P:(b + 1) * P], w, start=True, stop=True,
                                    skip_group_check=True)
                ins.then_inc(made, 1)

        @block.vector
        def _(v):
            for i, (lo, hi) in enumerate(groups):
                v.wait_ge(made, i + 1)
                o = (i % 8) * BANK
                v.tensor_copy(out[:, lo:hi, :], K.ps[:, o:o + (hi - lo) * cols].rearrange("p (b c) -> p b c", c=cols)
                              ).then_inc(copied, 1)
            v.wait_ge(copied, len(groups))


def store_table(nc, K, table, pieces, tag):
    with semaphore(nc, f"{tag}_stored") as stored, nc.Block() as block:
        @block.sync
        def _(sp):
            for col, width, ap in pieces:
                sp.dma_start(node_rows(table)[:, :, col:col + width], ap).then_inc(stored, 16)
            sp.wait_ge(stored, 16 * len(pieces))


def attention(nc, K, H, table, x, als, ald, z, tag):
    ctx = ExitStack()
    with ctx:
        GW = F + H
        HP = min(H, 2)

        def sb(name, shape, dt=FP32):
            return ctx.enter_context(nc.sbuf_tensor(f"{tag}_{name}", shape, dt))

        kept = sb("kept", [P, SLOTS, GW])
        hot = [sb(f"hot{k}", [P, CH, P]) for k in range(2)]
        spread = sb("spread", [P, NB, 2, H])
        selfw = sb("selfw", [P, NB, H])
        t0, t1 = sb("t0", [P, NB, H]), sb("t1", [P, NB, H])
        weight = sb("weight", [P, SLOTS, H])

        def gather_and_max():
            c = ExitStack()
            with c:
                def sb2(name, shape, dt=FP32):
                    return c.enter_context(nc.sbuf_tensor(f"{tag}_{name}", shape, dt))

                def sem(name):
                    return c.enter_context(semaphore(nc, f"{tag}_{name}"))

                ring = [sb2(f"ring{k}", [P, CH, GW]) for k in range(2)]
                idx = [sb2(f"idx{k}", [P, CH], I32) for k in range(2)]
                pen = [sb2(f"pen{k}", [H, CW]) for k in range(2)]
                run = [sb2(f"run{k}", [H, CW]) for k in range(2)]
                mx = [sb2(f"mx{k}", [P, CH * H]) for k in range(2)]
                idx_ready, hot_ready, chunk_free = sem("idx_ready"), sem("hot_ready"), sem("chunk_free")
                rows_in = [sem(f"rows_in{k}") for k in range(2)]
                pen_in = [sem(f"pen_in{k}") for k in range(2)]
                rows_kept, turned, scanned, back, mx_ready, start = (sem(n) for n in (
                    "rows_kept", "turned", "scanned", "back", "mx_ready", "start"))
                block = c.enter_context(nc.Block())

                @block.gpsimd
                def _(pool):
                    with pool.Fori(0, ITERS) as it:
                        for k in range(2):
                            pool.wait_ge(chunk_free, it * 2 + k + 1)
                            pool.wait_ge(rows_kept, it * 2 + k + 1)
                            pool.tensor_copy(idx[k][:, :], K.src_idx[:, bass.ds(it * (2 * CH) + k * CH, CH)]
                                             ).then_inc(idx_ready, 1)
                            pool.wait_ge(idx_ready, it * 2 + k + 1)
                            pool.nop(nofuse=True)
                            for j in range(CH):
                                pool.indirect_dma_start(out=ring[k][:, j, :], out_offset=None, in_=table,
                                                        in_offset=bass.IndirectOffsetOnAxis(ap=idx[k][:, j:j + 1], axis=0)
                                                        ).then_inc(rows_in[k], 16)

                @block.sync
                def _(sp):
                    with sp.Fori(0, ITERS) as it:
                        for k in range(2):
                            sp.wait_ge(scanned, it * 2 + k + 1)
                            rows = K.pen_rows[bass.ds(it * (2 * CH) + k * CH, CH), :]
                            sp.dma_start(pen[k][:, :], bcast_chunk(rows, H)).then_inc(pen_in[k], 16)

                @block.scalar
                def _(act):
                    act.sem_inc(rows_kept, 2)
                    with act.Fori(0, ITERS) as it:
                        for k in range(2):
                            act.wait_ge(rows_in[k], it * (16 * CH) + 16 * CH)
                            act.copy(kept[:, bass.ds(it * (2 * CH) + k * CH, CH), :], ring[k][:, :, :]).then_inc(rows_kept, 1)
                            act.wait_ge(back, it * 2 + k + 1)
                            act.copy(mx[k][:, :], K.ps[:, (3 + k) * BANK:(3 + k) * BANK + CH * H]).then_inc(mx_ready, 1)

                @block.vector
                def _(v):
                    v.memset(run[1][:, :], -BIG).then_inc(start, 1)
                    v.wait_ge(start, 1)
                    v.sem_inc(scanned, 2)
                    with v.Fori(0, ITERS) as it:
                        for k in range(2):
                            v.wait_ge(chunk_free, it * 2 + k + 1)
                            onehot(v, hot[k][:, :, :], K.iota_row[:, :],
                                   K.dl_end[:, bass.ds(it * (2 * CH) + k * CH, CH)]).then_inc(hot_ready, 1)
                            v.wait_ge(pen_in[k], it * 16 + 16)
                            v.wait_ge(turned, it * 2 + k + 1)
                            v.wait_ge(scanned, it * 2 + k + 2)
                            v.tensor_tensor_scan(run[k][:, :], pen[k][:, :], K.ps[0:H, (1 + k) * BANK:(2 + k) * BANK],
                                                 run[1 - k][:, CW - 1:CW], ALU.add, ALU.max).then_inc(scanned, 1)

                @block.tensor
                def _(pe):
                    clear_banks(pe, K, 0, 1).then_inc(chunk_free, 2)
                    with pe.Fori(0, ITERS) as it:
                        for k in range(2):
                            pe.wait_ge(rows_in[k], it * (16 * CH) + 16 * CH)
                            pe.wait_ge(scanned, it * 2 + k + 1)
                            pe.nop(nofuse=True)
                            for j in range(CH):
                                o = (1 + k) * BANK + j * P
                                ins = pe.transpose(K.ps[0:H, o:o + P], ring[k][:, j, F:GW], K.ident[:, :])
                            ins.then_inc(turned, 1)
                            pe.wait_ge(scanned, it * 2 + k + 3)
                            pe.nop(nofuse=True)
                            for j in range(CH):
                                o = (3 + k) * BANK + j * H
                                ins = pe.transpose(K.ps[:, o:o + H], run[k][:, j * P:(j + 1) * P], K.ident[0:H, 0:H])
                            ins.then_inc(back, 1)
                            pe.wait_ge(mx_ready, it * 2 + k + 1)
                            pe.wait_ge(hot_ready, it * 2 + k + 1)
                            for j in range(CH):
                                b = pe.value_load(K.blk_i[0:1, bass.ds(it * (2 * CH) + k * CH + j, 1)], min_val=0,
                                                  max_val=NB - 1)
                                ins = pe.matmul(K.ps[:, bass.ds(b * H, H)], hot[k][:, j, :], mx[k][:, j * H:(j + 1) * H],
                                                start=False, stop=False, skip_group_check=True)
                            ins.then_inc(chunk_free, 1)

        def node_maxima():
            with semaphore(nc, f"{tag}_nm") as steps, semaphore(nc, f"{tag}_nmw") as wanted, \
                    semaphore(nc, f"{tag}_nmr") as ready, nc.Block() as block:
                mxs = K.ps[:, 0:NB * H].rearrange("p (b h) -> p b h", h=H)

                @block.vector
                def _(v):
                    link = Link(v, steps)
                    link(v.tensor_scalar(K.deg1[:, :], K.has[:, :], -1.0, BIG, ALU.add, ALU.mult))
                    link(v.tensor_tensor(t0[:, :, :], mxs, per_node(K.deg1[:, :], H), ALU.add))
                    link(v.tensor_tensor(t0[:, :, :], t0[:, :, :], als, ALU.max))
                    link(v.tensor_tensor(t0[:, :, :], t0[:, :, :], ald, ALU.add))
                    link(v.scalar_tensor_tensor(out=spread[:, :, 1, :], in0=t0[:, :, :], scalar=0.2, in1=t0[:, :, :],
                                                op0=ALU.mult, op1=ALU.max))
                    link(v.tensor_copy(spread[:, :, 0, :], ald))
                    link(v.tensor_tensor(t0[:, :, :], als, ald, ALU.add))
                    link(v.scalar_tensor_tensor(out=t1[:, :, :], in0=t0[:, :, :], scalar=0.2, in1=t0[:, :, :],
                                                op0=ALU.mult, op1=ALU.max))
                    link(v.tensor_tensor(t1[:, :, :], t1[:, :, :], spread[:, :, 1, :], ALU.subtract))
                    v.sem_inc(wanted, 1)

                @block.scalar
                def _(act):
                    act.wait_ge(wanted, 1)
                    act.activation(selfw[:, :, :], t1[:, :, :], ACT.Exp).then_inc(ready, 1)
                    act.wait_ge(ready, 1)

        def edge_weights():
            c = ExitStack()
            with c:
                def sem(name):
                    return c.enter_context(semaphore(nc, f"{tag}_{name}"))

                dlb = [c.enter_context(nc.sbuf_tensor(f"{tag}_dlb{k}", [P, CW], FP32)) for k in range(2)]
                cold = [c.enter_context(nc.sbuf_tensor(f"{tag}_cold{k}", [P, CW], FP32)) for k in range(2)]
                score = [c.enter_context(nc.sbuf_tensor(f"{tag}_score{k}", [P, CH, H], FP32)) for k in range(2)]
                dl_in = [sem(f"dl_in{k}") for k in range(2)]
                cold_ready, spread_done, scored, steps, weighed = (sem(n) for n in (
                    "cold_ready", "spread_done", "scored", "steps", "weighed"))
                block = c.enter_context(nc.Block())

                @block.sync
                def _(sp):
                    with sp.Fori(0, ITERS) as it:
                        for k in range(2):
                            sp.wait_ge(cold_ready, it * 2 + k + 1)
                            rows = K.dl_rows[bass.ds(it * (2 * CH) + k * CH, CH), :]
                            sp.dma_start(dlb[k][:, :], bcast_chunk(rows, P)).then_inc(dl_in[k], 16)

                @block.vector
                def _(v):
                    v.sem_inc(cold_ready, 2)
                    link = Link(v, steps, per=8)
                    with v.Fori(0, ITERS) as it:
                        link.turn(it)
                        for k in range(2):
                            v.wait_ge(dl_in[k], it * 16 + 16)
                            v.wait_ge(spread_done, it * 2 + k + 1)
                            v.tensor_scalar(cold[k][:, :], dlb[k][:, :], K.iota_part[:, 0:1], None, ALU.is_equal
                                            ).then_inc(cold_ready, 1)
                            v.wait_ge(spread_done, it * 2 + k + 3)
                            v.wait_ge(weighed, it * 2 + k + 1)
                            got = K.ps[:, k * BANK:k * BANK + CH * 2 * H].rearrange("p (s t h) -> p s t h", t=2, h=H)
                            here = kept[:, bass.ds(it * (2 * CH) + k * CH, CH), :]
                            sc = score[k][:, :, :]
                            link(v.tensor_tensor(sc, here[:, :, F:GW], got[:, :, 0, :], ALU.add))
                            link(v.scalar_tensor_tensor(out=sc, in0=sc, scalar=0.2, in1=sc, op0=ALU.mult, op1=ALU.max))
                            link(v.tensor_tensor(sc, sc, got[:, :, 1, :], ALU.subtract))
                            link(v.tensor_scalar(sc, sc, 0.0, None, ALU.min))
                            v.sem_inc(scored, 1)

                @block.scalar
                def _(act):
                    act.sem_inc(weighed, 2)
                    with act.Fori(0, ITERS) as it:
                        for k in range(2):
                            act.wait_ge(scored, it * 2 + k + 1)
                            act.activation(weight[:, bass.ds(it * (2 * CH) + k * CH, CH), :], score[k][:, :, :], ACT.Exp
                                           ).then_inc(weighed, 1)

                @block.tensor
                def _(pe):
                    pe.sem_inc(spread_done, 2)
                    flat = spread[:, :, :, :].rearrange("p b t h -> p (b t h)")
                    with pe.Fori(0, ITERS) as it:
                        for k in range(2):
                            pe.wait_ge(cold_ready, it * 2 + k + 3)
                            pe.wait_ge(weighed, it * 2 + k + 1)
                            for j in range(CH):
                                b = pe.value_load(K.blk_i[0:1, bass.ds(it * (2 * CH) + k * CH + j, 1)], min_val=0,
                                                  max_val=NB - 1)
                                o = k * BANK + j * 2 * H
                                ins = pe.matmul(K.ps[:, o:o + 2 * H], cold[k][:, j * P:(j + 1) * P],
                                                flat[:, bass.ds(b * (2 * H), 2 * H)], start=True, stop=True,
                                                skip_group_check=True)
                            ins.then_inc(spread_done, 1)

        def weighted_sum(h0):
            c = ExitStack()
            DEN = NB * HP * F
            with c:
                msg = [c.enter_context(nc.sbuf_tensor(f"{tag}_msg{h0}{k}", [P, CH, HP, F], FP32)) for k in range(2)]
                msg_ready = c.enter_context(semaphore(nc, f"{tag}_msg_ready{h0}"))
                chunk_free = c.enter_context(semaphore(nc, f"{tag}_msg_free{h0}"))
                steps = c.enter_context(semaphore(nc, f"{tag}_norm{h0}"))
                block = c.enter_context(nc.Block())

                @block.vector
                def _(v):
                    with v.Fori(0, ITERS) as it:
                        for k in range(2):
                            v.wait_ge(chunk_free, it * 2 + k + 1)
                            at = it * (2 * CH) + k * CH
                            onehot(v, hot[k][:, :, :], K.iota_row[:, :], K.dl[:, bass.ds(at, CH)]).then_inc(msg_ready, 1)
                            v.tensor_tensor(msg[k][:, :, :, :],
                                            kept[:, bass.ds(at, CH), 0:F].unsqueeze(2).broadcast_to([P, CH, HP, F]),
                                            weight[:, bass.ds(at, CH), h0:h0 + HP].unsqueeze(3).broadcast_to([P, CH, HP, F]),
                                            ALU.mult).then_inc(msg_ready, 1)
                    v.wait_ge(chunk_free, 2 + 2 * ITERS)
                    link = Link(v, steps)
                    if h0 == 0:
                        link(v.tensor_tensor(t0[:, :, :], K.ps[:, DEN:DEN + NB * H].rearrange("p (b h) -> p b h", h=H),
                                             selfw[:, :, :], ALU.add))
                        link(v.tensor_scalar(t0[:, :, :], t0[:, :, :], 1.0e-16, None, ALU.add))
                        link(v.reciprocal(t0[:, :, :], t0[:, :, :]))
                    zz = z[:, :, h0:h0 + HP, :]
                    full = [P, NB, HP, F]
                    link(v.tensor_tensor(zz, x.unsqueeze(2).broadcast_to(full),
                                         selfw[:, :, h0:h0 + HP].unsqueeze(3).broadcast_to(full), ALU.mult))
                    link(v.tensor_tensor(zz, zz, K.ps[:, 0:DEN].rearrange("p (b h c) -> p b h c", h=HP, c=F), ALU.add))
                    link(v.tensor_tensor(zz, zz, t0[:, :, h0:h0 + HP].unsqueeze(3).broadcast_to(full), ALU.mult))

                @block.tensor
                def _(pe):
                    clear_banks(pe, K, 0, 7).then_inc(chunk_free, 2)
                    wflat = weight[:, :, :].rearrange("p s h -> p (s h)")
                    with pe.Fori(0, ITERS) as it:
                        for k in range(2):
                            pe.wait_ge(msg_ready, it * 4 + 2 * k + 2)
                            for j in range(CH):
                                at = it * (2 * CH) + k * CH + j
                                b = pe.value_load(K.blk_i[0:1, bass.ds(at, 1)], min_val=0, max_val=NB - 1)
                                if h0 == 0:
                                    pe.matmul(K.ps[:, bass.ds(b * H + DEN, H)], hot[k][:, j, :],
                                              wflat[:, bass.ds(it * (2 * CH * H) + (k * CH + j) * H, H)],
                                              start=False, stop=False, skip_group_check=True)
                                ins = pe.matmul(K.ps[:, bass.ds(b * (HP * F), HP * F)], hot[k][:, j, :],
                                                msg[k][:, j, :, :].rearrange("p h c -> p (h c)"),
                                                start=False, stop=False, skip_group_check=True)
                            ins.then_inc(chunk_free, 1)

        gather_and_max()
        node_maxima()
        edge_weights()
        for h0 in range(0, H, HP):
            weighted_sum(h0)


def bcast_chunk(rows, parts):
    return rows.rearrange("(o s) e -> o (s e)", o=1).broadcast_to([parts, CW])


def residual_norm(nc, K, add, tag):
    ctx = ExitStack()
    with ctx:
        y = ctx.enter_context(nc.sbuf_tensor(f"{tag}_y", [P, NB, F], FP32))
        sq = ctx.enter_context(nc.sbuf_tensor(f"{tag}_sq", [P, NB, F], FP32))
        mean = ctx.enter_context(nc.sbuf_tensor(f"{tag}_mean", [P, NB], FP32))
        var = ctx.enter_context(nc.sbuf_tensor(f"{tag}_var", [P, NB], FP32))
        steps = ctx.enter_context(semaphore(nc, f"{tag}_rn"))
        wanted = ctx.enter_context(semaphore(nc, f"{tag}_rnw"))
        ready = ctx.enter_context(semaphore(nc, f"{tag}_rnr"))
        block = ctx.enter_context(nc.Block())

        @block.vector
        def _(v):
            link = Link(v, steps)
            add(v, link, y)
            link(v.tensor_tensor(y[:, :, :], y[:, :, :], K.x[:, :, :], ALU.add))
            layernorm_steps(v, link, K, y[:, :, :], K.x[:, :, :], sq[:, :, :], mean[:, :], var[:, :], wanted, ready)

        @block.scalar
        def _(act):
            act.wait_ge(wanted, 1)
            act.activation(var[:, :], var[:, :], ACT.Sqrt).then_inc(ready, 1)


def gat(nc, K, A):
    H = HEADS
    ctx = ExitStack()
    with ctx:
        def sb(name, shape, dt=FP32):
            return ctx.enter_context(nc.sbuf_tensor(name, shape, dt))

        w1 = sb("w1", [F, H, F])
        w2a = sb("w2a", [F, H, F + 2])
        b1 = sb("b1c", [F, H])
        b2 = sb("b2r", [P, F])
        va = sb("va", [F, 2 * H])
        h2 = sb("h2", [P, NB, F + 2])
        prep = ExitStack()
        with prep:
            rows = prep.enter_context(nc.sbuf_tensor("att_rows", [F, 2, H, F], FP32))
            rows2 = prep.enter_context(nc.sbuf_tensor("att_rows2", [F, 2, F], FP32))
            prod = prep.enter_context(nc.sbuf_tensor("att_prod", [F, H, F], FP32))
            loaded = prep.enter_context(semaphore(nc, "gat_loaded"))
            steps = prep.enter_context(semaphore(nc, "gat_steps"))
            block = prep.enter_context(nc.Block())

            @block.sync
            def _(sp):
                sp.dma_start(w1[:, :, :], A["L1_gnn_W1"].rearrange("k (h o) -> k h o", h=H)).then_inc(loaded, 16)
                sp.dma_start(w2a[:, :, 0:F], A["L1_gnn_W2"].rearrange("(h k) o -> k h o", h=H)).then_inc(loaded, 16)
                with nc.allow_non_contiguous_dma(reason="a column of 256 biases"):
                    sp.dma_start(b1[:, :], A["L1_gnn_b1"].rearrange("(h k) -> k h", h=H)).then_inc(loaded, 16)
                sp.dma_start(b2[:, :], bcast_rows(A["L1_gnn_b2"], P)).then_inc(loaded, 16)
                for i, n in enumerate(("L1_gnn_a_src1", "L1_gnn_a_dst1")):
                    sp.dma_start(rows[:, i, :, :].rearrange("p h o -> p (h o)"),
                                 bcast_rows(A[n].rearrange("h o -> (h o)"), F)).then_inc(loaded, 16)
                for i, n in enumerate(("L1_gnn_a_src2", "L1_gnn_a_dst2")):
                    sp.dma_start(rows2[:, i, :], bcast_rows(A[n].rearrange("h o -> (h o)"), F)).then_inc(loaded, 16)

            @block.vector
            def _(v):
                link = Link(v, steps)
                v.wait_ge(loaded, 16 * 8)
                for i in range(2):
                    link(v.tensor_tensor(prod[:, :, :], w1[:, :, :], rows[:, i, :, :], ALU.mult))
                    link(v.tensor_reduce(va[:, i * H:(i + 1) * H], prod[:, :, :], AX.X, ALU.add))
                    link(v.tensor_tensor(prod[:, :, :], w2a[:, :, 0:F],
                                         rows2[:, i, :].unsqueeze(1).broadcast_to([F, H, F]), ALU.mult))
                    link(v.tensor_reduce(w2a[:, :, F + i], prod[:, :, :], AX.X, ALU.add))

        first = ExitStack()
        with first:
            al = first.enter_context(nc.sbuf_tensor("al1", [P, NB, 2 * H], FP32))
            z = first.enter_context(nc.sbuf_tensor("z1", [P, NB, H, F], FP32))
            with nc.sbuf_tensor("xT1", [F, NB * P], FP32) as xT:
                transpose_nodes(nc, K, K.x, xT, "g1t")
                project(nc, K, xT, va[:, :], 2 * H, al, "g1p")
            store_table(nc, K, K.tab_gat1, [(0, F, K.x[:, :, :]), (F, H, al[:, :, 0:H])], "g1s")
            attention(nc, K, H, K.tab_gat1, K.x[:, :, :], al[:, :, 0:H], al[:, :, H:2 * H], z, "g1")
            dense_heads(nc, K, z, w1, b1, w2a, h2)
        store_table(nc, K, K.tab_gat2, [(0, F + 1, h2[:, :, 0:F + 1])], "g2s")
        z2 = sb("z2", [P, NB, 1, F])
        attention(nc, K, 1, K.tab_gat2, h2[:, :, 0:F], h2[:, :, F:F + 1], h2[:, :, F + 1:F + 2], z2, "g2")

        def add(v, link, y):
            link(v.tensor_tensor(y[:, :, :], z2[:, :, 0, :], per_feature(b2[:, :]), ALU.add))
        residual_norm(nc, K, add, "g")


def dense_heads(nc, K, z, w1, b1, w2a, h2):
    H, C = HEADS, F + 2
    ctx = ExitStack()
    with ctx:
        def sem(name):
            return ctx.enter_context(semaphore(nc, name))

        zb = ctx.enter_context(nc.sbuf_tensor("zb", [P, H, F], FP32))
        zt = ctx.enter_context(nc.sbuf_tensor("zt", [F, H, P], FP32))
        ht = ctx.enter_context(nc.sbuf_tensor("ht", [F, H, P], FP32))
        staged, turned, zt_ready, hidden, ht_ready, made, copied = (sem(n) for n in (
            "d_staged", "d_turned", "d_zt_ready", "d_hidden", "d_ht_ready", "d_made", "d_copied"))
        block = ctx.enter_context(nc.Block())

        @block.scalar
        def _(act):
            act.sem_inc(ht_ready, H)
            with act.Fori(0, NB) as b:
                act.wait_ge(turned, b + 1)
                act.copy(zb[:, :, :], z[:, bass.ds(b, 1), :, :].rearrange("p b h c -> p (b h) c")).then_inc(staged, 1)
                act.wait_ge(hidden, b + 1)
                for h in range(H):
                    act.activation(ht[:, h, :], K.ps[0:F, BANK + h * P:BANK + (h + 1) * P], ACT.Relu, bias=b1[:, h:h + 1]
                                   ).then_inc(ht_ready, 1)

        @block.vector
        def _(v):
            v.sem_inc(copied, 1)
            with v.Fori(0, NB) as b:
                v.wait_ge(turned, b + 2)
                v.tensor_copy(zt[:, :, :], K.ps[0:F, 0:H * P].rearrange("p (h e) -> p h e", h=H)).then_inc(zt_ready, 1)
                v.wait_ge(made, b + 1)
                v.tensor_copy(h2[:, bass.ds(b, 1), :].rearrange("p b c -> p (b c)"), K.ps[:, 2 * BANK:2 * BANK + C]
                              ).then_inc(copied, 1)

        @block.tensor
        def _(pe):
            pe.sem_inc(turned, 1)
            with pe.Fori(0, NB) as b:
                pe.wait_ge(staged, b + 1)
                pe.nop(nofuse=True)
                for h in range(H):
                    ins = pe.transpose(K.ps[0:F, h * P:(h + 1) * P], zb[:, h, :], K.ident[:, :])
                ins.then_inc(turned, 1)
                pe.wait_ge(zt_ready, b + 1)
                pe.wait_ge(ht_ready, b * H + H)
                pe.nop(nofuse=True)
                for h in range(H):
                    ins = pe.matmul(K.ps[0:F, BANK + h * P:BANK + (h + 1) * P], w1[:, h, :], zt[:, h, :],
                                    start=True, stop=True, skip_group_check=True)
                ins.then_inc(hidden, 1)
                pe.wait_ge(ht_ready, b * H + 2 * H)
                pe.wait_ge(copied, b + 1)
                pe.nop(nofuse=True)
                for h in range(H):
                    ins = pe.matmul(K.ps[:, 2 * BANK:2 * BANK + C], ht[:, h, :], w2a[:, h, :], start=h == 0, stop=h == H - 1)
                ins.then_inc(made, 1)


def relational(nc, K, A):
    ctx = ExitStack()
    with ctx:
        def sb(name, shape, dt=FP32):
            return ctx.enter_context(nc.sbuf_tensor(name, shape, dt))

        rel = sb("rel", [F, REL, F])
        wself = sb("wself", [F, F])
        bias = sb("rel_bias", [P, F])
        own = sb("rel_own", [P, NB, F])
        xT = sb("xT2", [F, NB * P])
        prep = ExitStack()
        with prep:
            basis = prep.enter_context(nc.sbuf_tensor("basis", [NBASE, F, F], FP32))
            coeff = prep.enter_context(nc.sbuf_tensor("coeff", [REL, NBASE], FP32))
            coefT = prep.enter_context(nc.sbuf_tensor("coefT", [NBASE, REL], FP32))
            loaded = prep.enter_context(semaphore(nc, "rel_loaded"))
            turned = prep.enter_context(semaphore(nc, "rel_turned"))
            ready = prep.enter_context(semaphore(nc, "rel_coef"))
            made = prep.enter_context(semaphore(nc, "rel_made"))
            block = prep.enter_context(nc.Block())

            @block.sync
            def _(sp):
                sp.dma_start(basis[:, :, :], A["L2_gnn_basis"]).then_inc(loaded, 16)
                sp.dma_start(coeff[:, :], A["L2_gnn_coeff"]).then_inc(loaded, 16)
                sp.dma_start(wself[:, :], A["L2_gnn_self_weight"]).then_inc(loaded, 16)
                sp.dma_start(bias[:, :], bcast_rows(A["L2_gnn_bias"], P)).then_inc(loaded, 16)

            @block.tensor
            def _(pe):
                pe.wait_ge(loaded, 64)
                pe.transpose(K.ps[0:NBASE, 7 * BANK:7 * BANK + REL], coeff[:, :], K.ident[0:REL, 0:REL]).then_inc(turned, 1)
                pe.wait_ge(ready, 1)
                for o in range(F):
                    ins = pe.matmul(K.ps[0:F, o * REL:(o + 1) * REL], basis[:, :, o], coefT[:, :], start=True, stop=True,
                                    skip_group_check=True)
                ins.then_inc(made, 1)

            @block.vector
            def _(v):
                v.wait_ge(turned, 1)
                v.tensor_copy(coefT[:, :], K.ps[0:NBASE, 7 * BANK:7 * BANK + REL]).then_inc(ready, 1)
                v.wait_ge(made, 1)
                v.tensor_copy(rel[:, :, :], K.ps[0:F, 0:F * REL].rearrange("p (o r) -> p r o", r=REL)).then_inc(ready, 1)
                v.wait_ge(ready, 2)
        transpose_nodes(nc, K, K.x, xT, "r1t")
        project(nc, K, xT, wself[:, :], F, own, "r1p")
        relation_table(nc, K, rel, xT)
        gather_sum(nc, K, K.tab_rel.rearrange("n (r o) -> (n r) o", r=REL), K.rel_idx, "relg")

        def add(v, link, y):
            link(v.tensor_tensor(y[:, :, :], sums(K), per_node(K.rdeg[:, :]), ALU.mult))
            link(v.tensor_tensor(y[:, :, :], y[:, :, :], own[:, :, :], ALU.add))
            link(v.tensor_tensor(y[:, :, :], y[:, :, :], per_feature(bias[:, :]), ALU.add))
        residual_norm(nc, K, add, "r")


def relation_table(nc, K, rel, xT):
    ctx = ExitStack()
    with ctx:
        W = REL * F
        Q = W // BANK
        y = [ctx.enter_context(nc.sbuf_tensor(f"ytab{k}", [P, W], FP32)) for k in range(2)]
        xb = [ctx.enter_context(nc.sbuf_tensor(f"xtb{k}", [F, P], FP32)) for k in range(2)]
        staged, made, copied_v, copied_a = (ctx.enter_context(semaphore(nc, n)) for n in (
            "y_staged", "y_made", "y_copied_v", "y_copied_a"))
        stored = [ctx.enter_context(semaphore(nc, f"y_stored{k}")) for k in range(2)]
        block = ctx.enter_context(nc.Block())
        flat = rel[:, :, :].rearrange("p r o -> p (r o)")
        rows = node_rows(K.tab_rel)

        @block.tensor
        def _(pe):
            def one(b, k):
                pe.wait_ge(staged, b + 1)
                pe.wait_ge(copied_v, b * (Q // 2) + Q // 2)
                pe.wait_ge(copied_a, b * (Q // 2) + Q // 2)
                pe.nop(nofuse=True)
                for q in range(Q):
                    pe.matmul(K.ps[:, (4 * k + q) * BANK:(4 * k + q + 1) * BANK], xb[k][:, :],
                              flat[:, q * BANK:(q + 1) * BANK], start=True, stop=True).then_inc(made, 1)
            with pe.Fori(0, NB // 2) as it:
                for k in range(2):
                    one(it * 2 + k, k)
            one(NB - 1, 0)

        @block.scalar
        def _(act):
            def half(b, k, n):
                act.wait_ge(stored[k], n)
                for q in range(Q // 2, Q):
                    act.wait_ge(made, b * Q + q + 1)
                    act.copy(y[k][:, q * BANK:(q + 1) * BANK], K.ps[:, (4 * k + q) * BANK:(4 * k + q + 1) * BANK]
                             ).then_inc(copied_a, 1)
            act.sem_inc(copied_a, Q)
            with act.Fori(0, NB // 2) as it:
                for k in range(2):
                    half(it * 2 + k, k, it * 16 + 16)
            half(NB - 1, 0, (NB // 2) * 16 + 16)

        @block.vector
        def _(v):
            def half(b, k, n):
                v.wait_ge(copied_a, b * (Q // 2) + Q // 2)
                v.tensor_copy(xb[k][:, :], xT[:, bass.ds(b * P, P)] if not isinstance(b, int)
                              else xT[:, b * P:(b + 1) * P]).then_inc(staged, 1)
                v.wait_ge(stored[k], n)
                for q in range(Q // 2):
                    v.wait_ge(made, b * Q + q + 1)
                    v.tensor_copy(y[k][:, q * BANK:(q + 1) * BANK], K.ps[:, (4 * k + q) * BANK:(4 * k + q + 1) * BANK]
                                  ).then_inc(copied_v, 1)
            v.sem_inc(copied_v, Q)
            with v.Fori(0, NB // 2) as it:
                for k in range(2):
                    half(it * 2 + k, k, it * 16 + 16)
            half(NB - 1, 0, (NB // 2) * 16 + 16)

        @block.sync
        def _(sp):
            def one(b, k):
                sp.wait_ge(copied_v, b * (Q // 2) + Q + Q // 2)
                sp.wait_ge(copied_a, b * (Q // 2) + Q + Q // 2)
                out = rows[:, bass.ds(b, 1), :] if not isinstance(b, int) else rows[:, b:b + 1, :]
                sp.dma_start(out, y[k][:, :].unsqueeze(1)).then_inc(stored[k], 16)
            sp.sem_inc(stored[0], 16)
            sp.sem_inc(stored[1], 16)
            with sp.Fori(0, NB // 2) as it:
                for k in range(2):
                    one(it * 2 + k, k)
            one(NB - 1, 0)
            sp.wait_ge(stored[0], 16 + 16 * (NB // 2 + 1))
            sp.wait_ge(stored[1], 16 + 16 * (NB // 2))


def rows_of(nc, K, var, tag):
    ctx = ExitStack()
    with ctx:
        rr = ctx.enter_context(nc.sbuf_tensor(f"{tag}_rr", [P, 4, P], FP32))
        steps, wanted, ready, turned, stored = (ctx.enter_context(semaphore(nc, f"{tag}_{n}")) for n in (
            "steps", "wanted", "ready", "turned", "stored"))
        block = ctx.enter_context(nc.Block())

        @block.vector
        def _(v):
            link = Link(v, steps)
            link(v.tensor_scalar(var, var, 1.0 / F, EPS, ALU.mult, ALU.add))
            v.sem_inc(wanted, 1)
            v.wait_ge(ready, 1)
            link(v.reciprocal(var, var))
            v.wait_ge(turned, 1)
            link(v.tensor_copy(rr[0:SG, :, :], K.ps[0:SG, 0:4 * P].rearrange("p (g e) -> p g e", g=4)))

        @block.scalar
        def _(act):
            act.wait_ge(wanted, 1)
            act.activation(var, var, ACT.Sqrt).then_inc(ready, 1)

        @block.tensor
        def _(pe):
            pe.wait_ge(steps, 2)
            for g in range(4):
                ins = pe.transpose(K.ps[0:SG, g * P:(g + 1) * P], var[:, g * SG:(g + 1) * SG], K.ident[:, :])
            ins.then_inc(turned, 1)

        @block.sync
        def _(sp):
            sp.wait_ge(steps, 3)
            sp.dma_start(K.rstd_rows.rearrange("(g s) e -> s g e", g=4), rr[0:SG, :, :]).then_inc(stored, 16)
            sp.wait_ge(stored, 16)


def encode_edges(nc, K, A):
    ctx = ExitStack()
    with ctx:
        def sb(name, shape, dt=FP32):
            return ctx.enter_context(nc.sbuf_tensor(name, shape, dt))

        wd1 = sb("wd1", [4, F])
        wd2 = sb("wd2", [F, F])
        bd2r = sb("bd2r", [1, F])
        bd2 = sb("bd2", [F, 1])
        mean = sb("wmean", [F, 3])
        gb = sb("gb", [F, 4])
        var = sb("evar", [P, SLOTS])
        at = [sb(f"at{k}", [4, CW]) for k in range(2)]

        def weights():
            with semaphore(nc, "w_loaded") as loaded, semaphore(nc, "w_steps") as steps, \
                    semaphore(nc, "w_made") as made, nc.Block() as block:
                @block.sync
                def _(sp):
                    sp.dma_start(wd1[0:3, :], A["L3_gnn_Wd1"]).then_inc(loaded, 16)
                    sp.dma_start(wd1[3:4, :], bcast_rows(A["L3_gnn_bd1"], 1)).then_inc(loaded, 16)
                    sp.dma_start(wd2[:, :], A["L3_gnn_Wd2"]).then_inc(loaded, 16)
                    sp.dma_start(bd2r[:, :], bcast_rows(A["L3_gnn_bd2"], 1)).then_inc(loaded, 16)
                    with nc.allow_non_contiguous_dma(reason="columns of 64"):
                        for i, n in enumerate(("L3_gnn_g1", "L3_gnn_b1", "L3_gnn_g2", "L3_gnn_b2")):
                            sp.dma_start(gb[:, i:i + 1], A[n].rearrange("(c o) -> c o", o=1)).then_inc(loaded, 16)

                @block.vector
                def _(v):
                    link = Link(v, steps)
                    for k in range(2):
                        link(v.memset(at[k][:, :], 1.0))
                    v.wait_ge(loaded, 16 * 8)
                    for i, (w, n) in enumerate(((wd1, 4), (wd2, F), (bd2r, 1))):
                        link(v.tensor_reduce(mean[0:n, i:i + 1], w[:, :], AX.X, ALU.add))
                        link(v.tensor_scalar(mean[0:n, i:i + 1], mean[0:n, i:i + 1], -1.0 / F, None, ALU.mult))
                        link(v.tensor_scalar(w[:, :], w[:, :], mean[0:n, i:i + 1], None, ALU.add))
                    v.wait_ge(made, 1)
                    link(v.tensor_copy(bd2[:, :], K.ps[0:F, 0:1]))

                @block.tensor
                def _(pe):
                    pe.wait_ge(steps, 11)
                    pe.matmul(K.ps[0:F, 0:1], bd2r[:, :], K.ones[0:1, 0:1], start=True, stop=True).then_inc(made, 1)

        def attr_chunk(it, k):
            return K.attr_rows[:, bass.ds(it * (2 * CH) + k * CH, CH), :].rearrange("a s e -> a (s e)")

        def first_variance():
            c = ExitStack()
            with c:
                sq = [c.enter_context(nc.sbuf_tensor(f"esq{k}", [P, CH, F], FP32)) for k in range(2)]
                at_in = [c.enter_context(semaphore(nc, f"e_at_in{k}")) for k in range(2)]
                made, squared, summed = (c.enter_context(semaphore(nc, n)) for n in ("e_made", "e_squared", "e_summed"))
                block = c.enter_context(nc.Block())

                @block.sync
                def _(sp):
                    with sp.Fori(0, ITERS) as it:
                        for k in range(2):
                            sp.wait_ge(made, it * 2 + k + 1)
                            sp.dma_start(at[k][0:3, :], attr_chunk(it, k)).then_inc(at_in[k], 16)

                @block.tensor
                def _(pe):
                    pe.sem_inc(made, 2)
                    with pe.Fori(0, ITERS) as it:
                        for k in range(2):
                            pe.wait_ge(at_in[k], it * 16 + 16)
                            pe.wait_ge(squared, it * 2 + k + 1)
                            pe.nop(nofuse=True)
                            for j in range(CH):
                                o = k * BANK + j * F
                                ins = pe.matmul(K.ps[:, o:o + F], at[k][:, j * P:(j + 1) * P], wd1[:, :],
                                                start=True, stop=True, skip_group_check=True)
                            ins.then_inc(made, 1)

                @block.scalar
                def _(act):
                    act.sem_inc(squared, 2)
                    with act.Fori(0, ITERS) as it:
                        for k in range(2):
                            act.wait_ge(made, it * 2 + k + 3)
                            act.wait_ge(summed, it * 2 + k + 1)
                            act.activation(sq[k][:, :, :], K.ps[:, k * BANK:k * BANK + CH * F].rearrange(
                                "p (s c) -> p s c", c=F), ACT.Square).then_inc(squared, 1)

                @block.vector
                def _(v):
                    v.sem_inc(summed, 2)
                    with v.Fori(0, ITERS) as it:
                        for k in range(2):
                            v.wait_ge(squared, it * 2 + k + 3)
                            v.tensor_reduce(var[:, bass.ds(it * (2 * CH) + k * CH, CH)], sq[k][:, :, :], AX.X, ALU.add
                                            ).then_inc(summed, 1)

        def middle():
            c = ExitStack()
            with c:
                def pair(name, shape):
                    return [c.enter_context(nc.sbuf_tensor(f"{name}{k}", shape, FP32)) for k in range(2)]

                def sem(name):
                    return c.enter_context(semaphore(nc, name))

                ats, rs, d1, hh, sq = (pair(n, s) for n, s in (("ats", [4, CW]), ("ers", [4, CW]), ("ed1", [F, CW]),
                                                               ("ehh", [F, CW]), ("ehs", [F, CW])))
                at_in = [sem(f"m_in{k}") for k in range(2)]
                stored = [sem(f"m_stored{k}") for k in range(2)]
                scaled, first, gelued, second, moved, squared, summed, taken = (sem(f"m_{n}") for n in (
                    "scaled", "first", "gelued", "second", "moved", "squared", "summed", "taken"))
                block = c.enter_context(nc.Block())

                @block.sync
                def _(sp):
                    sp.sem_inc(stored[0], 16)
                    sp.sem_inc(stored[1], 16)
                    with sp.Fori(0, ITERS) as it:
                        for k in range(2):
                            sp.wait_ge(scaled, it * 2 + k + 1)
                            sp.dma_start(at[k][0:3, :], attr_chunk(it, k)).then_inc(at_in[k], 16)
                            sp.dma_start(rs[k][:, :], bcast_chunk(K.rstd_rows[bass.ds(it * (2 * CH) + k * CH, CH), :], 4)
                                         ).then_inc(at_in[k], 16)

                @block.vector
                def _(v):
                    v.sem_inc(scaled, 2)
                    v.sem_inc(squared, 2)
                    v.sem_inc(taken, 2)
                    with v.Fori(0, ITERS) as it:
                        for k in range(2):
                            v.wait_ge(at_in[k], it * 32 + 32)
                            v.wait_ge(first, it * 2 + k + 1)
                            v.tensor_tensor(ats[k][:, :], at[k][:, :], rs[k][:, :], ALU.mult).then_inc(scaled, 1)
                            v.wait_ge(moved, it * 2 + k + 1)
                            v.wait_ge(summed, it * 2 + k + 1)
                            v.tensor_tensor(sq[k][:, :], hh[k][:, :], hh[k][:, :], ALU.mult).then_inc(squared, 1)
                            v.wait_ge(summed, it * 2 + k + 3)
                            v.tensor_copy(var[:, bass.ds(it * (2 * CH) + k * CH, CH)],
                                          K.ps[:, (4 + k) * BANK:(4 + k) * BANK + CH]).then_inc(taken, 1)

                @block.scalar
                def _(act):
                    act.sem_inc(gelued, 2)
                    with act.Fori(0, ITERS) as it:
                        for k in range(2):
                            act.wait_ge(first, it * 2 + k + 3)
                            act.wait_ge(second, it * 2 + k + 1)
                            act.activation(d1[k][:, :], K.ps[0:F, k * BANK:(k + 1) * BANK], ACT.Gelu, bias=gb[:, 1:2],
                                           scale=gb[:, 0:1]).then_inc(gelued, 1)
                            act.wait_ge(second, it * 2 + k + 3)
                            act.wait_ge(stored[k], it * 16 + 16)
                            act.wait_ge(squared, it * 2 + k + 1)
                            act.activation(hh[k][:, :], K.ps[0:F, (2 + k) * BANK:(3 + k) * BANK], ACT.Identity,
                                           bias=bd2[:, 0:1]).then_inc(moved, 1)
                            act.wait_ge(moved, it * 2 + k + 1)
                            act.dma_start(K.enc[:, bass.ds(it * (2 * CW) + k * CW, CW)], hh[k][:, :]).then_inc(stored[k], 16)
                    act.wait_ge(stored[0], 16 + 16 * ITERS)
                    act.wait_ge(stored[1], 16 + 16 * ITERS)

                @block.tensor
                def _(pe):
                    pe.sem_inc(first, 2)
                    pe.sem_inc(second, 2)
                    pe.sem_inc(summed, 2)
                    with pe.Fori(0, ITERS) as it:
                        for k in range(2):
                            pe.wait_ge(scaled, it * 2 + k + 3)
                            pe.wait_ge(gelued, it * 2 + k + 1)
                            pe.nop(nofuse=True)
                            pe.matmul(K.ps[0:F, k * BANK:(k + 1) * BANK], wd1[:, :], ats[k][:, :], start=True, stop=True
                                      ).then_inc(first, 1)
                            pe.wait_ge(gelued, it * 2 + k + 3)
                            pe.nop(nofuse=True)
                            pe.matmul(K.ps[0:F, (2 + k) * BANK:(3 + k) * BANK], wd2[:, :], d1[k][:, :], start=True,
                                      stop=True).then_inc(second, 1)
                            pe.wait_ge(squared, it * 2 + k + 3)
                            pe.wait_ge(taken, it * 2 + k + 1)
                            pe.nop(nofuse=True)
                            for j in range(CH):
                                o = (4 + k) * BANK + j
                                ins = pe.matmul(K.ps[:, o:o + 1], sq[k][:, j * P:(j + 1) * P], K.ones[0:F, 0:1],
                                                start=True, stop=True, skip_group_check=True)
                            ins.then_inc(summed, 1)

        def finish():
            c = ExitStack()
            with c:
                def pair(name, shape):
                    return [c.enter_context(nc.sbuf_tensor(f"{name}{k}", shape, FP32)) for k in range(2)]

                hin, rs, prod, dd = (pair(n, [F, CW]) for n in ("fh", "frs", "fp", "fd"))
                h_in = [c.enter_context(semaphore(nc, f"f_in{k}")) for k in range(2)]
                stored = [c.enter_context(semaphore(nc, f"f_stored{k}")) for k in range(2)]
                scaled, gelued = (c.enter_context(semaphore(nc, n)) for n in ("f_scaled", "f_gelued"))
                block = c.enter_context(nc.Block())

                @block.sync
                def _(sp):
                    with sp.Fori(0, ITERS) as it:
                        for k in range(2):
                            sp.wait_ge(scaled, it * 2 + k + 1)
                            sp.dma_start(hin[k][:, :], K.enc[:, bass.ds(it * (2 * CW) + k * CW, CW)]).then_inc(h_in[k], 16)
                            sp.dma_start(rs[k][:, :], bcast_chunk(K.rstd_rows[bass.ds(it * (2 * CH) + k * CH, CH), :], F)
                                         ).then_inc(h_in[k], 16)

                @block.vector
                def _(v):
                    v.sem_inc(scaled, 2)
                    with v.Fori(0, ITERS) as it:
                        for k in range(2):
                            v.wait_ge(h_in[k], it * 32 + 32)
                            v.wait_ge(gelued, it * 2 + k + 1)
                            v.tensor_tensor(prod[k][:, :], hin[k][:, :], rs[k][:, :], ALU.mult).then_inc(scaled, 1)

                @block.scalar
                def _(act):
                    act.sem_inc(gelued, 2)
                    act.sem_inc(stored[0], 16)
                    act.sem_inc(stored[1], 16)
                    with act.Fori(0, ITERS) as it:
                        for k in range(2):
                            act.wait_ge(scaled, it * 2 + k + 3)
                            act.wait_ge(stored[k], it * 16 + 16)
                            act.activation(dd[k][:, :], prod[k][:, :], ACT.Gelu, bias=gb[:, 3:4], scale=gb[:, 2:3]
                                           ).then_inc(gelued, 1)
                            act.wait_ge(gelued, it * 2 + k + 3)
                            act.dma_start(K.enc[:, bass.ds(it * (2 * CW) + k * CW, CW)], dd[k][:, :]).then_inc(stored[k], 16)
                    act.wait_ge(stored[0], 16 + 16 * ITERS)
                    act.wait_ge(stored[1], 16 + 16 * ITERS)

        weights()
        first_variance()
        rows_of(nc, K, var[:, :], "v1")
        middle()
        rows_of(nc, K, var[:, :], "v2")
        finish()


def vector_attention(nc, K, A):
    ctx = ExitStack()
    with ctx:
        def sb(name, shape, dt=FP32):
            return ctx.enter_context(nc.sbuf_tensor(name, shape, dt))

        proj = sb("proj", [P, NB, 3, F])
        with nc.sbuf_tensor("wv", [F, 3, F], FP32) as wv, nc.sbuf_tensor("xT3", [F, NB * P], FP32) as xT:
            with semaphore(nc, "wv_in") as wv_in, semaphore(nc, "wv_neg") as wv_neg, nc.Block() as block:
                @block.sync
                def _(sp):
                    for i, n in enumerate(("L3_gnn_W2", "L3_gnn_W3", "L3_gnn_W1")):
                        sp.dma_start(wv[:, i, :], A[n]).then_inc(wv_in, 16)

                @block.vector
                def _(v):
                    v.wait_ge(wv_in, 48)
                    v.tensor_scalar(wv[:, 0, :], wv[:, 0, :], -1.0, None, ALU.mult).then_inc(wv_neg, 1)
                    v.wait_ge(wv_neg, 1)
            transpose_nodes(nc, K, K.x, xT, "v1t")
            project(nc, K, xT, wv[:, :, :].rearrange("p i o -> p (i o)"), 3 * F,
                    proj[:, :, :, :].rearrange("p b i o -> p b (i o)"), "v1p")
        store_table(nc, K, K.tab_vec, [(0, 2 * F, proj[:, :, 0:2, :].rearrange("p b i o -> p b (i o)"))], "v1s")
        scan_edges(nc, K, proj)

        def add(v, link, y):
            link(v.tensor_copy(y[:, :, :], sums(K)))
        residual_norm(nc, K, add, "vec")


def scan_edges(nc, K, proj):
    ctx = ExitStack()
    with ctx:
        def pair(name, shape, dt=FP32):
            return [ctx.enter_context(nc.sbuf_tensor(f"s_{name}{k}", shape, dt)) for k in range(2)]

        def sem(name):
            return ctx.enter_context(semaphore(nc, f"s_{name}"))

        ring, idx = pair("ring", [P, CH, 2 * F]), pair("idx", [P, CH], I32)
        dlb, pen, enc = pair("dlb", [P, CW]), pair("pen", [F, CW]), pair("enc", [F, CW])
        cold, hot = pair("cold", [P, CW]), pair("hot", [P, CH, P])
        w1 = pair("w1", [P, CH, F])
        mrun = pair("mrun", [F, CW + 1])
        arg, ex = pair("arg", [F, 2, CW]), pair("ex", [F, 2, CW])
        ev, ssum, nsum = pair("ev", [F, CW]), pair("ssum", [F, CW]), pair("nsum", [F, CW])
        res, rt = pair("res", [F, CW]), pair("rt", [P, CH, F])
        twice = ctx.enter_context(nc.sbuf_tensor("twice", [F, 2, F], FP32))
        rows_in = [sem(f"rows_in{k}") for k in range(2)]
        side_in = [sem(f"side_in{k}") for k in range(2)]
        idx_ready, started, cold_ready, hot_ready, w1_ready, logits, args, exps, steps, res_ready, back, rt_ready, done = (
            sem(n) for n in ("idx_ready", "started", "cold_ready", "hot_ready", "w1_ready", "logits", "args", "exps",
                             "steps", "res_ready", "back", "rt_ready", "done"))
        block = ctx.enter_context(nc.Block())
        PER = 9

        @block.gpsimd
        def _(pool):
            with pool.Fori(0, ITERS) as it:
                for k in range(2):
                    pool.wait_ge(logits, it * 2 + k + 1)
                    pool.tensor_copy(idx[k][:, :], K.src_idx[:, bass.ds(it * (2 * CH) + k * CH, CH)]).then_inc(idx_ready, 1)
                    pool.wait_ge(idx_ready, it * 2 + k + 1)
                    pool.nop(nofuse=True)
                    for j in range(CH):
                        pool.indirect_dma_start(out=ring[k][:, j, :], out_offset=None, in_=K.tab_vec,
                                                in_offset=bass.IndirectOffsetOnAxis(ap=idx[k][:, j:j + 1], axis=0)
                                                ).then_inc(rows_in[k], 16)

        @block.sync
        def _(sp):
            with sp.Fori(0, ITERS) as it:
                for k in range(2):
                    sp.wait_ge(args, it * 2 + k + 1)
                    at = it * (2 * CH) + k * CH
                    sp.dma_start(dlb[k][:, :], bcast_chunk(K.dl_rows[bass.ds(at, CH), :], P)).then_inc(side_in[k], 16)
                    sp.dma_start(pen[k][:, :], bcast_chunk(K.pen_rows[bass.ds(at, CH), :], F)).then_inc(side_in[k], 16)
                    sp.dma_start(enc[k][:, :], K.enc[:, bass.ds(it * (2 * CW) + k * CW, CW)]).then_inc(side_in[k], 16)

        @block.vector
        def _(v):
            for k in range(2):
                v.tensor_copy(twice[:, k, :], K.ident[0:F, 0:F]).then_inc(started, 1)
            v.memset(mrun[1][:, :], -BIG).then_inc(started, 1)
            v.memset(ssum[1][:, :], 0.0).then_inc(started, 1)
            v.memset(nsum[1][:, :], 0.0).then_inc(started, 1)
            v.wait_ge(started, 5)
            v.sem_inc(args, 2)
            link = Link(v, steps, per=2 * PER)
            with v.Fori(0, ITERS) as it:
                link.turn(it)
                for k in range(2):
                    at = it * (2 * CH) + k * CH
                    bank = K.ps[:, (4 + k) * BANK:(5 + k) * BANK]
                    v.wait_ge(side_in[k], it * 48 + 48)
                    v.wait_ge(logits, it * 2 + k + 1)
                    v.tensor_scalar(cold[k][:, :], dlb[k][:, :], K.iota_part[:, 0:1], None, ALU.is_equal).then_inc(cold_ready, 1)
                    v.wait_ge(done, it * 2 + k + 1)
                    onehot(v, hot[k][:, :, :], K.iota_row[:, :], K.dl_end[:, bass.ds(at, CH)]).then_inc(hot_ready, 1)
                    v.wait_ge(logits, it * 2 + k + 3)
                    link(v.tensor_copy(mrun[k][:, 0:1], mrun[1 - k][:, CW:CW + 1]))
                    link(v.tensor_tensor_scan(mrun[k][:, 1:CW + 1], pen[k][:, :], bank[0:F, :], mrun[k][:, 0:1],
                                              ALU.add, ALU.max))
                    link(v.tensor_tensor(arg[k][:, 0, :], mrun[k][:, 0:CW], pen[k][:, :], ALU.add))
                    link(v.tensor_tensor(arg[k][:, 0, :], arg[k][:, 0, :], mrun[k][:, 1:CW + 1], ALU.subtract))
                    v.tensor_tensor(arg[k][:, 1, :], bank[0:F, :], mrun[k][:, 1:CW + 1], ALU.subtract).then_inc(args, 1)
                    v.wait_ge(exps, it * 2 + k + 1)
                    link(v.tensor_tensor(ev[k][:, :], ex[k][:, 1, :], bank[F:P, :], ALU.mult))
                    link(v.tensor_tensor_scan(ssum[k][:, :], ex[k][:, 0, :], ex[k][:, 1, :], ssum[1 - k][:, CW - 1:CW],
                                              ALU.mult, ALU.add))
                    link(v.tensor_tensor_scan(nsum[k][:, :], ex[k][:, 0, :], ev[k][:, :], nsum[1 - k][:, CW - 1:CW],
                                              ALU.mult, ALU.add))
                    link(v.reciprocal(ev[k][:, :], ssum[k][:, :]))
                    v.wait_ge(back, it * 2 + k + 1)
                    link(v.tensor_tensor(res[k][:, :], nsum[k][:, :], ev[k][:, :], ALU.mult))
                    v.sem_inc(res_ready, 1)

        @block.scalar
        def _(act):
            with act.Fori(0, ITERS) as it:
                for k in range(2):
                    act.wait_ge(logits, it * 2 + k + 1)
                    for j in range(CH):
                        b = act.value_load(K.blk_i[0:1, bass.ds(it * (2 * CH) + k * CH + j, 1)], min_val=0, max_val=NB - 1)
                        act.copy(w1[k][:, j, :], proj[:, bass.ds(b, 1), 2, :].rearrange("p b o -> p (b o)")
                                 ).then_inc(w1_ready, 1)
                    act.wait_ge(args, it * 2 + k + 3)
                    act.activation(ex[k][:, :, :], arg[k][:, :, :], ACT.Exp).then_inc(exps, 1)
                    act.wait_ge(back, it * 2 + k + 3)
                    act.copy(rt[k][:, :, :], K.ps[:, (6 + k) * BANK:(6 + k) * BANK + CH * F].rearrange(
                        "p (s c) -> p s c", c=F)).then_inc(rt_ready, 1)

        @block.tensor
        def _(pe):
            clear_banks(pe, K, 0, 4).then_inc(done, 2)
            pe.wait_ge(started, 5)
            pe.sem_inc(logits, 2)
            pe.sem_inc(back, 2)
            with pe.Fori(0, ITERS) as it:
                for k in range(2):
                    bank = K.ps[:, (4 + k) * BANK:(5 + k) * BANK]
                    pe.wait_ge(side_in[k], it * 48 + 48)
                    pe.wait_ge(rows_in[k], it * (16 * CH) + 16 * CH)
                    pe.wait_ge(cold_ready, it * 2 + k + 1)
                    pe.wait_ge(w1_ready, it * (2 * CH) + k * CH + CH)
                    pe.nop(nofuse=True)
                    pe.matmul(bank, twice[:, :, :].rearrange("p a c -> p (a c)"), enc[k][:, :], start=True, stop=False,
                              skip_group_check=True)
                    for j in range(CH):
                        cols = bank[:, j * P:(j + 1) * P]
                        pe.matmul(cols, ring[k][:, j, :], K.ident[:, :], start=False, stop=False, skip_group_check=True)
                        ins = pe.matmul(cols[0:F, :], w1[k][:, j, :], cold[k][:, j * P:(j + 1) * P], start=False, stop=True,
                                        skip_group_check=True)
                    ins.then_inc(logits, 1)
                    pe.wait_ge(res_ready, it * 2 + k + 1)
                    pe.nop(nofuse=True)
                    for j in range(CH):
                        o = (6 + k) * BANK + j * F
                        ins = pe.transpose(K.ps[:, o:o + F], res[k][:, j * P:(j + 1) * P], K.ident[0:F, 0:F])
                    ins.then_inc(back, 1)
                    pe.wait_ge(rt_ready, it * 2 + k + 1)
                    pe.wait_ge(hot_ready, it * 2 + k + 1)
                    for j in range(CH):
                        b = pe.value_load(K.blk_i[0:1, bass.ds(it * (2 * CH) + k * CH + j, 1)], min_val=0, max_val=NB - 1)
                        ins = pe.matmul(K.ps[:, bass.ds(b * F, F)], hot[k][:, j, :], rt[k][:, j, :], start=False,
                                        stop=False, skip_group_check=True)
                    ins.then_inc(done, 1)



def build(nc, A, out):
    K = Space()
    ctx = ExitStack()
    with ctx:
        def sb(name, shape, dt=FP32):
            return ctx.enter_context(nc.sbuf_tensor(name, shape, dt))

        def dram(name, shape, dt=FP32):
            return nc.dram_tensor(name, shape, dt, kind="Internal").ap()

        K.ps = ctx.enter_context(nc.psum_tensor("ps", [P, 8 * BANK], FP32))
        K.ident = sb("ident", [P, P])
        K.iota_row = sb("iota_row", [P, P])
        K.iota_part = sb("iota_part", [P, 1])
        K.ones = sb("ones", [P, P])
        K.zeros = sb("zeros", [P, BANK])
        K.dl = sb("dl", [P, SLOTS])
        K.dl_end = sb("dl_end", [P, SLOTS])
        K.src_idx = sb("src_idx", [P, SLOTS], I32)
        K.rel_idx = sb("rel_idx", [P, SLOTS], I32)
        K.blk_i = sb("blk_i", [P, SLOTS], I32)
        K.x = sb("x_nodes", [P, NB, F])
        K.deg, K.deg1, K.has, K.rdeg, K.dis = (sb(n, [P, NB]) for n in ("deg", "deg1", "has", "rdeg", "dis"))
        K.dl_rows = dram("dl_rows", [SLOTS, P])
        K.pen_rows = dram("pen_rows", [SLOTS, P])
        K.attr_rows = dram("attr_rows", [3, SLOTS, P])
        K.tab64 = dram("tab64", [NB * P, F])
        K.tab_gat1 = dram("tab_gat1", [NB * P, F + HEADS])
        K.tab_gat2 = dram("tab_gat2", [NB * P, F + 1])
        K.tab_rel = dram("tab_rel", [NB * P, REL * F])
        K.tab_vec = dram("tab_vec", [NB * P, 2 * F])
        K.rstd_rows = dram("rstd_rows", [SLOTS, P])
        K.enc = dram("enc", [F, SLOTS * P])
        with nc.cleanup_on_exit():
            build_slots(nc, K, A["dst"], A["src"], A["edge_type_32"], A["edge_attr_3"])
            count_degrees(nc, K)
        with nc.cleanup_on_exit():
            appnp(nc, K, A["x"], A["L0_gnn_alpha"])
        with nc.cleanup_on_exit():
            gat(nc, K, A)
        with nc.cleanup_on_exit():
            relational(nc, K, A)
        with nc.cleanup_on_exit():
            encode_edges(nc, K, A)
        with nc.cleanup_on_exit():
            vector_attention(nc, K, A)
        store_out(nc, K, out)


_INS = ['x', 'src', 'dst', 'edge_attr_3', 'edge_type_32', 'L0_gnn_alpha', 'L1_gnn_W1', 'L1_gnn_a_src1', 'L1_gnn_a_dst1',
        'L1_gnn_b1', 'L1_gnn_W2', 'L1_gnn_a_src2', 'L1_gnn_a_dst2', 'L1_gnn_b2', 'L2_gnn_basis', 'L2_gnn_coeff',
        'L2_gnn_self_weight', 'L2_gnn_bias', 'L3_gnn_Wd1', 'L3_gnn_bd1', 'L3_gnn_g1', 'L3_gnn_b1', 'L3_gnn_Wd2',
        'L3_gnn_bd2', 'L3_gnn_g2', 'L3_gnn_b2', 'L3_gnn_W1', 'L3_gnn_W2', 'L3_gnn_W3']


def kernel(**inputs):
    import numpy as _np
    import concourse.bacc as _bacc
    from concourse import mybir as _mybir
    from concourse.bass_utils import run_bass_kernel_spmd as _run

    nc = _bacc.Bacc("TRN2", target_bir_lowering=False, num_devices=1)
    arrays, args = {}, {}
    for name in _INS:
        a = _np.ascontiguousarray(inputs[name])
        arrays[f"in_{name}_dram"] = a
        args[name] = nc.dram_tensor(f"in_{name}_dram", a.shape, _mybir.dt.from_np(a.dtype), kind="ExternalInput").ap()
    out = nc.dram_tensor("out_0_dram", (N, F), FP32, kind="ExternalOutput").ap()
    build(nc, args, out)
    r = _run(nc, [arrays], core_ids=[0])
    return r.results[0]["out_0_dram"]
```

```python
import concourse.bass as bass
from concourse import mybir
from contextlib import ExitStack, contextmanager

FP32 = mybir.dt.float32
I32 = mybir.dt.int32
ALU = mybir.AluOpType
ACT = mybir.ActivationFunctionType
AX = mybir.AxisListType

P = 128
N = 3125
F = 64
E = 50000
REL = 32
NBASE = 30
HEADS = 4
NB = -(-N // P)
NFULL = N // P
NREM = N - NFULL * P
T = -(-E // P)
TG = -(-T // P)
SLOTS = -(-(T + NB - 1) // 16) * 16
SG = SLOTS // 4
CH = 4
CW = CH * P
ITERS = SLOTS // (2 * CH)
BANK = 512
BIG = 1.0e30
EPS = 1.0e-5


class Link:

    def __init__(self, eng, sem, per=0):
        self.eng, self.sem, self.per, self.base, self.n = eng, sem, per, 0, 0

    def turn(self, it):
        self.base, self.n = it * self.per, 0

    def __call__(self, ins):
        self.n += 1
        ins.then_inc(self.sem, 1)
        self.eng.wait_ge(self.sem, self.base + self.n)


@contextmanager
def semaphore(nc, name):
    yield nc.alloc_semaphore(name=name)


class Space:
    pass


def bcast_rows(ap, parts):
    return ap.rearrange("(o n) -> o n", o=1).broadcast_to([parts, ap.shape[0]])


def node_rows(tab):
    return tab.rearrange("(b p) c -> p b c", p=P)


def build_slots(nc, K, dst, src, edge_type, edge_attr):
    ctx = ExitStack()
    with ctx:
        def sb(name, shape, dt=FP32):
            return ctx.enter_context(nc.sbuf_tensor(name, shape, dt))

        def sem(name):
            return ctx.enter_context(semaphore(nc, name))

        NARR = 5
        dst_i, prev_i, next_i, src_i, typ_i = (sb(n, [P, TG, P], I32) for n in
                                               ("dst_i", "prev_i", "next_i", "src_i", "typ_i"))
        raw = sb("raw", [P, TG, NARR, P])
        att = sb("att", [P, TG, 3 * P])
        thr = sb("thr", [P, NB - 1])
        cmp0 = sb("cmp0", [P, TG, NB - 1])
        cmp1 = sb("cmp1", [P, TG, NB - 1])
        bmin, bmax, dmax, live, cnt, cum, cumex, bmc = (sb(n, [P, TG]) for n in
                                                       ("bmin", "bmax", "dmax", "live", "cnt", "cum", "cumex", "bmc"))
        bmcb = sb("bmcb", [P, TG, P])
        tri = sb("tri", [P, P])
        ones = sb("ones_sq", [P, P])
        iota_s = sb("iota_s", [P, SLOTS])
        iota_g = sb("iota_g", [P, 4])
        own = sb("own", [P, TG, SLOTS])
        ge = sb("ge", [P, SLOTS])
        blk = sb("blk", [P, SLOTS])
        tmp = sb("tmp", [P, SLOTS])
        tmp2 = sb("tmp2", [P, SLOTS])
        rows = sb("rows", [P, 4, 2, P])
        arows = sb("arows", [P, 4, 3, P])
        bcol = sb("bcol", [P, 4])

        pads = sem("pads")
        loads = sem("edge_loads")
        iotas = sem("iotas")
        tri0 = sem("tri0")
        dve = sem("slot_dve")
        counted = sem("tiles_counted")
        cum_ready = sem("cum_ready")
        own_ready = sem("own_ready")
        slots_ready = sem("slots_ready")
        rows_ready = sem("rows_ready")
        rows_taken = sem("rows_taken")
        rows_out = sem("rows_out")
        ident0 = sem("ident0")

        block = ctx.enter_context(nc.Block())
        G3 = TG - 1
        full = T - 1 - G3 * P
        last = E - (T - 1) * P

        @block.gpsimd
        def _(pool):
            for t, v in ((dst_i, -1), (prev_i, -5), (next_i, -1), (src_i, 0), (typ_i, 0)):
                pool.memset(t[:, :, :], v).then_inc(pads, 1)
            pool.memset(att[:, :, :], 0.0).then_inc(pads, 1)
            pool.iota(thr[:, :], pattern=[[P, NB - 1]], base=P, channel_multiplier=0,
                      allow_small_or_imprecise_dtypes=True).then_inc(iotas, 1)
            pool.iota(iota_s[:, :], pattern=[[1, SLOTS]], base=0, channel_multiplier=0,
                      allow_small_or_imprecise_dtypes=True).then_inc(iotas, 1)
            pool.iota(iota_g[:, :], pattern=[[SG, 4]], base=0, channel_multiplier=1,
                      allow_small_or_imprecise_dtypes=True).then_inc(iotas, 1)
            pool.iota(K.iota_row[:, :], pattern=[[1, P]], base=0, channel_multiplier=0,
                      allow_small_or_imprecise_dtypes=True).then_inc(iotas, 1)
            pool.iota(K.iota_part[:, :], pattern=[[0, 1]], base=0, channel_multiplier=1,
                      allow_small_or_imprecise_dtypes=True).then_inc(iotas, 1)
            pool.memset(tri[:, :], 1.0).then_inc(tri0, 1)
            pool.memset(ones[:, :], 1.0).then_inc(tri0, 1)
            pool.memset(K.ones[:, :], 1.0).then_inc(tri0, 1)
            pool.memset(K.zeros[:, :], 0.0).then_inc(tri0, 1)
            pool.memset(K.ident[:, :], 0.0).then_inc(ident0, 1)
            pool.wait_ge(tri0, 4)
            pool.affine_select(out=tri[:, :], in_=tri[:, :], compare_op=ALU.is_ge, fill=0.0, base=0,
                               pattern=[[1, P]], channel_multiplier=-1).then_inc(iotas, 1)
            pool.wait_ge(ident0, 1)
            pool.affine_select(out=K.ident[:, :], in_=K.ident[:, :], compare_op=ALU.not_equal, fill=1.0, base=0,
                               pattern=[[-1, P]], channel_multiplier=1).then_inc(iotas, 1)

        @block.sync
        def _(sp):
            sp.wait_ge(pads, 6)
            body = G3 * P * P
            for t, a in ((dst_i, dst), (src_i, src), (typ_i, edge_type)):
                sp.dma_start(t[:, 0:G3, :], a[0:body].rearrange("(g p e) -> p g e", p=P, e=P)).then_inc(loads, 16)
                sp.dma_start(t[0:full, G3, :], a[body:body + full * P].rearrange("(p e) -> p e", e=P)).then_inc(loads, 16)
                sp.dma_start(t[full:full + 1, G3, 0:last],
                             a[E - last:E].rearrange("(o e) -> o e", o=1)).then_inc(loads, 16)
            sp.dma_start(next_i[:, 0:G3, :], dst[1:body + 1].rearrange("(g p e) -> p g e", p=P, e=P)).then_inc(loads, 16)
            sp.dma_start(next_i[0:full, G3, :],
                         dst[body + 1:body + 1 + full * P].rearrange("(p e) -> p e", e=P)).then_inc(loads, 16)
            sp.dma_start(next_i[full:full + 1, G3, 0:last - 1],
                         dst[E - last + 1:E].rearrange("(o e) -> o e", o=1)).then_inc(loads, 16)
            sp.dma_start(prev_i[0:1, 0, 1:P], dst[0:P - 1].rearrange("(o e) -> o e", o=1)).then_inc(loads, 16)
            sp.dma_start(prev_i[1:P, 0, :], dst[P - 1:P * P - 1].rearrange("(p e) -> p e", e=P)).then_inc(loads, 16)
            sp.dma_start(prev_i[:, 1:G3, :], dst[P * P - 1:body - 1].rearrange("(g p e) -> p g e", p=P, e=P)).then_inc(loads, 16)
            sp.dma_start(prev_i[0:full, G3, :],
                         dst[body - 1:body - 1 + full * P].rearrange("(p e) -> p e", e=P)).then_inc(loads, 16)
            sp.dma_start(prev_i[full:full + 1, G3, 0:last],
                         dst[E - last - 1:E - 1].rearrange("(o e) -> o e", o=1)).then_inc(loads, 16)
            sp.dma_start(att[:, 0:G3, :],
                         edge_attr[0:body, :].rearrange("(g p e) a -> p g (e a)", p=P, e=P)).then_inc(loads, 16)
            sp.dma_start(att[0:full, G3, :],
                         edge_attr[body:body + full * P, :].rearrange("(p e) a -> p (e a)", e=P)).then_inc(loads, 16)
            sp.dma_start(att[full:full + 1, G3, 0:3 * last],
                         edge_attr[E - last:E, :].rearrange("(o e) a -> o (e a)", o=1)).then_inc(loads, 16)
            for sg in range(4):
                sp.wait_ge(rows_taken, 1 + sg)
                sp.dma_start(K.dl_rows[sg * SG:(sg + 1) * SG, :], rows[0:SG, sg, 0, :]).then_inc(rows_out, 16)
                sp.dma_start(K.pen_rows[sg * SG:(sg + 1) * SG, :], rows[0:SG, sg, 1, :]).then_inc(rows_out, 16)
                for a in range(3):
                    sp.dma_start(K.attr_rows[a, sg * SG:(sg + 1) * SG, :], arows[0:SG, sg, a, :]).then_inc(rows_out, 16)
            sp.wait_ge(rows_out, 16 * 5 * 4)

        @block.vector
        def _(v):
            link = Link(v, dve)
            v.wait_ge(loads, 16 * 20)
            v.wait_ge(iotas, 7)
            link(v.tensor_copy(raw[:, :, 0, :], dst_i[:, :, :]))
            link(v.tensor_tensor(raw[:, :, 1, :], dst_i[:, :, :], prev_i[:, :, :], ALU.is_equal))
            link(v.tensor_copy(raw[:, :, 2, :], src_i[:, :, :]))
            link(v.tensor_copy(raw[:, :, 3, :], typ_i[:, :, :]))
            link(v.tensor_tensor(raw[:, :, 4, :], dst_i[:, :, :], next_i[:, :, :], ALU.not_equal))
            link(v.tensor_tensor(cmp0[:, :, :], raw[:, :, 0, 0:1].broadcast_to([P, TG, NB - 1]),
                                 thr[:, :].unsqueeze(1).broadcast_to([P, TG, NB - 1]), ALU.is_ge))
            link(v.tensor_reduce(bmin[:, :], cmp0[:, :, :], AX.X, ALU.add))
            link(v.tensor_reduce(dmax[:, :], raw[:, :, 0, :], AX.X, ALU.max))
            link(v.tensor_tensor(cmp1[:, :, :], dmax[:, :].unsqueeze(2).broadcast_to([P, TG, NB - 1]),
                                 thr[:, :].unsqueeze(1).broadcast_to([P, TG, NB - 1]), ALU.is_ge))
            link(v.tensor_reduce(bmax[:, :], cmp1[:, :, :], AX.X, ALU.add))
            link(v.tensor_scalar(live[:, :], raw[:, :, 0, 0], 0.0, None, ALU.is_ge))
            link(v.scalar_tensor_tensor(out=cnt[:, :], in0=bmax[:, :], scalar=1.0, in1=bmin[:, :],
                                        op0=ALU.add, op1=ALU.subtract))
            link(v.tensor_tensor(cnt[:, :], cnt[:, :], live[:, :], ALU.mult))
            v.sem_inc(counted, 1)
            v.wait_ge(cum_ready, 1)
            link(v.tensor_copy(cum[:, :], K.ps[:, 0:TG]))
            link(v.tensor_tensor(cumex[:, :], cum[:, :], cnt[:, :], ALU.subtract))
            link(v.tensor_tensor(bmc[:, :], bmin[:, :], cumex[:, :], ALU.subtract))
            link(v.tensor_copy(bmcb[:, :, :], bmc[:, :].unsqueeze(2).broadcast_to([P, TG, P])))
            for g in range(TG):
                link(v.tensor_scalar(ge[:, :], iota_s[:, :], cum[:, g:g + 1], None, ALU.is_ge))
                link(v.scalar_tensor_tensor(out=own[:, g, :], in0=iota_s[:, :], scalar=cumex[:, g:g + 1],
                                            in1=ge[:, :], op0=ALU.is_ge, op1=ALU.subtract))
            v.sem_inc(own_ready, 1)
            v.wait_ge(slots_ready, 5)
            link(v.tensor_tensor(blk[:, :], K.ps[:, 4 * BANK:4 * BANK + SLOTS], iota_s[:, :], ALU.add))
            link(v.tensor_scalar(blk[:, :], blk[:, :], float(NB - 1), None, ALU.min))
            link(v.tensor_copy(K.blk_i[:, :], blk[:, :]))
            link(v.scalar_tensor_tensor(out=K.dl[:, :], in0=blk[:, :], scalar=-float(P),
                                        in1=K.ps[:, 0:SLOTS], op0=ALU.mult, op1=ALU.add))
            link(v.tensor_copy(K.src_idx[:, :], K.ps[:, BANK:BANK + SLOTS]))
            link(v.tensor_copy(tmp[:, :], K.ps[:, BANK:BANK + SLOTS]))
            link(v.scalar_tensor_tensor(out=tmp2[:, :], in0=tmp[:, :], scalar=float(REL),
                                        in1=K.ps[:, 2 * BANK:2 * BANK + SLOTS], op0=ALU.mult, op1=ALU.add))
            link(v.tensor_copy(K.rel_idx[:, :], tmp2[:, :]))
            link(v.scalar_tensor_tensor(out=tmp[:, :], in0=K.dl[:, :], scalar=1.0,
                                        in1=K.ps[:, 3 * BANK:3 * BANK + SLOTS], op0=ALU.add, op1=ALU.mult))
            link(v.tensor_scalar(K.dl_end[:, :], tmp[:, :], -1.0, None, ALU.add))
            for sg in range(4):
                v.wait_ge(rows_ready, sg + 1)
                o = 5 * BANK
                link(v.tensor_tensor(bcol[0:SG, sg:sg + 1], K.ps[0:SG, o + 2 * P:o + 2 * P + 1],
                                     iota_g[0:SG, sg:sg + 1], ALU.add))
                link(v.tensor_scalar(bcol[0:SG, sg:sg + 1], bcol[0:SG, sg:sg + 1], float(NB - 1), -float(P),
                                     ALU.min, ALU.mult))
                link(v.tensor_scalar(rows[0:SG, sg, 0, :], K.ps[0:SG, o:o + P], bcol[0:SG, sg:sg + 1], None, ALU.add))
                link(v.tensor_scalar(rows[0:SG, sg, 1, :], K.ps[0:SG, o + P:o + 2 * P], -1.0, BIG, ALU.add, ALU.mult))
                o = 6 * BANK
                link(v.tensor_copy(arows[0:SG, sg, :, :], K.ps[0:SG, o:o + 3 * P].rearrange("p (e a) -> p a e", a=3)))
                v.sem_inc(rows_taken, 1)

        @block.tensor
        def _(pe):
            pe.wait_ge(counted, 1)
            for g in range(TG):
                pe.matmul(K.ps[:, g:g + 1], tri[:, :], cnt[:, g:g + 1], start=True, stop=g == 0, skip_group_check=True)
                for h in range(g):
                    ins = pe.matmul(K.ps[:, g:g + 1], ones[:, :], cnt[:, h:h + 1], start=False, stop=h == g - 1,
                                    skip_group_check=True)
            ins.then_inc(cum_ready, 1)
            pe.wait_ge(own_ready, 1)
            for b, k in enumerate((0, 2, 3, 4, None)):
                for g in range(TG):
                    lhs = bmcb[:, g, :] if k is None else raw[:, g, k, :]
                    ins = pe.matmul(K.ps[:, b * BANK:b * BANK + SLOTS], lhs, own[:, g, :], start=g == 0, stop=g == TG - 1)
                ins.then_inc(slots_ready, 1)
            for sg in range(4):
                if sg:
                    pe.wait_ge(rows_taken, sg)
                part = own[:, :, sg * SG:(sg + 1) * SG]
                for g in range(TG):
                    pe.matmul(K.ps[0:SG, 5 * BANK:5 * BANK + 2 * P], part[:, g, :],
                              raw[:, g, 0:2, :].rearrange("p k e -> p (k e)"), start=g == 0, stop=g == TG - 1)
                for g in range(TG):
                    pe.matmul(K.ps[0:SG, 5 * BANK + 2 * P:5 * BANK + 2 * P + 1], part[:, g, :], bmc[:, g:g + 1],
                              start=False, stop=g == TG - 1, skip_group_check=True)
                for g in range(TG):
                    ins = pe.matmul(K.ps[0:SG, 6 * BANK:6 * BANK + 3 * P], part[:, g, :], att[:, g, :],
                                    start=g == 0, stop=g == TG - 1)
                ins.then_inc(rows_ready, 1)


def slot_blocks(nc, K, eng, it):
    return nc.values_load_multi_w_load_instructions(
        K.blk_i[0:1, bass.ds(it * (2 * CH), 2 * CH)], engines=[eng.engine], min_val=0, max_val=NB - 1,
        skip_runtime_bounds_check_because="build_slots clamps every block number to 0..NB - 1")[1]


def onehot(v, out, iota_row, dl_chunk):
    return v.tensor_tensor(out, iota_row.unsqueeze(1).broadcast_to([P, CH, P]),
                           dl_chunk.unsqueeze(2).broadcast_to([P, CH, P]), ALU.is_equal)


def clear_banks(pe, K, first, count):
    for b in range(first, first + count):
        ins = pe.matmul(K.ps[:, b * BANK:(b + 1) * BANK], K.zeros[:, 0:P], K.zeros[:, :], start=True, stop=False,
                        skip_group_check=True)
    return ins


def count_degrees(nc, K):
    ctx = ExitStack()
    with ctx:
        hot = [ctx.enter_context(nc.sbuf_tensor(f"hot{k}", [P, CH, P], FP32)) for k in range(2)]
        hot_ready = ctx.enter_context(semaphore(nc, "deg_hot_ready"))
        hot_free = ctx.enter_context(semaphore(nc, "deg_hot_free"))
        deg_link = ctx.enter_context(semaphore(nc, "deg_link"))
        root_ready = ctx.enter_context(semaphore(nc, "deg_root"))
        block = ctx.enter_context(nc.Block())

        @block.vector
        def _(v):
            with v.Fori(0, ITERS) as it:
                for k in range(2):
                    v.wait_ge(hot_free, it * 2 + k + 1)
                    onehot(v, hot[k][:, :, :], K.iota_row[:, :],
                           K.dl[:, bass.ds(it * (2 * CH) + k * CH, CH)]).then_inc(hot_ready, 1)
            link = Link(v, deg_link)
            v.wait_ge(hot_free, 2 + 2 * ITERS)
            link(v.tensor_copy(K.deg[:, :], K.ps[:, 0:NB]))
            link(v.tensor_scalar(K.deg1[:, :], K.deg[:, :], 1.0, None, ALU.max))
            link(v.tensor_scalar(K.has[:, :], K.deg[:, :], 0.0, None, ALU.is_gt))
            link(v.reciprocal(K.rdeg[:, :], K.deg1[:, :]))
            v.wait_ge(root_ready, 1)
            link(v.tensor_tensor(K.dis[:, :], K.dis[:, :], K.has[:, :], ALU.mult))

        @block.scalar
        def _(act):
            act.wait_ge(deg_link, 4)
            act.activation(K.dis[:, :], K.rdeg[:, :], ACT.Sqrt).then_inc(root_ready, 1)

        @block.tensor
        def _(pe):
            clear_banks(pe, K, 0, 1).then_inc(hot_free, 2)
            with pe.Fori(0, ITERS) as it:
                blocks = slot_blocks(nc, K, pe, it)
                for k in range(2):
                    pe.wait_ge(hot_ready, it * 2 + k + 1)
                    for j in range(CH):
                        b = blocks[k * CH + j]
                        ins = pe.matmul(K.ps[:, bass.ds(b, 1)], hot[k][:, j, :], K.ones[:, 0:1], start=False, stop=False,
                                        skip_group_check=True)
                    ins.then_inc(hot_free, 1)


def pipeline(eng, stages, before_turn=None):
    edge = -(-max(lag for lag, _ in stages) // 2)

    def turn(t):
        for k in range(2):
            for lag, step in stages:
                c = t * 2 + (k - lag)
                if isinstance(t, int) and not 0 <= c < 2 * ITERS:
                    continue
                step(c, (k - lag) % 2, t + (k - lag) // 2)

    for t in range(edge):
        turn(t)
    with eng.Fori(edge, ITERS) as t:
        turn(t)
    for t in range(ITERS, ITERS + edge):
        turn(t)


def chunk_blocks(nc, K, eng, c):
    return nc.values_load_multi_w_load_instructions(
        K.blk_i[0:1, bass.ds(c * CH, CH)], engines=[eng.engine], min_val=0, max_val=NB - 1,
        skip_runtime_bounds_check_because="build_slots clamps every block number to 0..NB - 1")[1]


def gather(pool, ring, idx, table, rows_in):
    for j in range(CH):
        pool.indirect_dma_start(out=ring[:, j, :], out_offset=None, in_=table,
                                in_offset=bass.IndirectOffsetOnAxis(ap=idx[:, j:j + 1], axis=0)).then_inc(rows_in, 16)


class NoSide:
    def sync(self, sp): return []
    def vector(self, v): return []
    def scalar(self, act): return []
    def tensor(self, pe): return []
    def finish(self, sp): pass


def gather_sum(nc, K, table, index, tag, side):
    ctx = ExitStack()
    with ctx:
        hot = [ctx.enter_context(nc.sbuf_tensor(f"{tag}_hot{k}", [P, CH, P], FP32)) for k in range(2)]
        ring = [ctx.enter_context(nc.sbuf_tensor(f"{tag}_ring{k}", [P, CH, F], FP32)) for k in range(2)]
        idx = [ctx.enter_context(nc.sbuf_tensor(f"{tag}_idx{k}", [P, CH], I32)) for k in range(2)]
        hot_ready = ctx.enter_context(semaphore(nc, f"{tag}_hot_ready"))
        idx_ready = ctx.enter_context(semaphore(nc, f"{tag}_idx_ready"))
        rows_in = [ctx.enter_context(semaphore(nc, f"{tag}_rows_in{k}")) for k in range(2)]
        chunk_free = ctx.enter_context(semaphore(nc, f"{tag}_chunk_free"))
        block = ctx.enter_context(nc.Block())

        @block.gpsimd
        def _(pool):
            def rows(c, k, turn):
                pool.wait_ge(idx_ready, c + 1)
                pool.nop(nofuse=True)
                gather(pool, ring[k], idx[k], table, rows_in[k])
            pipeline(pool, [(0, rows)])

        @block.vector
        def _(v):
            def prepare(c, k, turn):
                v.wait_ge(chunk_free, c + 1)
                v.tensor_copy(idx[k][:, :], index[:, bass.ds(c * CH, CH)]).then_inc(idx_ready, 1)
                onehot(v, hot[k][:, :, :], K.iota_row[:, :], K.dl[:, bass.ds(c * CH, CH)]).then_inc(hot_ready, 1)
            pipeline(v, [(0, prepare)] + side.vector(v))

        @block.tensor
        def _(pe):
            clear_banks(pe, K, 0, 4).then_inc(chunk_free, 2)

            def add(c, k, turn):
                blocks = chunk_blocks(nc, K, pe, c)
                pe.wait_ge(hot_ready, c + 1)
                pe.wait_ge(rows_in[k], turn * (16 * CH) + 16 * CH)
                pe.nop(nofuse=True)
                for j in range(CH):
                    ins = pe.matmul(K.ps[:, bass.ds(blocks[j] * F, F)], hot[k][:, j, :], ring[k][:, j, :],
                                    start=False, stop=False, skip_group_check=True)
                ins.then_inc(chunk_free, 1)
            pipeline(pe, [(0, add)] + side.tensor(pe))

        @block.scalar
        def _(act):
            stages = side.scalar(act)
            if stages:
                pipeline(act, stages)

        @block.sync
        def _(sp):
            stages = side.sync(sp)
            if stages:
                pipeline(sp, stages)
            side.finish(sp)


def per_node(ap, width=F):
    return ap.unsqueeze(2).broadcast_to([P, NB, width])


def per_feature(ap):
    return ap.unsqueeze(1).broadcast_to([P, NB, F])


def sums(K):
    return K.ps[:, 0:NB * F].rearrange("p (b c) -> p b c", c=F)


def layernorm_steps(v, link, K, y, out, sq, mean, var, std_wanted, std_ready):
    link(v.tensor_reduce(mean, y, AX.X, ALU.add))
    link(v.tensor_scalar(mean, mean, -1.0 / F, None, ALU.mult))
    link(v.tensor_tensor(y, y, per_node(mean), ALU.add))
    link(v.tensor_tensor(sq, y, y, ALU.mult))
    link(v.tensor_reduce(var, sq, AX.X, ALU.add))
    link(v.tensor_scalar(var, var, 1.0 / F, EPS, ALU.mult, ALU.add))
    v.sem_inc(std_wanted, 1)
    v.wait_ge(std_ready, 1)
    link(v.reciprocal(var, var))
    link(v.tensor_tensor(out, y, per_node(var), ALU.mult))


def appnp(nc, K, x_in, alpha, enc):
    ctx = ExitStack()
    with ctx:
        scaled = ctx.enter_context(nc.sbuf_tensor("scaled", [P, NB, F], FP32))
        total = ctx.enter_context(nc.sbuf_tensor("total", [P, NB, F], FP32))
        hop = ctx.enter_context(nc.sbuf_tensor("hop", [P, NB, F], FP32))
        al = ctx.enter_context(nc.sbuf_tensor("al", [P, 3], FP32))
        mean = ctx.enter_context(nc.sbuf_tensor("mean0", [P, NB], FP32))
        var = ctx.enter_context(nc.sbuf_tensor("var0", [P, NB], FP32))

        def prepare():
            c2 = ExitStack()
            with c2:
                x_loaded = c2.enter_context(semaphore(nc, "x_loaded"))
                x_pad = c2.enter_context(semaphore(nc, "x_pad"))
                made = c2.enter_context(semaphore(nc, "a_made"))
                stored = c2.enter_context(semaphore(nc, "a_stored"))
                block = c2.enter_context(nc.Block())

                @block.sync
                def _(sp):
                    sp.wait_ge(x_pad, 1)
                    sp.dma_start(K.x[:, 0:NFULL, :], node_rows(x_in[0:NFULL * P, :])).then_inc(x_loaded, 16)
                    sp.dma_start(K.x[0:NREM, NFULL, :], x_in[NFULL * P:N, :]).then_inc(x_loaded, 16)
                    sp.dma_start(al[:, :], bcast_rows(alpha, P)).then_inc(x_loaded, 16)
                    sp.wait_ge(made, 1)
                    sp.dma_start(node_rows(K.tab64), scaled[:, :, :]).then_inc(stored, 16)
                    sp.wait_ge(stored, 16)

                @block.vector
                def _(v):
                    v.memset(K.x[:, NFULL, :], 0.0).then_inc(x_pad, 1)
                    v.wait_ge(x_loaded, 48)
                    v.tensor_tensor(scaled[:, :, :], K.x[:, :, :], per_node(K.dis[:, :]), ALU.mult).then_inc(made, 1)

        def between(second):
            c2 = ExitStack()
            with c2:
                made = c2.enter_context(semaphore(nc, f"a_made{second}"))
                steps = c2.enter_context(semaphore(nc, f"a_steps{second}"))
                stored = c2.enter_context(semaphore(nc, f"a_stored{second}"))
                wanted = c2.enter_context(semaphore(nc, f"a_wanted{second}"))
                ready = c2.enter_context(semaphore(nc, f"a_ready{second}"))
                block = c2.enter_context(nc.Block())

                @block.vector
                def _(v):
                    link = Link(v, steps)
                    link(v.tensor_tensor(hop[:, :, :], sums(K), per_node(K.dis[:, :]), ALU.mult))
                    if not second:
                        v.tensor_tensor(scaled[:, :, :], hop[:, :, :], per_node(K.dis[:, :]), ALU.mult).then_inc(made, 1)
                        link(v.tensor_scalar(total[:, :, :], K.x[:, :, :], al[:, 0:1], None, ALU.mult))
                    link(v.scalar_tensor_tensor(out=total[:, :, :], in0=hop[:, :, :], scalar=al[:, 1 + second:2 + second],
                                                in1=total[:, :, :], op0=ALU.mult, op1=ALU.add))
                    if second:
                        link(v.tensor_tensor(total[:, :, :], total[:, :, :], K.x[:, :, :], ALU.add))
                        layernorm_steps(v, link, K, total[:, :, :], K.x[:, :, :], hop[:, :, :], mean[:, :], var[:, :],
                                        wanted, ready)

                if second:
                    @block.scalar
                    def _(act):
                        act.wait_ge(wanted, 1)
                        act.activation(var[:, :], var[:, :], ACT.Sqrt).then_inc(ready, 1)
                else:
                    @block.sync
                    def _(sp):
                        sp.wait_ge(made, 1)
                        sp.dma_start(node_rows(K.tab64), scaled[:, :, :]).then_inc(stored, 16)
                        sp.wait_ge(stored, 16)

        prepare()
        with ExitStack() as c:
            gather_sum(nc, K, K.tab64, K.src_idx, "hop1", FirstVariance(nc, K, c, enc))
        between(0)
        rows_of(nc, K, enc.var[:, :], "v1")
        with ExitStack() as c:
            gather_sum(nc, K, K.tab64, K.src_idx, "hop2", SecondProduct(nc, K, c, enc))
        between(1)


def store_out(nc, K, out):
    with semaphore(nc, "out_stored") as stored, nc.Block() as block:
        @block.sync
        def _(sp):
            sp.dma_start(node_rows(out[0:NFULL * P, :]), K.x[:, 0:NFULL, :]).then_inc(stored, 16)
            sp.dma_start(out[NFULL * P:N, :], K.x[0:NREM, NFULL, :]).then_inc(stored, 16)
            sp.wait_ge(stored, 32)



def transpose_nodes(nc, K, nodes, out, tag):
    with semaphore(nc, f"{tag}_turned") as turned, semaphore(nc, f"{tag}_taken") as taken, nc.Block() as block:
        groups = [(q, min(q + 4, NB)) for q in range(0, NB, 4)]

        @block.tensor
        def _(pe):
            for i, (lo, hi) in enumerate(groups):
                for b in range(lo, hi):
                    o = i * BANK + (b - lo) * P
                    ins = pe.transpose(K.ps[0:F, o:o + P], nodes[:, b, :], K.ident[:, :])
                ins.then_inc(turned, 1)

        @block.vector
        def _(v):
            for i, (lo, hi) in enumerate(groups):
                v.wait_ge(turned, i + 1)
                v.tensor_copy(out[:, lo * P:hi * P], K.ps[0:F, i * BANK:i * BANK + (hi - lo) * P]).then_inc(taken, 1)
            v.wait_ge(taken, len(groups))


def project(nc, K, xT, w, cols, out, tag):
    per = BANK // cols
    groups = [(q, min(q + per, NB)) for q in range(0, NB, per)]
    with semaphore(nc, f"{tag}_made") as made, semaphore(nc, f"{tag}_copied") as copied, nc.Block() as block:
        @block.tensor
        def _(pe):
            for i, (lo, hi) in enumerate(groups):
                if i >= 8:
                    pe.wait_ge(copied, i - 7)
                for b in range(lo, hi):
                    o = (i % 8) * BANK + (b - lo) * cols
                    ins = pe.matmul(K.ps[:, o:o + cols], xT[:, b * P:(b + 1) * P], w, start=True, stop=True,
                                    skip_group_check=True)
                ins.then_inc(made, 1)

        @block.vector
        def _(v):
            for i, (lo, hi) in enumerate(groups):
                v.wait_ge(made, i + 1)
                o = (i % 8) * BANK
                v.tensor_copy(out[:, lo:hi, :], K.ps[:, o:o + (hi - lo) * cols].rearrange("p (b c) -> p b c", c=cols)
                              ).then_inc(copied, 1)
            v.wait_ge(copied, len(groups))


def store_table(nc, K, table, pieces, tag):
    with semaphore(nc, f"{tag}_stored") as stored, nc.Block() as block:
        @block.sync
        def _(sp):
            for col, width, ap in pieces:
                sp.dma_start(node_rows(table)[:, :, col:col + width], ap).then_inc(stored, 16)
            sp.wait_ge(stored, 16 * len(pieces))


def attention(nc, K, H, table, x, als, ald, z, tag):
    ctx = ExitStack()
    with ctx:
        GW = F + H
        HP = min(H, 2)

        def sb(name, shape, dt=FP32):
            return ctx.enter_context(nc.sbuf_tensor(f"{tag}_{name}", shape, dt))

        kept = sb("kept", [P, SLOTS, GW])
        hot = [sb(f"hot{k}", [P, CH, P]) for k in range(2)]
        spread = sb("spread", [P, NB, 2, H])
        selfw = sb("selfw", [P, NB, H])
        t0, t1 = sb("t0", [P, NB, H]), sb("t1", [P, NB, H])
        weight = sb("weight", [P, SLOTS, H])

        def gather_and_max():
            c = ExitStack()
            with c:
                def sb2(name, shape, dt=FP32):
                    return c.enter_context(nc.sbuf_tensor(f"{tag}_{name}", shape, dt))

                def sem(name):
                    return c.enter_context(semaphore(nc, f"{tag}_{name}"))

                ring = [sb2(f"ring{k}", [P, CH, GW]) for k in range(2)]
                idx = [sb2(f"idx{k}", [P, CH], I32) for k in range(2)]
                pen = [sb2(f"pen{k}", [H, CW]) for k in range(2)]
                run = [sb2(f"run{k}", [H, CW]) for k in range(2)]
                mx = [sb2(f"mx{k}", [P, CH * H]) for k in range(2)]
                idx_ready, hot_ready, added = sem("idx_ready"), sem("hot_ready"), sem("added")
                rows_in = [sem(f"rows_in{k}") for k in range(2)]
                pen_in = [sem(f"pen_in{k}") for k in range(2)]
                rows_kept, turned, scanned, back, mx_ready, start = (sem(n) for n in (
                    "rows_kept", "turned", "scanned", "back", "mx_ready", "start"))
                block = c.enter_context(nc.Block())

                @block.gpsimd
                def _(pool):
                    def rows(c, k, turn):
                        pool.wait_ge(idx_ready, c + 1)
                        pool.nop(nofuse=True)
                        gather(pool, ring[k], idx[k], table, rows_in[k])
                    pipeline(pool, [(0, rows)])

                @block.sync
                def _(sp):
                    def penalties(c, k, turn):
                        sp.wait_ge(scanned, c + 1)
                        sp.dma_start(pen[k][:, :], bcast_chunk(K.pen_rows[bass.ds(c * CH, CH), :], H)).then_inc(pen_in[k], 16)
                    pipeline(sp, [(0, penalties)])

                @block.scalar
                def _(act):
                    act.sem_inc(rows_kept, 2)

                    def keep(c, k, turn):
                        act.wait_ge(rows_in[k], turn * (16 * CH) + 16 * CH)
                        act.copy(kept[:, bass.ds(c * CH, CH), :], ring[k][:, :, :]).then_inc(rows_kept, 1)

                    def maxima(c, k, turn):
                        act.wait_ge(back, c + 1)
                        act.wait_ge(added, c + 1)
                        act.copy(mx[k][:, :], K.ps[:, (3 + k) * BANK:(3 + k) * BANK + CH * H]).then_inc(mx_ready, 1)
                    pipeline(act, [(0, keep), (2, maxima)])

                @block.vector
                def _(v):
                    v.memset(run[1][:, :], -BIG).then_inc(start, 1)
                    v.wait_ge(start, 1)
                    v.sem_inc(scanned, 2)

                    def indices(c, k, turn):
                        v.wait_ge(rows_kept, c + 1)
                        v.wait_ge(turned, c + 1)
                        v.tensor_copy(idx[k][:, :], K.src_idx[:, bass.ds(c * CH, CH)]).then_inc(idx_ready, 1)

                    def scan(c, k, turn):
                        v.wait_ge(pen_in[k], turn * 16 + 16)
                        v.wait_ge(turned, c + 3)
                        if not (isinstance(c, int) and c < 2):
                            v.wait_ge(back, c - 1)
                        v.wait_ge(scanned, c + 2)
                        v.tensor_tensor_scan(run[k][:, :], pen[k][:, :], K.ps[0:H, (1 + k) * BANK:(2 + k) * BANK],
                                             run[1 - k][:, CW - 1:CW], ALU.add, ALU.max).then_inc(scanned, 1)

                    def ends(c, k, turn):
                        v.wait_ge(added, c + 1)
                        onehot(v, hot[k][:, :, :], K.iota_row[:, :], K.dl_end[:, bass.ds(c * CH, CH)]).then_inc(hot_ready, 1)
                    pipeline(v, [(0, indices), (1, scan), (2, ends)])

                @block.tensor
                def _(pe):
                    clear_banks(pe, K, 0, 1).then_inc(added, 2)
                    pe.sem_inc(turned, 2)

                    def turn_scores(c, k, turn):
                        pe.wait_ge(rows_in[k], turn * (16 * CH) + 16 * CH)
                        pe.wait_ge(scanned, c + 1)
                        pe.nop(nofuse=True)
                        for j in range(CH):
                            o = (1 + k) * BANK + j * P
                            ins = pe.transpose(K.ps[0:H, o:o + P], ring[k][:, j, F:GW], K.ident[:, :])
                        ins.then_inc(turned, 1)

                    def turn_back(c, k, turn):
                        pe.wait_ge(scanned, c + 3)
                        if not (isinstance(c, int) and c < 2):
                            pe.wait_ge(mx_ready, c - 1)
                        pe.nop(nofuse=True)
                        for j in range(CH):
                            o = (3 + k) * BANK + j * H
                            ins = pe.transpose(K.ps[:, o:o + H], run[k][:, j * P:(j + 1) * P], K.ident[0:H, 0:H])
                        ins.then_inc(back, 1)

                    def pick_ends(c, k, turn):
                        blocks = chunk_blocks(nc, K, pe, c)
                        pe.wait_ge(mx_ready, c + 1)
                        pe.wait_ge(hot_ready, c + 1)
                        pe.nop(nofuse=True)
                        for j in range(CH):
                            ins = pe.matmul(K.ps[:, bass.ds(blocks[j] * H, H)], hot[k][:, j, :], mx[k][:, j * H:(j + 1) * H],
                                            start=False, stop=False, skip_group_check=True)
                        ins.then_inc(added, 1)
                    pipeline(pe, [(0, turn_scores), (2, turn_back), (3, pick_ends)])

        def node_maxima():
            with semaphore(nc, f"{tag}_nm") as steps, semaphore(nc, f"{tag}_nmw") as wanted, \
                    semaphore(nc, f"{tag}_nmr") as ready, nc.Block() as block:
                mxs = K.ps[:, 0:NB * H].rearrange("p (b h) -> p b h", h=H)

                @block.vector
                def _(v):
                    link = Link(v, steps)
                    link(v.tensor_scalar(K.deg1[:, :], K.has[:, :], -1.0, BIG, ALU.add, ALU.mult))
                    link(v.tensor_tensor(t0[:, :, :], mxs, per_node(K.deg1[:, :], H), ALU.add))
                    link(v.tensor_tensor(t0[:, :, :], t0[:, :, :], als, ALU.max))
                    link(v.tensor_tensor(t0[:, :, :], t0[:, :, :], ald, ALU.add))
                    link(v.scalar_tensor_tensor(out=spread[:, :, 1, :], in0=t0[:, :, :], scalar=0.2, in1=t0[:, :, :],
                                                op0=ALU.mult, op1=ALU.max))
                    link(v.tensor_copy(spread[:, :, 0, :], ald))
                    link(v.tensor_tensor(t0[:, :, :], als, ald, ALU.add))
                    link(v.scalar_tensor_tensor(out=t1[:, :, :], in0=t0[:, :, :], scalar=0.2, in1=t0[:, :, :],
                                                op0=ALU.mult, op1=ALU.max))
                    link(v.tensor_tensor(t1[:, :, :], t1[:, :, :], spread[:, :, 1, :], ALU.subtract))
                    v.sem_inc(wanted, 1)

                @block.scalar
                def _(act):
                    act.wait_ge(wanted, 1)
                    act.activation(selfw[:, :, :], t1[:, :, :], ACT.Exp).then_inc(ready, 1)
                    act.wait_ge(ready, 1)

        def edge_weights():
            c = ExitStack()
            with c:
                def sem(name):
                    return c.enter_context(semaphore(nc, f"{tag}_{name}"))

                dlb = [c.enter_context(nc.sbuf_tensor(f"{tag}_dlb{k}", [P, CW], FP32)) for k in range(2)]
                cold = [c.enter_context(nc.sbuf_tensor(f"{tag}_cold{k}", [P, CW], FP32)) for k in range(2)]
                score = [c.enter_context(nc.sbuf_tensor(f"{tag}_score{k}", [P, CH, H], FP32)) for k in range(2)]
                dl_in = [sem(f"dl_in{k}") for k in range(2)]
                cold_ready, spread_done, scored, steps, weighed = (sem(n) for n in (
                    "cold_ready", "spread_done", "scored", "steps", "weighed"))
                block = c.enter_context(nc.Block())

                @block.sync
                def _(sp):
                    def targets(c, k, turn):
                        sp.wait_ge(cold_ready, c + 1)
                        sp.dma_start(dlb[k][:, :], bcast_chunk(K.dl_rows[bass.ds(c * CH, CH), :], P)).then_inc(dl_in[k], 16)
                    pipeline(sp, [(0, targets)])

                @block.vector
                def _(v):
                    v.sem_inc(cold_ready, 2)
                    link = Link(v, steps, per=4)

                    def build(c, k, turn):
                        v.wait_ge(dl_in[k], turn * 16 + 16)
                        v.wait_ge(spread_done, c + 1)
                        v.tensor_scalar(cold[k][:, :], dlb[k][:, :], K.iota_part[:, 0:1], None, ALU.is_equal
                                        ).then_inc(cold_ready, 1)

                    def scores(c, k, turn):
                        link.turn(c)
                        v.wait_ge(spread_done, c + 3)
                        v.wait_ge(weighed, c + 1)
                        got = K.ps[:, k * BANK:k * BANK + CH * 2 * H].rearrange("p (s t h) -> p s t h", t=2, h=H)
                        here = kept[:, bass.ds(c * CH, CH), :]
                        sc = score[k][:, :, :]
                        link(v.tensor_tensor(sc, here[:, :, F:GW], got[:, :, 0, :], ALU.add))
                        link(v.scalar_tensor_tensor(out=sc, in0=sc, scalar=0.2, in1=sc, op0=ALU.mult, op1=ALU.max))
                        link(v.tensor_tensor(sc, sc, got[:, :, 1, :], ALU.subtract))
                        link(v.tensor_scalar(sc, sc, 0.0, None, ALU.min))
                        v.sem_inc(scored, 1)
                    pipeline(v, [(0, build), (1, scores)])

                @block.scalar
                def _(act):
                    act.sem_inc(weighed, 2)

                    def weigh(c, k, turn):
                        act.wait_ge(scored, c + 1)
                        act.activation(weight[:, bass.ds(c * CH, CH), :], score[k][:, :, :], ACT.Exp).then_inc(weighed, 1)
                    pipeline(act, [(0, weigh)])

                @block.tensor
                def _(pe):
                    pe.sem_inc(spread_done, 2)
                    flat = spread[:, :, :, :].rearrange("p b t h -> p (b t h)")

                    def spread_out(c, k, turn):
                        blocks = chunk_blocks(nc, K, pe, c)
                        pe.wait_ge(cold_ready, c + 3)
                        pe.wait_ge(weighed, c + 1)
                        pe.nop(nofuse=True)
                        for j in range(CH):
                            o = k * BANK + j * 2 * H
                            ins = pe.matmul(K.ps[:, o:o + 2 * H], cold[k][:, j * P:(j + 1) * P],
                                            flat[:, bass.ds(blocks[j] * (2 * H), 2 * H)], start=True, stop=True,
                                            skip_group_check=True)
                        ins.then_inc(spread_done, 1)
                    pipeline(pe, [(0, spread_out)])

        def weighted_sum(h0):
            c = ExitStack()
            DEN = NB * HP * F
            with c:
                msg = [c.enter_context(nc.sbuf_tensor(f"{tag}_msg{h0}{k}", [P, CH, HP, F], FP32)) for k in range(2)]
                msg_ready = c.enter_context(semaphore(nc, f"{tag}_msg_ready{h0}"))
                chunk_free = c.enter_context(semaphore(nc, f"{tag}_msg_free{h0}"))
                steps = c.enter_context(semaphore(nc, f"{tag}_norm{h0}"))
                block = c.enter_context(nc.Block())

                @block.vector
                def _(v):
                    with v.Fori(0, ITERS) as it:
                        for k in range(2):
                            v.wait_ge(chunk_free, it * 2 + k + 1)
                            at = it * (2 * CH) + k * CH
                            onehot(v, hot[k][:, :, :], K.iota_row[:, :], K.dl[:, bass.ds(at, CH)]).then_inc(msg_ready, 1)
                            v.tensor_tensor(msg[k][:, :, :, :],
                                            kept[:, bass.ds(at, CH), 0:F].unsqueeze(2).broadcast_to([P, CH, HP, F]),
                                            weight[:, bass.ds(at, CH), h0:h0 + HP].unsqueeze(3).broadcast_to([P, CH, HP, F]),
                                            ALU.mult).then_inc(msg_ready, 1)
                    v.wait_ge(chunk_free, 2 + 2 * ITERS)
                    link = Link(v, steps)
                    if h0 == 0:
                        link(v.tensor_tensor(t0[:, :, :], K.ps[:, DEN:DEN + NB * H].rearrange("p (b h) -> p b h", h=H),
                                             selfw[:, :, :], ALU.add))
                        link(v.tensor_scalar(t0[:, :, :], t0[:, :, :], 1.0e-16, None, ALU.add))
                        link(v.reciprocal(t0[:, :, :], t0[:, :, :]))
                    zz = z[:, :, h0:h0 + HP, :]
                    full = [P, NB, HP, F]
                    link(v.tensor_tensor(zz, x.unsqueeze(2).broadcast_to(full),
                                         selfw[:, :, h0:h0 + HP].unsqueeze(3).broadcast_to(full), ALU.mult))
                    link(v.tensor_tensor(zz, zz, K.ps[:, 0:DEN].rearrange("p (b h c) -> p b h c", h=HP, c=F), ALU.add))
                    link(v.tensor_tensor(zz, zz, t0[:, :, h0:h0 + HP].unsqueeze(3).broadcast_to(full), ALU.mult))

                @block.tensor
                def _(pe):
                    clear_banks(pe, K, 0, 7).then_inc(chunk_free, 2)
                    wflat = weight[:, :, :].rearrange("p s h -> p (s h)")
                    with pe.Fori(0, ITERS) as it:
                        blocks = slot_blocks(nc, K, pe, it)
                        for k in range(2):
                            pe.wait_ge(msg_ready, it * 4 + 2 * k + 2)
                            for j in range(CH):
                                at = it * (2 * CH) + k * CH + j
                                b = blocks[k * CH + j]
                                if h0 == 0:
                                    pe.matmul(K.ps[:, bass.ds(b * H + DEN, H)], hot[k][:, j, :],
                                              wflat[:, bass.ds(it * (2 * CH * H) + (k * CH + j) * H, H)],
                                              start=False, stop=False, skip_group_check=True)
                                ins = pe.matmul(K.ps[:, bass.ds(b * (HP * F), HP * F)], hot[k][:, j, :],
                                                msg[k][:, j, :, :].rearrange("p h c -> p (h c)"),
                                                start=False, stop=False, skip_group_check=True)
                            ins.then_inc(chunk_free, 1)

        gather_and_max()
        node_maxima()
        edge_weights()
        for h0 in range(0, H, HP):
            weighted_sum(h0)


def bcast_chunk(rows, parts):
    return rows.rearrange("(o s) e -> o (s e)", o=1).broadcast_to([parts, CW])


def residual_norm(nc, K, add, tag):
    ctx = ExitStack()
    with ctx:
        y = ctx.enter_context(nc.sbuf_tensor(f"{tag}_y", [P, NB, F], FP32))
        sq = ctx.enter_context(nc.sbuf_tensor(f"{tag}_sq", [P, NB, F], FP32))
        mean = ctx.enter_context(nc.sbuf_tensor(f"{tag}_mean", [P, NB], FP32))
        var = ctx.enter_context(nc.sbuf_tensor(f"{tag}_var", [P, NB], FP32))
        steps = ctx.enter_context(semaphore(nc, f"{tag}_rn"))
        wanted = ctx.enter_context(semaphore(nc, f"{tag}_rnw"))
        ready = ctx.enter_context(semaphore(nc, f"{tag}_rnr"))
        block = ctx.enter_context(nc.Block())

        @block.vector
        def _(v):
            link = Link(v, steps)
            add(v, link, y)
            link(v.tensor_tensor(y[:, :, :], y[:, :, :], K.x[:, :, :], ALU.add))
            layernorm_steps(v, link, K, y[:, :, :], K.x[:, :, :], sq[:, :, :], mean[:, :], var[:, :], wanted, ready)

        @block.scalar
        def _(act):
            act.wait_ge(wanted, 1)
            act.activation(var[:, :], var[:, :], ACT.Sqrt).then_inc(ready, 1)


def gat(nc, K, A):
    H = HEADS
    ctx = ExitStack()
    with ctx:
        def sb(name, shape, dt=FP32):
            return ctx.enter_context(nc.sbuf_tensor(name, shape, dt))

        w1 = sb("w1", [F, H, F])
        w2a = sb("w2a", [F, H, F + 2])
        b1 = sb("b1c", [F, H])
        b2 = sb("b2r", [P, F])
        va = sb("va", [F, 2 * H])
        h2 = sb("h2", [P, NB, F + 2])
        prep = ExitStack()
        with prep:
            rows = prep.enter_context(nc.sbuf_tensor("att_rows", [F, 2, H, F], FP32))
            rows2 = prep.enter_context(nc.sbuf_tensor("att_rows2", [F, 2, F], FP32))
            prod = prep.enter_context(nc.sbuf_tensor("att_prod", [F, H, F], FP32))
            loaded = prep.enter_context(semaphore(nc, "gat_loaded"))
            steps = prep.enter_context(semaphore(nc, "gat_steps"))
            block = prep.enter_context(nc.Block())

            @block.sync
            def _(sp):
                sp.dma_start(w1[:, :, :], A["L1_gnn_W1"].rearrange("k (h o) -> k h o", h=H)).then_inc(loaded, 16)
                sp.dma_start(w2a[:, :, 0:F], A["L1_gnn_W2"].rearrange("(h k) o -> k h o", h=H)).then_inc(loaded, 16)
                with nc.allow_non_contiguous_dma(reason="a column of 256 biases"):
                    sp.dma_start(b1[:, :], A["L1_gnn_b1"].rearrange("(h k) -> k h", h=H)).then_inc(loaded, 16)
                sp.dma_start(b2[:, :], bcast_rows(A["L1_gnn_b2"], P)).then_inc(loaded, 16)
                for i, n in enumerate(("L1_gnn_a_src1", "L1_gnn_a_dst1")):
                    sp.dma_start(rows[:, i, :, :].rearrange("p h o -> p (h o)"),
                                 bcast_rows(A[n].rearrange("h o -> (h o)"), F)).then_inc(loaded, 16)
                for i, n in enumerate(("L1_gnn_a_src2", "L1_gnn_a_dst2")):
                    sp.dma_start(rows2[:, i, :], bcast_rows(A[n].rearrange("h o -> (h o)"), F)).then_inc(loaded, 16)

            @block.vector
            def _(v):
                link = Link(v, steps)
                v.wait_ge(loaded, 16 * 8)
                for i in range(2):
                    link(v.tensor_tensor(prod[:, :, :], w1[:, :, :], rows[:, i, :, :], ALU.mult))
                    link(v.tensor_reduce(va[:, i * H:(i + 1) * H], prod[:, :, :], AX.X, ALU.add))
                    link(v.tensor_tensor(prod[:, :, :], w2a[:, :, 0:F],
                                         rows2[:, i, :].unsqueeze(1).broadcast_to([F, H, F]), ALU.mult))
                    link(v.tensor_reduce(w2a[:, :, F + i], prod[:, :, :], AX.X, ALU.add))

        first = ExitStack()
        with first:
            al = first.enter_context(nc.sbuf_tensor("al1", [P, NB, 2 * H], FP32))
            z = first.enter_context(nc.sbuf_tensor("z1", [P, NB, H, F], FP32))
            with nc.sbuf_tensor("xT1", [F, NB * P], FP32) as xT:
                transpose_nodes(nc, K, K.x, xT, "g1t")
                project(nc, K, xT, va[:, :], 2 * H, al, "g1p")
            store_table(nc, K, K.tab_gat1, [(0, F, K.x[:, :, :]), (F, H, al[:, :, 0:H])], "g1s")
            attention(nc, K, H, K.tab_gat1, K.x[:, :, :], al[:, :, 0:H], al[:, :, H:2 * H], z, "g1")
            dense_heads(nc, K, z, w1, b1, w2a, h2)
        store_table(nc, K, K.tab_gat2, [(0, F + 1, h2[:, :, 0:F + 1])], "g2s")
        z2 = sb("z2", [P, NB, 1, F])
        attention(nc, K, 1, K.tab_gat2, h2[:, :, 0:F], h2[:, :, F:F + 1], h2[:, :, F + 1:F + 2], z2, "g2")

        def add(v, link, y):
            link(v.tensor_tensor(y[:, :, :], z2[:, :, 0, :], per_feature(b2[:, :]), ALU.add))
        residual_norm(nc, K, add, "g")


def dense_heads(nc, K, z, w1, b1, w2a, h2):
    H, C = HEADS, F + 2
    ctx = ExitStack()
    with ctx:
        def sem(name):
            return ctx.enter_context(semaphore(nc, name))

        zb = ctx.enter_context(nc.sbuf_tensor("zb", [P, H, F], FP32))
        zt = ctx.enter_context(nc.sbuf_tensor("zt", [F, H, P], FP32))
        ht = ctx.enter_context(nc.sbuf_tensor("ht", [F, H, P], FP32))
        staged, turned, zt_ready, hidden, ht_ready, made, copied = (sem(n) for n in (
            "d_staged", "d_turned", "d_zt_ready", "d_hidden", "d_ht_ready", "d_made", "d_copied"))
        block = ctx.enter_context(nc.Block())

        @block.scalar
        def _(act):
            act.sem_inc(ht_ready, H)
            with act.Fori(0, NB) as b:
                act.wait_ge(turned, b + 1)
                act.copy(zb[:, :, :], z[:, bass.ds(b, 1), :, :].rearrange("p b h c -> p (b h) c")).then_inc(staged, 1)
                act.wait_ge(hidden, b + 1)
                for h in range(H):
                    act.activation(ht[:, h, :], K.ps[0:F, BANK + h * P:BANK + (h + 1) * P], ACT.Relu, bias=b1[:, h:h + 1]
                                   ).then_inc(ht_ready, 1)

        @block.vector
        def _(v):
            v.sem_inc(copied, 1)
            with v.Fori(0, NB) as b:
                v.wait_ge(turned, b + 2)
                v.tensor_copy(zt[:, :, :], K.ps[0:F, 0:H * P].rearrange("p (h e) -> p h e", h=H)).then_inc(zt_ready, 1)
                v.wait_ge(made, b + 1)
                v.tensor_copy(h2[:, bass.ds(b, 1), :].rearrange("p b c -> p (b c)"), K.ps[:, 2 * BANK:2 * BANK + C]
                              ).then_inc(copied, 1)

        @block.tensor
        def _(pe):
            pe.sem_inc(turned, 1)
            with pe.Fori(0, NB) as b:
                pe.wait_ge(staged, b + 1)
                pe.nop(nofuse=True)
                for h in range(H):
                    ins = pe.transpose(K.ps[0:F, h * P:(h + 1) * P], zb[:, h, :], K.ident[:, :])
                ins.then_inc(turned, 1)
                pe.wait_ge(zt_ready, b + 1)
                pe.wait_ge(ht_ready, b * H + H)
                pe.nop(nofuse=True)
                for h in range(H):
                    ins = pe.matmul(K.ps[0:F, BANK + h * P:BANK + (h + 1) * P], w1[:, h, :], zt[:, h, :],
                                    start=True, stop=True, skip_group_check=True)
                ins.then_inc(hidden, 1)
                pe.wait_ge(ht_ready, b * H + 2 * H)
                pe.wait_ge(copied, b + 1)
                pe.nop(nofuse=True)
                for h in range(H):
                    ins = pe.matmul(K.ps[:, 2 * BANK:2 * BANK + C], ht[:, h, :], w2a[:, h, :], start=h == 0, stop=h == H - 1)
                ins.then_inc(made, 1)


def relational(nc, K, A):
    ctx = ExitStack()
    with ctx:
        def sb(name, shape, dt=FP32):
            return ctx.enter_context(nc.sbuf_tensor(name, shape, dt))

        rel = sb("rel", [F, REL, F])
        wself = sb("wself", [F, F])
        bias = sb("rel_bias", [P, F])
        own = sb("rel_own", [P, NB, F])
        xT = sb("xT2", [F, NB * P])
        prep = ExitStack()
        with prep:
            basis = prep.enter_context(nc.sbuf_tensor("basis", [NBASE, F, F], FP32))
            coeff = prep.enter_context(nc.sbuf_tensor("coeff", [REL, NBASE], FP32))
            coefT = prep.enter_context(nc.sbuf_tensor("coefT", [NBASE, REL], FP32))
            loaded = prep.enter_context(semaphore(nc, "rel_loaded"))
            turned = prep.enter_context(semaphore(nc, "rel_turned"))
            ready = prep.enter_context(semaphore(nc, "rel_coef"))
            made = prep.enter_context(semaphore(nc, "rel_made"))
            block = prep.enter_context(nc.Block())

            @block.sync
            def _(sp):
                sp.dma_start(basis[:, :, :], A["L2_gnn_basis"]).then_inc(loaded, 16)
                sp.dma_start(coeff[:, :], A["L2_gnn_coeff"]).then_inc(loaded, 16)
                sp.dma_start(wself[:, :], A["L2_gnn_self_weight"]).then_inc(loaded, 16)
                sp.dma_start(bias[:, :], bcast_rows(A["L2_gnn_bias"], P)).then_inc(loaded, 16)

            @block.tensor
            def _(pe):
                pe.wait_ge(loaded, 64)
                pe.transpose(K.ps[0:NBASE, 7 * BANK:7 * BANK + REL], coeff[:, :], K.ident[0:REL, 0:REL]).then_inc(turned, 1)
                pe.wait_ge(ready, 1)
                for o in range(F):
                    ins = pe.matmul(K.ps[0:F, o * REL:(o + 1) * REL], basis[:, :, o], coefT[:, :], start=True, stop=True,
                                    skip_group_check=True)
                ins.then_inc(made, 1)

            @block.vector
            def _(v):
                v.wait_ge(turned, 1)
                v.tensor_copy(coefT[:, :], K.ps[0:NBASE, 7 * BANK:7 * BANK + REL]).then_inc(ready, 1)
                v.wait_ge(made, 1)
                v.tensor_copy(rel[:, :, :], K.ps[0:F, 0:F * REL].rearrange("p (o r) -> p r o", r=REL)).then_inc(ready, 1)
                v.wait_ge(ready, 2)
        transpose_nodes(nc, K, K.x, xT, "r1t")
        project(nc, K, xT, wself[:, :], F, own, "r1p")
        rows_of(nc, K, K.sq_var[:, :], "v2")
        relation_table(nc, K, rel, xT)
        with ExitStack() as c:
            gather_sum(nc, K, K.tab_rel.rearrange("n (r o) -> (n r) o", r=REL), K.rel_idx, "relg", FinishEncoding(nc, K, c))

        def add(v, link, y):
            link(v.tensor_tensor(y[:, :, :], sums(K), per_node(K.rdeg[:, :]), ALU.mult))
            link(v.tensor_tensor(y[:, :, :], y[:, :, :], own[:, :, :], ALU.add))
            link(v.tensor_tensor(y[:, :, :], y[:, :, :], per_feature(bias[:, :]), ALU.add))
        residual_norm(nc, K, add, "r")


def relation_table(nc, K, rel, xT):
    ctx = ExitStack()
    with ctx:
        W = REL * F
        Q = W // BANK
        y = [ctx.enter_context(nc.sbuf_tensor(f"ytab{k}", [P, W], FP32)) for k in range(2)]
        xb = [ctx.enter_context(nc.sbuf_tensor(f"xtb{k}", [F, P], FP32)) for k in range(2)]
        staged, made, copied_v, copied_a = (ctx.enter_context(semaphore(nc, n)) for n in (
            "y_staged", "y_made", "y_copied_v", "y_copied_a"))
        stored = [ctx.enter_context(semaphore(nc, f"y_stored{k}")) for k in range(2)]
        block = ctx.enter_context(nc.Block())
        flat = rel[:, :, :].rearrange("p r o -> p (r o)")
        rows = node_rows(K.tab_rel)

        @block.tensor
        def _(pe):
            def one(b, k):
                pe.wait_ge(staged, b + 1)
                pe.wait_ge(copied_v, b * (Q // 2) + Q // 2)
                pe.wait_ge(copied_a, b * (Q // 2) + Q // 2)
                pe.nop(nofuse=True)
                for q in range(Q):
                    pe.matmul(K.ps[:, (4 * k + q) * BANK:(4 * k + q + 1) * BANK], xb[k][:, :],
                              flat[:, q * BANK:(q + 1) * BANK], start=True, stop=True).then_inc(made, 1)
            with pe.Fori(0, NB // 2) as it:
                for k in range(2):
                    one(it * 2 + k, k)
            one(NB - 1, 0)

        @block.scalar
        def _(act):
            def half(b, k, n):
                act.wait_ge(stored[k], n)
                for q in range(Q // 2, Q):
                    act.wait_ge(made, b * Q + q + 1)
                    act.copy(y[k][:, q * BANK:(q + 1) * BANK], K.ps[:, (4 * k + q) * BANK:(4 * k + q + 1) * BANK]
                             ).then_inc(copied_a, 1)
            act.sem_inc(copied_a, Q)
            with act.Fori(0, NB // 2) as it:
                for k in range(2):
                    half(it * 2 + k, k, it * 16 + 16)
            half(NB - 1, 0, (NB // 2) * 16 + 16)

        @block.vector
        def _(v):
            def half(b, k, n):
                v.wait_ge(copied_a, b * (Q // 2) + Q // 2)
                v.tensor_copy(xb[k][:, :], xT[:, bass.ds(b * P, P)] if not isinstance(b, int)
                              else xT[:, b * P:(b + 1) * P]).then_inc(staged, 1)
                v.wait_ge(stored[k], n)
                for q in range(Q // 2):
                    v.wait_ge(made, b * Q + q + 1)
                    v.tensor_copy(y[k][:, q * BANK:(q + 1) * BANK], K.ps[:, (4 * k + q) * BANK:(4 * k + q + 1) * BANK]
                                  ).then_inc(copied_v, 1)
            v.sem_inc(copied_v, Q)
            with v.Fori(0, NB // 2) as it:
                for k in range(2):
                    half(it * 2 + k, k, it * 16 + 16)
            half(NB - 1, 0, (NB // 2) * 16 + 16)

        @block.sync
        def _(sp):
            def one(b, k):
                sp.wait_ge(copied_v, b * (Q // 2) + Q + Q // 2)
                sp.wait_ge(copied_a, b * (Q // 2) + Q + Q // 2)
                out = rows[:, bass.ds(b, 1), :] if not isinstance(b, int) else rows[:, b:b + 1, :]
                sp.dma_start(out, y[k][:, :].unsqueeze(1)).then_inc(stored[k], 16)
            sp.sem_inc(stored[0], 16)
            sp.sem_inc(stored[1], 16)
            with sp.Fori(0, NB // 2) as it:
                for k in range(2):
                    one(it * 2 + k, k)
            one(NB - 1, 0)
            sp.wait_ge(stored[0], 16 + 16 * (NB // 2 + 1))
            sp.wait_ge(stored[1], 16 + 16 * (NB // 2))


def rows_of(nc, K, var, tag):
    ctx = ExitStack()
    with ctx:
        rr = ctx.enter_context(nc.sbuf_tensor(f"{tag}_rr", [P, 4, P], FP32))
        steps, wanted, ready, turned, stored = (ctx.enter_context(semaphore(nc, f"{tag}_{n}")) for n in (
            "steps", "wanted", "ready", "turned", "stored"))
        block = ctx.enter_context(nc.Block())

        @block.vector
        def _(v):
            link = Link(v, steps)
            link(v.tensor_scalar(var, var, 1.0 / F, EPS, ALU.mult, ALU.add))
            v.sem_inc(wanted, 1)
            v.wait_ge(ready, 1)
            link(v.reciprocal(var, var))
            v.wait_ge(turned, 1)
            link(v.tensor_copy(rr[0:SG, :, :], K.ps[0:SG, 0:4 * P].rearrange("p (g e) -> p g e", g=4)))

        @block.scalar
        def _(act):
            act.wait_ge(wanted, 1)
            act.activation(var, var, ACT.Sqrt).then_inc(ready, 1)

        @block.tensor
        def _(pe):
            pe.wait_ge(steps, 2)
            for g in range(4):
                ins = pe.transpose(K.ps[0:SG, g * P:(g + 1) * P], var[:, g * SG:(g + 1) * SG], K.ident[:, :])
            ins.then_inc(turned, 1)

        @block.sync
        def _(sp):
            sp.wait_ge(steps, 3)
            sp.dma_start(K.rstd_rows.rearrange("(g s) e -> s g e", g=4), rr[0:SG, :, :]).then_inc(stored, 16)
            sp.wait_ge(stored, 16)


class EdgeWeights:

    def __init__(self, nc, K, A, ctx):
        def sb(name, shape, dt=FP32):
            return ctx.enter_context(nc.sbuf_tensor(name, shape, dt))

        wd1 = self.wd1 = sb("wd1", [4, F])
        wd2 = self.wd2 = sb("wd2", [F, F])
        bd2r = sb("bd2r", [1, F])
        bd2 = self.bd2 = sb("bd2", [F, 1])
        mean = sb("wmean", [F, 3])
        gb = self.gb = K.gb
        self.var = K.sq_var
        at = self.at = [sb(f"at{k}", [4, CW]) for k in range(2)]
        with semaphore(nc, "w_loaded") as loaded, semaphore(nc, "w_steps") as steps, \
                semaphore(nc, "w_made") as made, nc.Block() as block:
            @block.sync
            def _(sp):
                sp.dma_start(wd1[0:3, :], A["L3_gnn_Wd1"]).then_inc(loaded, 16)
                sp.dma_start(wd1[3:4, :], bcast_rows(A["L3_gnn_bd1"], 1)).then_inc(loaded, 16)
                sp.dma_start(wd2[:, :], A["L3_gnn_Wd2"]).then_inc(loaded, 16)
                sp.dma_start(bd2r[:, :], bcast_rows(A["L3_gnn_bd2"], 1)).then_inc(loaded, 16)
                with nc.allow_non_contiguous_dma(reason="columns of 64"):
                    for i, n in enumerate(("L3_gnn_g1", "L3_gnn_b1", "L3_gnn_g2", "L3_gnn_b2")):
                        sp.dma_start(gb[:, i:i + 1], A[n].rearrange("(c o) -> c o", o=1)).then_inc(loaded, 16)

            @block.vector
            def _(v):
                link = Link(v, steps)
                for k in range(2):
                    link(v.memset(at[k][:, :], 1.0))
                v.wait_ge(loaded, 16 * 8)
                for i, (w, n) in enumerate(((wd1, 4), (wd2, F), (bd2r, 1))):
                    link(v.tensor_reduce(mean[0:n, i:i + 1], w[:, :], AX.X, ALU.add))
                    link(v.tensor_scalar(mean[0:n, i:i + 1], mean[0:n, i:i + 1], -1.0 / F, None, ALU.mult))
                    link(v.tensor_scalar(w[:, :], w[:, :], mean[0:n, i:i + 1], None, ALU.add))
                v.wait_ge(made, 1)
                link(v.tensor_copy(bd2[:, :], K.ps[0:F, 0:1]))

            @block.tensor
            def _(pe):
                pe.wait_ge(steps, 11)
                pe.matmul(K.ps[0:F, 0:1], bd2r[:, :], K.ones[0:1, 0:1], start=True, stop=True).then_inc(made, 1)


def attr_chunk(K, c):
    return K.attr_rows[:, bass.ds(c * CH, CH), :].rearrange("a s e -> a (s e)")


class FirstVariance:

    def __init__(self, nc, K, ctx, enc):
        def sem(name):
            return ctx.enter_context(semaphore(nc, name))

        self.K, self.enc = K, enc
        self.sq = [ctx.enter_context(nc.sbuf_tensor(f"esq{k}", [P, CH, F], FP32)) for k in range(2)]
        self.at_in = [sem(f"e_at_in{k}") for k in range(2)]
        self.made, self.squared, self.summed = sem("e_made"), sem("e_squared"), sem("e_summed")

    def sync(self, sp):
        def load(c, k, turn):
            sp.wait_ge(self.made, c + 1)
            sp.dma_start(self.enc.at[k][0:3, :], attr_chunk(self.K, c)).then_inc(self.at_in[k], 16)
        return [(0, load)]

    def finish(self, sp):
        pass

    def tensor(self, pe):
        pe.sem_inc(self.made, 2)

        def product(c, k, turn):
            pe.wait_ge(self.at_in[k], turn * 16 + 16)
            pe.wait_ge(self.squared, c + 1)
            pe.nop(nofuse=True)
            for j in range(CH):
                o = (4 + k) * BANK + j * F
                ins = pe.matmul(self.K.ps[:, o:o + F], self.enc.at[k][:, j * P:(j + 1) * P], self.enc.wd1[:, :],
                                start=True, stop=True, skip_group_check=True)
            ins.then_inc(self.made, 1)
        return [(0, product)]

    def scalar(self, act):
        act.sem_inc(self.squared, 2)

        def square(c, k, turn):
            act.wait_ge(self.made, c + 3)
            act.wait_ge(self.summed, c + 1)
            act.activation(self.sq[k][:, :, :], self.K.ps[:, (4 + k) * BANK:(4 + k) * BANK + CH * F].rearrange(
                "p (s c) -> p s c", c=F), ACT.Square).then_inc(self.squared, 1)
        return [(0, square)]

    def vector(self, v):
        v.sem_inc(self.summed, 2)

        def total(c, k, turn):
            v.wait_ge(self.squared, c + 3)
            v.tensor_reduce(self.enc.var[:, bass.ds(c * CH, CH)], self.sq[k][:, :, :], AX.X, ALU.add).then_inc(self.summed, 1)
        return [(1, total)]


class SecondProduct:

    def __init__(self, nc, K, ctx, enc):
        def pair(name, shape):
            return [ctx.enter_context(nc.sbuf_tensor(f"{name}{k}", shape, FP32)) for k in range(2)]

        def sem(name):
            return ctx.enter_context(semaphore(nc, name))

        self.K, self.enc = K, enc
        self.ats, self.rs, self.d1, self.hh, self.sq = (pair(n, s) for n, s in (
            ("ats", [4, CW]), ("ers", [4, CW]), ("ed1", [F, CW]), ("ehh", [F, CW]), ("ehs", [F, CW])))
        self.at_in = [sem(f"m_in{k}") for k in range(2)]
        self.stored = [sem(f"m_stored{k}") for k in range(2)]
        self.scaled, self.first, self.gelued, self.second, self.moved, self.squared, self.summed, self.taken = (
            sem(f"m_{n}") for n in ("scaled", "first", "gelued", "second", "moved", "squared", "summed", "taken"))

    def sync(self, sp):
        K = self.K
        for k in range(2):
            sp.sem_inc(self.stored[k], 16)

        def load(c, k, turn):
            sp.wait_ge(self.scaled, c + 1)
            sp.dma_start(self.enc.at[k][0:3, :], attr_chunk(K, c)).then_inc(self.at_in[k], 16)
            sp.dma_start(self.rs[k][:, :], bcast_chunk(K.rstd_rows[bass.ds(c * CH, CH), :], 4)).then_inc(self.at_in[k], 16)

        def store(c, k, turn):
            sp.wait_ge(self.moved, c + 1)
            sp.dma_start(K.enc[:, bass.ds(c * CW, CW)], self.hh[k][:, :]).then_inc(self.stored[k], 16)
        return [(0, load), (2, store)]

    def finish(self, sp):
        for k in range(2):
            sp.wait_ge(self.stored[k], 16 + 16 * ITERS)

    def vector(self, v):
        for s in (self.scaled, self.squared):
            v.sem_inc(s, 2)
        v.sem_inc(self.taken, 1)

        def scale(c, k, turn):
            v.wait_ge(self.at_in[k], turn * 32 + 32)
            v.wait_ge(self.first, c + 1)
            v.tensor_tensor(self.ats[k][:, :], self.enc.at[k][:, :], self.rs[k][:, :], ALU.mult).then_inc(self.scaled, 1)

        def square(c, k, turn):
            v.wait_ge(self.moved, c + 1)
            v.wait_ge(self.summed, c + 1)
            v.tensor_tensor(self.sq[k][:, :], self.hh[k][:, :], self.hh[k][:, :], ALU.mult).then_inc(self.squared, 1)

        def take(c, k, turn):
            v.wait_ge(self.summed, c + 3)
            v.tensor_copy(self.enc.var[:, bass.ds(c * CH, CH)], self.K.ps[:, 7 * BANK:7 * BANK + CH]).then_inc(self.taken, 1)
        return [(0, scale), (2, square), (4, take)]

    def scalar(self, act):
        K, gb = self.K, self.enc.gb
        act.sem_inc(self.gelued, 2)

        def gelu(c, k, turn):
            act.wait_ge(self.first, c + 3)
            act.wait_ge(self.second, c + 1)
            act.activation(self.d1[k][:, :], K.ps[0:F, (4 + k) * BANK:(5 + k) * BANK], ACT.Gelu, bias=gb[:, 1:2],
                           scale=gb[:, 0:1]).then_inc(self.gelued, 1)

        def move(c, k, turn):
            act.wait_ge(self.second, c + 3)
            act.wait_ge(self.stored[k], turn * 16 + 16)
            act.wait_ge(self.squared, c + 1)
            act.activation(self.hh[k][:, :], K.ps[0:F, 6 * BANK:7 * BANK], ACT.Identity, bias=self.enc.bd2[:, 0:1]
                           ).then_inc(self.moved, 1)
        return [(0, gelu), (1, move)]

    def tensor(self, pe):
        K, enc = self.K, self.enc
        for s in (self.first, self.second, self.summed):
            pe.sem_inc(s, 2)

        def first(c, k, turn):
            pe.wait_ge(self.scaled, c + 3)
            pe.wait_ge(self.gelued, c + 1)
            pe.nop(nofuse=True)
            pe.matmul(K.ps[0:F, (4 + k) * BANK:(5 + k) * BANK], enc.wd1[:, :], self.ats[k][:, :], start=True, stop=True
                      ).then_inc(self.first, 1)

        def second(c, k, turn):
            pe.wait_ge(self.gelued, c + 3)
            if not (isinstance(c, int) and c == 0):
                pe.wait_ge(self.moved, c)
            pe.nop(nofuse=True)
            pe.matmul(K.ps[0:F, 6 * BANK:7 * BANK], enc.wd2[:, :], self.d1[k][:, :], start=True, stop=True
                      ).then_inc(self.second, 1)

        def total(c, k, turn):
            pe.wait_ge(self.squared, c + 3)
            pe.wait_ge(self.taken, c + 1)
            pe.nop(nofuse=True)
            for j in range(CH):
                ins = pe.matmul(K.ps[:, 7 * BANK + j:7 * BANK + j + 1], self.sq[k][:, j * P:(j + 1) * P], K.ones[0:F, 0:1],
                                start=True, stop=True, skip_group_check=True)
            ins.then_inc(self.summed, 1)
        return [(0, first), (1, second), (3, total)]


class FinishEncoding:

    def __init__(self, nc, K, ctx):
        def pair(name):
            return [ctx.enter_context(nc.sbuf_tensor(f"{name}{k}", [F, CW], FP32)) for k in range(2)]

        def sem(name):
            return ctx.enter_context(semaphore(nc, name))

        self.K = K
        self.hin, self.rs, self.prod, self.dd = (pair(n) for n in ("fh", "frs", "fp", "fd"))
        self.h_in = [sem(f"f_in{k}") for k in range(2)]
        self.stored = [sem(f"f_stored{k}") for k in range(2)]
        self.scaled, self.gelued = sem("f_scaled"), sem("f_gelued")

    def sync(self, sp):
        K = self.K
        for k in range(2):
            sp.sem_inc(self.stored[k], 16)

        def load(c, k, turn):
            sp.wait_ge(self.scaled, c + 1)
            sp.dma_start(self.hin[k][:, :], K.enc[:, bass.ds(c * CW, CW)]).then_inc(self.h_in[k], 16)
            sp.dma_start(self.rs[k][:, :], bcast_chunk(K.rstd_rows[bass.ds(c * CH, CH), :], F)).then_inc(self.h_in[k], 16)

        def store(c, k, turn):
            sp.wait_ge(self.gelued, c + 3)
            sp.dma_start(K.enc[:, bass.ds(c * CW, CW)], self.dd[k][:, :]).then_inc(self.stored[k], 16)
        return [(0, load), (2, store)]

    def finish(self, sp):
        for k in range(2):
            sp.wait_ge(self.stored[k], 16 + 16 * ITERS)

    def vector(self, v):
        v.sem_inc(self.scaled, 2)

        def scale(c, k, turn):
            v.wait_ge(self.h_in[k], turn * 32 + 32)
            v.wait_ge(self.gelued, c + 1)
            v.tensor_tensor(self.prod[k][:, :], self.hin[k][:, :], self.rs[k][:, :], ALU.mult).then_inc(self.scaled, 1)
        return [(0, scale)]

    def scalar(self, act):
        act.sem_inc(self.gelued, 2)

        def gelu(c, k, turn):
            act.wait_ge(self.scaled, c + 3)
            act.wait_ge(self.stored[k], turn * 16 + 16)
            act.activation(self.dd[k][:, :], self.prod[k][:, :], ACT.Gelu, bias=self.K.gb[:, 3:4], scale=self.K.gb[:, 2:3]
                           ).then_inc(self.gelued, 1)
        return [(0, gelu)]

    def tensor(self, pe):
        return []


def vector_attention(nc, K, A):
    ctx = ExitStack()
    with ctx:
        def sb(name, shape, dt=FP32):
            return ctx.enter_context(nc.sbuf_tensor(name, shape, dt))

        proj = sb("proj", [P, NB, 3, F])
        with nc.sbuf_tensor("wv", [F, 3, F], FP32) as wv, nc.sbuf_tensor("xT3", [F, NB * P], FP32) as xT:
            with semaphore(nc, "wv_in") as wv_in, semaphore(nc, "wv_neg") as wv_neg, nc.Block() as block:
                @block.sync
                def _(sp):
                    for i, n in enumerate(("L3_gnn_W2", "L3_gnn_W3", "L3_gnn_W1")):
                        sp.dma_start(wv[:, i, :], A[n]).then_inc(wv_in, 16)

                @block.vector
                def _(v):
                    v.wait_ge(wv_in, 48)
                    v.tensor_scalar(wv[:, 0, :], wv[:, 0, :], -1.0, None, ALU.mult).then_inc(wv_neg, 1)
                    v.wait_ge(wv_neg, 1)
            transpose_nodes(nc, K, K.x, xT, "v1t")
            project(nc, K, xT, wv[:, :, :].rearrange("p i o -> p (i o)"), 3 * F,
                    proj[:, :, :, :].rearrange("p b i o -> p b (i o)"), "v1p")
        store_table(nc, K, K.tab_vec, [(0, 2 * F, proj[:, :, 0:2, :].rearrange("p b i o -> p b (i o)"))], "v1s")
        scan_edges(nc, K, proj)

        def add(v, link, y):
            link(v.tensor_copy(y[:, :, :], sums(K)))
        residual_norm(nc, K, add, "vec")


def scan_edges(nc, K, proj):
    ctx = ExitStack()
    with ctx:
        def pair(name, shape, dt=FP32):
            return [ctx.enter_context(nc.sbuf_tensor(f"s_{name}{k}", shape, dt)) for k in range(2)]

        def sem(name):
            return ctx.enter_context(semaphore(nc, f"s_{name}"))

        ring, idx = pair("ring", [P, CH, 2 * F]), pair("idx", [P, CH], I32)
        dlb, pen, enc = pair("dlb", [P, CW]), pair("pen", [F, CW]), pair("enc", [F, CW])
        cold, hot = pair("cold", [P, CW]), pair("hot", [P, CH, P])
        w1 = pair("w1", [P, CH, F])
        mrun = pair("mrun", [F, CW + 1])
        arg = pair("arg", [F, 2, CW])
        ex = pair("ex", [P, 2, CW])
        sums2 = pair("sums", [P, CW])
        rt = pair("rt", [P, CH, 2, F])
        quo = pair("quo", [P, CH, F])
        inv = pair("inv", [P, CH, F])
        twice = ctx.enter_context(nc.sbuf_tensor("twice", [F, 2, F], FP32))
        rows_in = [sem(f"rows_in{k}") for k in range(2)]
        side_in = [sem(f"side_in{k}") for k in range(2)]
        (idx_ready, started, cold_ready, hot_ready, w1_ready, logits, max_steps, args, exps, sum_steps, summed, back,
         rt_ready, quo_steps, done) = (
            sem(n) for n in ("idx_ready", "started", "cold_ready", "hot_ready", "w1_ready", "logits", "max_steps", "args",
                             "exps", "sum_steps", "summed", "back", "rt_ready", "quo_steps", "done"))
        block = ctx.enter_context(nc.Block())

        def bank(k):
            return K.ps[:, (4 + k) * BANK:(5 + k) * BANK]

        @block.gpsimd
        def _(pool):
            def rows(c, k, turn):
                pool.wait_ge(idx_ready, c + 1)
                pool.nop(nofuse=True)
                gather(pool, ring[k], idx[k], K.tab_vec, rows_in[k])
            pipeline(pool, [(0, rows)])

        @block.sync
        def _(sp):
            def load(c, k, turn):
                sp.wait_ge(args, c + 1)
                sp.dma_start(dlb[k][:, :], bcast_chunk(K.dl_rows[bass.ds(c * CH, CH), :], P)).then_inc(side_in[k], 16)
                sp.dma_start(pen[k][:, :], bcast_chunk(K.pen_rows[bass.ds(c * CH, CH), :], F)).then_inc(side_in[k], 16)
                sp.dma_start(enc[k][:, :], K.enc[:, bass.ds(c * CW, CW)]).then_inc(side_in[k], 16)
            pipeline(sp, [(0, load)])

        @block.vector
        def _(v):
            for k in range(2):
                v.tensor_copy(twice[:, k, :], K.ident[0:F, 0:F]).then_inc(started, 1)
            v.memset(mrun[1][:, :], -BIG).then_inc(started, 1)
            v.memset(sums2[1][:, :], 0.0).then_inc(started, 1)
            v.wait_ge(started, 4)
            v.sem_inc(args, 2)
            v.sem_inc(summed, 2)
            link_max, link_sum, link_quo = Link(v, max_steps, 4), Link(v, sum_steps, 2), Link(v, quo_steps, 2)

            def prepare(c, k, turn):
                v.wait_ge(logits, c + 1)
                v.tensor_copy(idx[k][:, :], K.src_idx[:, bass.ds(c * CH, CH)]).then_inc(idx_ready, 1)
                v.wait_ge(side_in[k], turn * 48 + 48)
                v.tensor_scalar(cold[k][:, :], dlb[k][:, :], K.iota_part[:, 0:1], None, ALU.is_equal).then_inc(cold_ready, 1)

            def maxima(c, k, turn):
                link_max.turn(c)
                v.wait_ge(logits, c + 3)
                link_max(v.tensor_copy(mrun[k][:, 0:1], mrun[1 - k][:, CW:CW + 1]))
                link_max(v.tensor_tensor_scan(mrun[k][:, 1:CW + 1], pen[k][:, :], bank(k)[0:F, :], mrun[k][:, 0:1],
                                              ALU.add, ALU.max))
                if not (isinstance(c, int) and c < 2):
                    v.wait_ge(exps, c - 1)
                link_max(v.tensor_tensor(arg[k][:, 0, :], mrun[k][:, 0:CW], pen[k][:, :], ALU.add))
                link_max(v.tensor_tensor(arg[k][:, 0, :], arg[k][:, 0, :], mrun[k][:, 1:CW + 1], ALU.subtract))
                v.tensor_tensor(arg[k][:, 1, :], bank(k)[0:F, :], mrun[k][:, 1:CW + 1], ALU.subtract).then_inc(args, 1)

            def add_up(c, k, turn):
                link_sum.turn(c)
                v.wait_ge(exps, c + 1)
                link_sum(v.tensor_tensor(ex[k][F:P, 1, :], ex[k][F:P, 1, :], bank(k)[F:P, :], ALU.mult))
                v.wait_ge(back, c + 1)
                link_sum(v.tensor_tensor_scan(sums2[k][:, :], ex[k][:, 0, :], ex[k][:, 1, :], sums2[1 - k][:, CW - 1:CW],
                                              ALU.mult, ALU.add))
                v.sem_inc(summed, 1)

            def quotients(c, k, turn):
                v.wait_ge(done, c + 1)
                onehot(v, hot[k][:, :, :], K.iota_row[:, :], K.dl_end[:, bass.ds(c * CH, CH)]).then_inc(hot_ready, 1)
                link_quo.turn(c)
                v.wait_ge(rt_ready, c + 1)
                link_quo(v.reciprocal(inv[k][:, :, :], rt[k][:, :, 0, :]))
                link_quo(v.tensor_tensor(quo[k][:, :, :], inv[k][:, :, :], rt[k][:, :, 1, :], ALU.mult))
            pipeline(v, [(0, prepare), (2, add_up), (1, maxima), (4, quotients)])

        @block.scalar
        def _(act):
            def targets(c, k, turn):
                blocks = chunk_blocks(nc, K, act, c)
                act.wait_ge(logits, c + 1)
                for j in range(CH):
                    act.copy(w1[k][:, j, :], proj[:, bass.ds(blocks[j], 1), 2, :].rearrange("p b o -> p (b o)")
                             ).then_inc(w1_ready, 1)

            def exponentials(c, k, turn):
                act.wait_ge(args, c + 3)
                act.wait_ge(summed, c + 1)
                for half in range(2):
                    ins = act.activation(ex[k][half * F:(half + 1) * F, :, :], arg[k][:, :, :], ACT.Exp)
                ins.then_inc(exps, 1)

            def by_edge(c, k, turn):
                act.wait_ge(back, c + 3)
                if not (isinstance(c, int) and c < 2):
                    act.wait_ge(quo_steps, c * 2 - 2)
                act.copy(rt[k][:, :, :, :].rearrange("p s t c -> p (s t c)"), K.ps[:, (6 + k) * BANK:(7 + k) * BANK]
                         ).then_inc(rt_ready, 1)
            pipeline(act, [(0, targets), (1, exponentials), (3, by_edge)])

        @block.tensor
        def _(pe):
            clear_banks(pe, K, 0, 4).then_inc(done, 2)
            pe.wait_ge(started, 4)
            pe.sem_inc(logits, 2)
            pe.sem_inc(back, 2)

            def products(c, k, turn):
                pe.wait_ge(side_in[k], turn * 48 + 48)
                pe.wait_ge(summed, c + 1)
                pe.wait_ge(cold_ready, c + 1)
                pe.wait_ge(w1_ready, c * CH + CH)
                pe.wait_ge(rows_in[k], turn * (16 * CH) + 16 * CH)
                pe.nop(nofuse=True)
                pe.matmul(bank(k), twice[:, :, :].rearrange("p a c -> p (a c)"), enc[k][:, :], start=True, stop=False,
                          skip_group_check=True)
                for j in range(CH):
                    cols = bank(k)[:, j * P:(j + 1) * P]
                    pe.matmul(cols, ring[k][:, j, :], K.ident[:, :], start=False, stop=False, skip_group_check=True)
                    ins = pe.matmul(cols[0:F, :], w1[k][:, j, :], cold[k][:, j * P:(j + 1) * P], start=False, stop=True,
                                    skip_group_check=True)
                ins.then_inc(logits, 1)

            def turn_back(c, k, turn):
                pe.wait_ge(summed, c + 3)
                if not (isinstance(c, int) and c < 2):
                    pe.wait_ge(rt_ready, c - 1)
                pe.nop(nofuse=True)
                for j in range(CH):
                    o = (6 + k) * BANK + j * P
                    ins = pe.transpose(K.ps[:, o:o + P], sums2[k][:, j * P:(j + 1) * P], K.ident[:, :])
                ins.then_inc(back, 1)

            def pick_ends(c, k, turn):
                blocks = chunk_blocks(nc, K, pe, c)
                pe.wait_ge(quo_steps, c * 2 + 2)
                pe.wait_ge(hot_ready, c + 1)
                pe.nop(nofuse=True)
                for j in range(CH):
                    ins = pe.matmul(K.ps[:, bass.ds(blocks[j] * F, F)], hot[k][:, j, :], quo[k][:, j, :], start=False,
                                    stop=False, skip_group_check=True)
                ins.then_inc(done, 1)
            pipeline(pe, [(0, products), (3, turn_back), (5, pick_ends)])



def build(nc, A, out):
    K = Space()
    ctx = ExitStack()
    with ctx:
        def sb(name, shape, dt=FP32):
            return ctx.enter_context(nc.sbuf_tensor(name, shape, dt))

        def dram(name, shape, dt=FP32):
            return nc.dram_tensor(name, shape, dt, kind="Internal").ap()

        K.ps = ctx.enter_context(nc.psum_tensor("ps", [P, 8 * BANK], FP32))
        K.ident = sb("ident", [P, P])
        K.iota_row = sb("iota_row", [P, P])
        K.iota_part = sb("iota_part", [P, 1])
        K.ones = sb("ones", [P, P])
        K.zeros = sb("zeros", [P, BANK])
        K.dl = sb("dl", [P, SLOTS])
        K.dl_end = sb("dl_end", [P, SLOTS])
        K.src_idx = sb("src_idx", [P, SLOTS], I32)
        K.rel_idx = sb("rel_idx", [P, SLOTS], I32)
        K.blk_i = sb("blk_i", [P, SLOTS], I32)
        K.x = sb("x_nodes", [P, NB, F])
        K.deg, K.deg1, K.has, K.rdeg, K.dis = (sb(n, [P, NB]) for n in ("deg", "deg1", "has", "rdeg", "dis"))
        K.dl_rows = dram("dl_rows", [SLOTS, P])
        K.pen_rows = dram("pen_rows", [SLOTS, P])
        K.attr_rows = dram("attr_rows", [3, SLOTS, P])
        K.tab64 = dram("tab64", [NB * P, F])
        K.tab_gat1 = dram("tab_gat1", [NB * P, F + HEADS])
        K.tab_gat2 = dram("tab_gat2", [NB * P, F + 1])
        K.tab_rel = dram("tab_rel", [NB * P, REL * F])
        K.tab_vec = dram("tab_vec", [NB * P, 2 * F])
        K.rstd_rows = dram("rstd_rows", [SLOTS, P])
        K.enc = dram("enc", [F, SLOTS * P])
        with nc.cleanup_on_exit():
            build_slots(nc, K, A["dst"], A["src"], A["edge_type_32"], A["edge_attr_3"])
            count_degrees(nc, K)
        K.sq_var = sb("sq_var", [P, SLOTS])
        K.gb = sb("gb", [F, 4])
        with nc.cleanup_on_exit(), ExitStack() as c:
            enc = EdgeWeights(nc, K, A, c)
            appnp(nc, K, A["x"], A["L0_gnn_alpha"], enc)
        with nc.cleanup_on_exit():
            gat(nc, K, A)
        with nc.cleanup_on_exit():
            relational(nc, K, A)
        with nc.cleanup_on_exit():
            vector_attention(nc, K, A)
        store_out(nc, K, out)


_INS = ['x', 'src', 'dst', 'edge_attr_3', 'edge_type_32', 'L0_gnn_alpha', 'L1_gnn_W1', 'L1_gnn_a_src1', 'L1_gnn_a_dst1',
        'L1_gnn_b1', 'L1_gnn_W2', 'L1_gnn_a_src2', 'L1_gnn_a_dst2', 'L1_gnn_b2', 'L2_gnn_basis', 'L2_gnn_coeff',
        'L2_gnn_self_weight', 'L2_gnn_bias', 'L3_gnn_Wd1', 'L3_gnn_bd1', 'L3_gnn_g1', 'L3_gnn_b1', 'L3_gnn_Wd2',
        'L3_gnn_bd2', 'L3_gnn_g2', 'L3_gnn_b2', 'L3_gnn_W1', 'L3_gnn_W2', 'L3_gnn_W3']


def kernel(**inputs):
    import numpy as _np
    import concourse.bacc as _bacc
    from concourse import mybir as _mybir
    from concourse.bass_utils import run_bass_kernel_spmd as _run

    nc = _bacc.Bacc("TRN2", target_bir_lowering=False, num_devices=1)
    arrays, args = {}, {}
    for name in _INS:
        a = _np.ascontiguousarray(inputs[name])
        arrays[f"in_{name}_dram"] = a
        args[name] = nc.dram_tensor(f"in_{name}_dram", a.shape, _mybir.dt.from_np(a.dtype), kind="ExternalInput").ap()
    out = nc.dram_tensor("out_0_dram", (N, F), FP32, kind="ExternalOutput").ap()
    build(nc, args, out)
    r = _run(nc, [arrays], core_ids=[0])
    return r.results[0]["out_0_dram"]
```

```python
import concourse.bass as bass
from concourse import mybir
from contextlib import ExitStack, contextmanager

FP32 = mybir.dt.float32
BF16 = mybir.dt.bfloat16
I32 = mybir.dt.int32
ALU = mybir.AluOpType
ACT = mybir.ActivationFunctionType
AX = mybir.AxisListType

P = 128
N = 3125
F = 64
E = 50000
REL = 32
NBASE = 30
HEADS = 4
NB = -(-N // P)
NFULL = N // P
NREM = N - NFULL * P
T = -(-E // P)
TG = -(-T // P)
SLOTS = -(-(T + NB - 1) // 16) * 16
SG = SLOTS // 4
CH = 4
CW = CH * P
CHUNKS = SLOTS // CH
ITERS = CHUNKS // 2
UNROLL = 4
LOAD = 16
BANK = 512
BIG = 1.0e30
EPS = 1.0e-5


class Link:

    def __init__(self, eng, sem, per=0):
        self.eng, self.sem, self.per, self.base, self.n = eng, sem, per, 0, 0

    def turn(self, it):
        self.base, self.n = it * self.per, 0

    def __call__(self, ins):
        self.n += 1
        ins.then_inc(self.sem, 1)
        self.eng.wait_ge(self.sem, self.base + self.n)


@contextmanager
def semaphore(nc, name):
    yield nc.alloc_semaphore(name=name)


class Space:
    pass


def bcast_rows(ap, parts):
    return ap.rearrange("(o n) -> o n", o=1).broadcast_to([parts, ap.shape[0]])


def node_rows(tab):
    return tab.rearrange("(b p) c -> p b c", p=P)


def build_slots(nc, K, dst, src, edge_type, edge_attr):
    ctx = ExitStack()
    with ctx:
        def sb(name, shape, dt=FP32):
            return ctx.enter_context(nc.sbuf_tensor(name, shape, dt))

        def sem(name):
            return ctx.enter_context(semaphore(nc, name))

        NARR = 5
        dst_i, prev_i, next_i, src_i, typ_i = (sb(n, [P, TG, P], I32) for n in
                                               ("dst_i", "prev_i", "next_i", "src_i", "typ_i"))
        raw = sb("raw", [P, TG, NARR, P])
        att = sb("att", [P, TG, 3 * P])
        thr = sb("thr", [P, NB - 1])
        cmp0 = sb("cmp0", [P, TG, NB - 1])
        cmp1 = sb("cmp1", [P, TG, NB - 1])
        bmin, bmax, dmax, live, cnt, cum, cumex, bmc = (sb(n, [P, TG]) for n in
                                                       ("bmin", "bmax", "dmax", "live", "cnt", "cum", "cumex", "bmc"))
        bmcb = sb("bmcb", [P, TG, P])
        tri = sb("tri", [P, P])
        ones = sb("ones_sq", [P, P])
        iota_s = sb("iota_s", [P, SLOTS])
        iota_g = sb("iota_g", [P, 4])
        own = sb("own", [P, TG, SLOTS])
        ge = sb("ge", [P, SLOTS])
        blk = sb("blk", [P, SLOTS])
        tmp = sb("tmp", [P, SLOTS])
        tmp2 = sb("tmp2", [P, SLOTS])
        rows = sb("rows", [P, 4, 2, P])
        arows = sb("arows", [P, 4, 3, P])
        bcol = sb("bcol", [P, 4])

        pads = sem("pads")
        loads = sem("edge_loads")
        iotas = sem("iotas")
        tri0 = sem("tri0")
        dve = sem("slot_dve")
        counted = sem("tiles_counted")
        cum_ready = sem("cum_ready")
        own_ready = sem("own_ready")
        slots_ready = sem("slots_ready")
        rows_ready = sem("rows_ready")
        rows_taken = sem("rows_taken")
        rows_out = sem("rows_out")
        ident0 = sem("ident0")

        block = ctx.enter_context(nc.Block())
        G3 = TG - 1
        full = T - 1 - G3 * P
        last = E - (T - 1) * P

        @block.gpsimd
        def _(pool):
            for t, v in ((dst_i, -1), (prev_i, -5), (next_i, -1), (src_i, 0), (typ_i, 0)):
                pool.memset(t[:, :, :], v).then_inc(pads, 1)
            pool.memset(att[:, :, :], 0.0).then_inc(pads, 1)
            pool.iota(thr[:, :], pattern=[[P, NB - 1]], base=P, channel_multiplier=0,
                      allow_small_or_imprecise_dtypes=True).then_inc(iotas, 1)
            pool.iota(iota_s[:, :], pattern=[[1, SLOTS]], base=0, channel_multiplier=0,
                      allow_small_or_imprecise_dtypes=True).then_inc(iotas, 1)
            pool.iota(iota_g[:, :], pattern=[[SG, 4]], base=0, channel_multiplier=1,
                      allow_small_or_imprecise_dtypes=True).then_inc(iotas, 1)
            pool.iota(K.iota_row[:, :], pattern=[[1, P]], base=0, channel_multiplier=0,
                      allow_small_or_imprecise_dtypes=True).then_inc(iotas, 1)
            pool.iota(K.iota_part[:, :], pattern=[[0, 1]], base=0, channel_multiplier=1,
                      allow_small_or_imprecise_dtypes=True).then_inc(iotas, 1)
            pool.memset(tri[:, :], 1.0).then_inc(tri0, 1)
            pool.memset(ones[:, :], 1.0).then_inc(tri0, 1)
            pool.memset(K.ones[:, :], 1.0).then_inc(tri0, 1)
            pool.memset(K.zeros[:, :], 0.0).then_inc(tri0, 1)
            pool.memset(K.ident[:, :], 0.0).then_inc(ident0, 1)
            pool.wait_ge(tri0, 4)
            pool.affine_select(out=tri[:, :], in_=tri[:, :], compare_op=ALU.is_ge, fill=0.0, base=0,
                               pattern=[[1, P]], channel_multiplier=-1).then_inc(iotas, 1)
            pool.wait_ge(ident0, 1)
            pool.affine_select(out=K.ident[:, :], in_=K.ident[:, :], compare_op=ALU.not_equal, fill=1.0, base=0,
                               pattern=[[-1, P]], channel_multiplier=1).then_inc(iotas, 1)

        @block.sync
        def _(sp):
            sp.wait_ge(pads, 6)
            body = G3 * P * P
            for t, a in ((dst_i, dst), (src_i, src), (typ_i, edge_type)):
                sp.dma_start(t[:, 0:G3, :], a[0:body].rearrange("(g p e) -> p g e", p=P, e=P)).then_inc(loads, 16)
                sp.dma_start(t[0:full, G3, :], a[body:body + full * P].rearrange("(p e) -> p e", e=P)).then_inc(loads, 16)
                sp.dma_start(t[full:full + 1, G3, 0:last],
                             a[E - last:E].rearrange("(o e) -> o e", o=1)).then_inc(loads, 16)
            sp.dma_start(next_i[:, 0:G3, :], dst[1:body + 1].rearrange("(g p e) -> p g e", p=P, e=P)).then_inc(loads, 16)
            sp.dma_start(next_i[0:full, G3, :],
                         dst[body + 1:body + 1 + full * P].rearrange("(p e) -> p e", e=P)).then_inc(loads, 16)
            sp.dma_start(next_i[full:full + 1, G3, 0:last - 1],
                         dst[E - last + 1:E].rearrange("(o e) -> o e", o=1)).then_inc(loads, 16)
            sp.dma_start(prev_i[0:1, 0, 1:P], dst[0:P - 1].rearrange("(o e) -> o e", o=1)).then_inc(loads, 16)
            sp.dma_start(prev_i[1:P, 0, :], dst[P - 1:P * P - 1].rearrange("(p e) -> p e", e=P)).then_inc(loads, 16)
            sp.dma_start(prev_i[:, 1:G3, :], dst[P * P - 1:body - 1].rearrange("(g p e) -> p g e", p=P, e=P)).then_inc(loads, 16)
            sp.dma_start(prev_i[0:full, G3, :],
                         dst[body - 1:body - 1 + full * P].rearrange("(p e) -> p e", e=P)).then_inc(loads, 16)
            sp.dma_start(prev_i[full:full + 1, G3, 0:last],
                         dst[E - last - 1:E - 1].rearrange("(o e) -> o e", o=1)).then_inc(loads, 16)
            sp.dma_start(att[:, 0:G3, :],
                         edge_attr[0:body, :].rearrange("(g p e) a -> p g (e a)", p=P, e=P)).then_inc(loads, 16)
            sp.dma_start(att[0:full, G3, :],
                         edge_attr[body:body + full * P, :].rearrange("(p e) a -> p (e a)", e=P)).then_inc(loads, 16)
            sp.dma_start(att[full:full + 1, G3, 0:3 * last],
                         edge_attr[E - last:E, :].rearrange("(o e) a -> o (e a)", o=1)).then_inc(loads, 16)
            for sg in range(4):
                sp.wait_ge(rows_taken, 1 + sg)
                sp.dma_start(K.dl_rows[sg * SG:(sg + 1) * SG, :], rows[0:SG, sg, 0, :]).then_inc(rows_out, 16)
                sp.dma_start(K.pen_rows[sg * SG:(sg + 1) * SG, :], rows[0:SG, sg, 1, :]).then_inc(rows_out, 16)
                for a in range(3):
                    sp.dma_start(K.attr_rows[a, sg * SG:(sg + 1) * SG, :], arows[0:SG, sg, a, :]).then_inc(rows_out, 16)
            sp.wait_ge(rows_out, 16 * 5 * 4)

        @block.vector
        def _(v):
            link = Link(v, dve)
            v.wait_ge(loads, 16 * 20)
            v.wait_ge(iotas, 7)
            link(v.tensor_copy(raw[:, :, 0, :], dst_i[:, :, :]))
            link(v.tensor_tensor(raw[:, :, 1, :], dst_i[:, :, :], prev_i[:, :, :], ALU.is_equal))
            link(v.tensor_copy(raw[:, :, 2, :], src_i[:, :, :]))
            link(v.tensor_copy(raw[:, :, 3, :], typ_i[:, :, :]))
            link(v.tensor_tensor(raw[:, :, 4, :], dst_i[:, :, :], next_i[:, :, :], ALU.not_equal))
            link(v.tensor_tensor(cmp0[:, :, :], raw[:, :, 0, 0:1].broadcast_to([P, TG, NB - 1]),
                                 thr[:, :].unsqueeze(1).broadcast_to([P, TG, NB - 1]), ALU.is_ge))
            link(v.tensor_reduce(bmin[:, :], cmp0[:, :, :], AX.X, ALU.add))
            link(v.tensor_reduce(dmax[:, :], raw[:, :, 0, :], AX.X, ALU.max))
            link(v.tensor_tensor(cmp1[:, :, :], dmax[:, :].unsqueeze(2).broadcast_to([P, TG, NB - 1]),
                                 thr[:, :].unsqueeze(1).broadcast_to([P, TG, NB - 1]), ALU.is_ge))
            link(v.tensor_reduce(bmax[:, :], cmp1[:, :, :], AX.X, ALU.add))
            link(v.tensor_scalar(live[:, :], raw[:, :, 0, 0], 0.0, None, ALU.is_ge))
            link(v.scalar_tensor_tensor(out=cnt[:, :], in0=bmax[:, :], scalar=1.0, in1=bmin[:, :],
                                        op0=ALU.add, op1=ALU.subtract))
            link(v.tensor_tensor(cnt[:, :], cnt[:, :], live[:, :], ALU.mult))
            v.sem_inc(counted, 1)
            v.wait_ge(cum_ready, 1)
            link(v.tensor_copy(cum[:, :], K.ps[:, 0:TG]))
            link(v.tensor_tensor(cumex[:, :], cum[:, :], cnt[:, :], ALU.subtract))
            link(v.tensor_tensor(bmc[:, :], bmin[:, :], cumex[:, :], ALU.subtract))
            link(v.tensor_copy(bmcb[:, :, :], bmc[:, :].unsqueeze(2).broadcast_to([P, TG, P])))
            for g in range(TG):
                link(v.tensor_scalar(ge[:, :], iota_s[:, :], cum[:, g:g + 1], None, ALU.is_ge))
                link(v.scalar_tensor_tensor(out=own[:, g, :], in0=iota_s[:, :], scalar=cumex[:, g:g + 1],
                                            in1=ge[:, :], op0=ALU.is_ge, op1=ALU.subtract))
            v.sem_inc(own_ready, 1)
            v.wait_ge(slots_ready, 5)
            link(v.tensor_tensor(blk[:, :], K.ps[:, 4 * BANK:4 * BANK + SLOTS], iota_s[:, :], ALU.add))
            link(v.tensor_scalar(blk[:, :], blk[:, :], float(NB - 1), None, ALU.min))
            link(v.tensor_copy(K.blk_i[:, :], blk[:, :]))
            link(v.scalar_tensor_tensor(out=K.dl[:, :], in0=blk[:, :], scalar=-float(P),
                                        in1=K.ps[:, 0:SLOTS], op0=ALU.mult, op1=ALU.add))
            link(v.tensor_copy(K.src_idx[:, :], K.ps[:, BANK:BANK + SLOTS]))
            link(v.tensor_copy(tmp[:, :], K.ps[:, BANK:BANK + SLOTS]))
            link(v.scalar_tensor_tensor(out=tmp2[:, :], in0=tmp[:, :], scalar=float(REL),
                                        in1=K.ps[:, 2 * BANK:2 * BANK + SLOTS], op0=ALU.mult, op1=ALU.add))
            link(v.tensor_copy(K.rel_idx[:, :], tmp2[:, :]))
            link(v.scalar_tensor_tensor(out=tmp[:, :], in0=K.dl[:, :], scalar=1.0,
                                        in1=K.ps[:, 3 * BANK:3 * BANK + SLOTS], op0=ALU.add, op1=ALU.mult))
            link(v.tensor_scalar(K.dl_end[:, :], tmp[:, :], -1.0, None, ALU.add))
            for sg in range(4):
                v.wait_ge(rows_ready, sg + 1)
                o = 5 * BANK
                link(v.tensor_tensor(bcol[0:SG, sg:sg + 1], K.ps[0:SG, o + 2 * P:o + 2 * P + 1],
                                     iota_g[0:SG, sg:sg + 1], ALU.add))
                link(v.tensor_scalar(bcol[0:SG, sg:sg + 1], bcol[0:SG, sg:sg + 1], float(NB - 1), -float(P),
                                     ALU.min, ALU.mult))
                link(v.tensor_scalar(rows[0:SG, sg, 0, :], K.ps[0:SG, o:o + P], bcol[0:SG, sg:sg + 1], None, ALU.add))
                link(v.tensor_scalar(rows[0:SG, sg, 1, :], K.ps[0:SG, o + P:o + 2 * P], -1.0, BIG, ALU.add, ALU.mult))
                o = 6 * BANK
                link(v.tensor_copy(arows[0:SG, sg, :, :], K.ps[0:SG, o:o + 3 * P].rearrange("p (e a) -> p a e", a=3)))
                v.sem_inc(rows_taken, 1)

        @block.tensor
        def _(pe):
            pe.wait_ge(counted, 1)
            for g in range(TG):
                pe.matmul(K.ps[:, g:g + 1], tri[:, :], cnt[:, g:g + 1], start=True, stop=g == 0, skip_group_check=True)
                for h in range(g):
                    ins = pe.matmul(K.ps[:, g:g + 1], ones[:, :], cnt[:, h:h + 1], start=False, stop=h == g - 1,
                                    skip_group_check=True)
            ins.then_inc(cum_ready, 1)
            pe.wait_ge(own_ready, 1)
            for b, k in enumerate((0, 2, 3, 4, None)):
                for g in range(TG):
                    lhs = bmcb[:, g, :] if k is None else raw[:, g, k, :]
                    ins = pe.matmul(K.ps[:, b * BANK:b * BANK + SLOTS], lhs, own[:, g, :], start=g == 0, stop=g == TG - 1)
                ins.then_inc(slots_ready, 1)
            for sg in range(4):
                if sg:
                    pe.wait_ge(rows_taken, sg)
                part = own[:, :, sg * SG:(sg + 1) * SG]
                for g in range(TG):
                    pe.matmul(K.ps[0:SG, 5 * BANK:5 * BANK + 2 * P], part[:, g, :],
                              raw[:, g, 0:2, :].rearrange("p k e -> p (k e)"), start=g == 0, stop=g == TG - 1)
                for g in range(TG):
                    pe.matmul(K.ps[0:SG, 5 * BANK + 2 * P:5 * BANK + 2 * P + 1], part[:, g, :], bmc[:, g:g + 1],
                              start=False, stop=g == TG - 1, skip_group_check=True)
                for g in range(TG):
                    ins = pe.matmul(K.ps[0:SG, 6 * BANK:6 * BANK + 3 * P], part[:, g, :], att[:, g, :],
                                    start=g == 0, stop=g == TG - 1)
                ins.then_inc(rows_ready, 1)


def onehot(v, out, iota_row, dl_chunk):
    return v.tensor_tensor(out, iota_row.unsqueeze(1).broadcast_to([P, CH, P]),
                           dl_chunk.unsqueeze(2).broadcast_to([P, CH, P]), ALU.is_equal)


def split3(v, link, parts, rest):
    for q, part in enumerate(parts):
        link(v.tensor_copy(part, rest))
        if q < 2:
            link(v.tensor_tensor(rest, rest, part, ALU.subtract))


def clear_banks(pe, K, first, count):
    for b in range(first, first + count):
        ins = pe.matmul(K.ps[:, b * BANK:(b + 1) * BANK], K.zeros[:, 0:P], K.zeros[:, :], start=True, stop=False,
                        skip_group_check=True)
    return ins


def count_degrees(nc, K):
    ctx = ExitStack()
    with ctx:
        hot = [ctx.enter_context(nc.sbuf_tensor(f"hot{k}", [P, CH, P], BF16)) for k in range(2)]
        one = ctx.enter_context(nc.sbuf_tensor("deg_one", [P, 1], BF16))
        hot_ready = ctx.enter_context(semaphore(nc, "deg_hot_ready"))
        hot_free = ctx.enter_context(semaphore(nc, "deg_hot_free"))
        deg_link = ctx.enter_context(semaphore(nc, "deg_link"))
        root_ready = ctx.enter_context(semaphore(nc, "deg_root"))
        block = ctx.enter_context(nc.Block())

        @block.vector
        def _(v):
            v.memset(one[:, :], 1.0).then_inc(hot_ready, 1)

            def targets(c, k, turn):
                v.wait_ge(hot_free, c + 1)
                onehot(v, hot[k][:, :, :], K.iota_row[:, :], K.dl[:, bass.ds(c * CH, CH)]).then_inc(hot_ready, 1)
            pipeline(v, [(0, targets)])
            link = Link(v, deg_link)
            v.wait_ge(hot_free, 2 + 2 * ITERS)
            link(v.tensor_copy(K.deg[:, :], K.ps[:, 0:NB]))
            link(v.tensor_scalar(K.deg1[:, :], K.deg[:, :], 1.0, None, ALU.max))
            link(v.tensor_scalar(K.has[:, :], K.deg[:, :], 0.0, None, ALU.is_gt))
            link(v.reciprocal(K.rdeg[:, :], K.deg1[:, :]))
            v.wait_ge(root_ready, 1)
            link(v.tensor_tensor(K.dis[:, :], K.dis[:, :], K.has[:, :], ALU.mult))

        @block.scalar
        def _(act):
            act.wait_ge(deg_link, 4)
            act.activation(K.dis[:, :], K.rdeg[:, :], ACT.Sqrt).then_inc(root_ready, 1)

        @block.tensor
        def _(pe):
            clear_banks(pe, K, 0, 1).then_inc(hot_free, 2)

            blocks = SlotBlocks(nc, K, pe)

            def count(c, k, turn):
                at = blocks.now()
                pe.wait_ge(hot_ready, c + 2)
                pe.nop(nofuse=True)
                for j in range(CH):
                    ins = pe.matmul(K.ps[:, bass.ds(at[j], 1)], hot[k][:, j, :], one[:, :], start=False, stop=False,
                                    skip_group_check=True)
                ins.then_inc(hot_free, 1)
            pipeline(pe, [(0, count)], blocks=blocks)


def pipeline(eng, stages, chunks=CHUNKS, blocks=None):
    stages = [st if len(st) == 3 else st + (2,) for st in stages]
    lags = max(lag for lag, _, _ in stages)
    head, full = -(-(lags + 2) // UNROLL), chunks // UNROLL

    def turn(t):
        if blocks:
            blocks.turn(t)
        for k in range(UNROLL):
            for lag, step, buffers in stages:
                c = t * UNROLL + (k - lag)
                if isinstance(t, int) and not 0 <= c < chunks:
                    continue
                if blocks:
                    blocks.offset = k - lag
                step(c, (k - lag) % buffers, t * (UNROLL // buffers) + (k - lag) // buffers)

    for t in range(head):
        turn(t)
    with eng.Fori(head, full) as t:
        turn(t)
    for t in range(full, -(-(chunks + lags) // UNROLL)):
        turn(t)


class SlotBlocks:

    def __init__(self, nc, K, eng, back=0):
        self.nc, self.K, self.eng, self.back = nc, K, eng, back

    def turn(self, t):
        self.first, end = t * UNROLL - self.back, t * UNROLL + UNROLL
        count = UNROLL + self.back
        self.skipped = 0
        if isinstance(t, int):
            self.skipped = max(0, -self.first)
            self.first += self.skipped
            count = min(end, CHUNKS) - self.first
        self.registers = []
        for lo in range(0, count * CH, LOAD):
            self.registers += self.nc.values_load_multi_w_load_instructions(
                self.K.blk_i[0:1, bass.ds(self.first * CH + lo, min(LOAD, count * CH - lo))], engines=[self.eng.engine],
                min_val=0, max_val=NB - 1,
                skip_runtime_bounds_check_because="build_slots clamps every block number to 0..NB - 1")[1]

    def now(self):
        at = (self.offset + self.back - self.skipped) * CH
        return self.registers[at:at + CH]


def gather(pool, ring, idx, table, rows_in):
    for j in range(CH):
        pool.indirect_dma_start(out=ring[:, j, :], out_offset=None, in_=table,
                                in_offset=bass.IndirectOffsetOnAxis(ap=idx[:, j:j + 1], axis=0)).then_inc(rows_in, 16)


def gather_sum(nc, K, table, index, tag, side):
    ctx = ExitStack()
    with ctx:
        hot = [ctx.enter_context(nc.sbuf_tensor(f"{tag}_hot{k}", [P, CH, P], FP32)) for k in range(2)]
        ring = [ctx.enter_context(nc.sbuf_tensor(f"{tag}_ring{k}", [P, CH, F], FP32)) for k in range(4)]
        idx = [ctx.enter_context(nc.sbuf_tensor(f"{tag}_idx{k}", [P, CH], I32)) for k in range(4)]
        hot_ready = ctx.enter_context(semaphore(nc, f"{tag}_hot_ready"))
        idx_ready = ctx.enter_context(semaphore(nc, f"{tag}_idx_ready"))
        rows_in = [ctx.enter_context(semaphore(nc, f"{tag}_rows_in{k}")) for k in range(4)]
        chunk_free = ctx.enter_context(semaphore(nc, f"{tag}_chunk_free"))
        block = ctx.enter_context(nc.Block())

        @block.gpsimd
        def _(pool):
            def rows(c, k, turn):
                pool.wait_ge(idx_ready, c + 1)
                pool.nop(nofuse=True)
                gather(pool, ring[k], idx[k], table, rows_in[k])
            pipeline(pool, [(0, rows, 4)])

        @block.vector
        def _(v):
            def indices(c, k, turn):
                v.wait_ge(chunk_free, c + 1)
                v.tensor_copy(idx[k][:, :], index[:, bass.ds(c * CH, CH)]).then_inc(idx_ready, 1)

            def targets(c, k, turn):
                v.wait_ge(chunk_free, c + 3)
                onehot(v, hot[k][:, :, :], K.iota_row[:, :], K.dl[:, bass.ds(c * CH, CH)]).then_inc(hot_ready, 1)
            pipeline(v, [(0, indices, 4), (2, targets)] + [(st[0] + 2, *st[1:]) for st in side.vector(v)])

        @block.tensor
        def _(pe):
            clear_banks(pe, K, 0, 4).then_inc(chunk_free, 4)
            blocks = SlotBlocks(nc, K, pe)

            def add(c, k, turn):
                at = blocks.now()
                pe.wait_ge(hot_ready, c + 1)
                pe.wait_ge(rows_in[k], turn * (16 * CH) + 16 * CH)
                pe.nop(nofuse=True)
                for j in range(CH):
                    ins = pe.matmul(K.ps[:, bass.ds(at[j] * F, F)], hot[k % 2][:, j, :], ring[k][:, j, :],
                                    start=False, stop=False, skip_group_check=True)
                ins.then_inc(chunk_free, 1)
            pipeline(pe, [(0, add, 4)] + side.tensor(pe), blocks=blocks)

        @block.scalar
        def _(act):
            stages = side.scalar(act)
            if stages:
                pipeline(act, stages)

        @block.sync
        def _(sp):
            stages = side.sync(sp)
            if stages:
                pipeline(sp, stages)
            side.finish(sp)


def per_node(ap, width=F):
    return ap.unsqueeze(2).broadcast_to([P, NB, width])


def per_feature(ap):
    return ap.unsqueeze(1).broadcast_to([P, NB, F])


def sums(K):
    return K.ps[:, 0:NB * F].rearrange("p (b c) -> p b c", c=F)


def layernorm_steps(v, link, K, y, out, sq, mean, var, std_wanted, std_ready):
    link(v.tensor_reduce(mean, y, AX.X, ALU.add))
    link(v.tensor_scalar(mean, mean, -1.0 / F, None, ALU.mult))
    link(v.tensor_tensor(y, y, per_node(mean), ALU.add))
    link(v.tensor_tensor(sq, y, y, ALU.mult))
    link(v.tensor_reduce(var, sq, AX.X, ALU.add))
    link(v.tensor_scalar(var, var, 1.0 / F, EPS, ALU.mult, ALU.add))
    v.sem_inc(std_wanted, 1)
    v.wait_ge(std_ready, 1)
    link(v.reciprocal(var, var))
    link(v.tensor_tensor(out, y, per_node(var), ALU.mult))


def appnp(nc, K, x_in, alpha, enc):
    ctx = ExitStack()
    with ctx:
        scaled = ctx.enter_context(nc.sbuf_tensor("scaled", [P, NB, F], FP32))
        total = ctx.enter_context(nc.sbuf_tensor("total", [P, NB, F], FP32))
        hop = ctx.enter_context(nc.sbuf_tensor("hop", [P, NB, F], FP32))
        al = ctx.enter_context(nc.sbuf_tensor("al", [P, 3], FP32))
        mean = ctx.enter_context(nc.sbuf_tensor("mean0", [P, NB], FP32))
        var = ctx.enter_context(nc.sbuf_tensor("var0", [P, NB], FP32))

        def prepare():
            c2 = ExitStack()
            with c2:
                x_loaded = c2.enter_context(semaphore(nc, "x_loaded"))
                x_pad = c2.enter_context(semaphore(nc, "x_pad"))
                made = c2.enter_context(semaphore(nc, "a_made"))
                stored = c2.enter_context(semaphore(nc, "a_stored"))
                block = c2.enter_context(nc.Block())

                @block.sync
                def _(sp):
                    sp.wait_ge(x_pad, 1)
                    sp.dma_start(K.x[:, 0:NFULL, :], node_rows(x_in[0:NFULL * P, :])).then_inc(x_loaded, 16)
                    sp.dma_start(K.x[0:NREM, NFULL, :], x_in[NFULL * P:N, :]).then_inc(x_loaded, 16)
                    sp.dma_start(al[:, :], bcast_rows(alpha, P)).then_inc(x_loaded, 16)
                    sp.wait_ge(made, 1)
                    sp.dma_start(node_rows(K.tab64), scaled[:, :, :]).then_inc(stored, 16)
                    sp.wait_ge(stored, 16)

                @block.vector
                def _(v):
                    v.memset(K.x[:, NFULL, :], 0.0).then_inc(x_pad, 1)
                    v.wait_ge(x_loaded, 48)
                    v.tensor_tensor(scaled[:, :, :], K.x[:, :, :], per_node(K.dis[:, :]), ALU.mult).then_inc(made, 1)

        def between(second):
            c2 = ExitStack()
            with c2:
                made = c2.enter_context(semaphore(nc, f"a_made{second}"))
                steps = c2.enter_context(semaphore(nc, f"a_steps{second}"))
                stored = c2.enter_context(semaphore(nc, f"a_stored{second}"))
                wanted = c2.enter_context(semaphore(nc, f"a_wanted{second}"))
                ready = c2.enter_context(semaphore(nc, f"a_ready{second}"))
                block = c2.enter_context(nc.Block())

                @block.vector
                def _(v):
                    link = Link(v, steps)
                    link(v.tensor_tensor(hop[:, :, :], sums(K), per_node(K.dis[:, :]), ALU.mult))
                    if not second:
                        v.tensor_tensor(scaled[:, :, :], hop[:, :, :], per_node(K.dis[:, :]), ALU.mult).then_inc(made, 1)
                        link(v.tensor_scalar(total[:, :, :], K.x[:, :, :], al[:, 0:1], None, ALU.mult))
                    link(v.scalar_tensor_tensor(out=total[:, :, :], in0=hop[:, :, :], scalar=al[:, 1 + second:2 + second],
                                                in1=total[:, :, :], op0=ALU.mult, op1=ALU.add))
                    if second:
                        link(v.tensor_tensor(total[:, :, :], total[:, :, :], K.x[:, :, :], ALU.add))
                        layernorm_steps(v, link, K, total[:, :, :], K.x[:, :, :], hop[:, :, :], mean[:, :], var[:, :],
                                        wanted, ready)

                if second:
                    @block.scalar
                    def _(act):
                        act.wait_ge(wanted, 1)
                        act.activation(var[:, :], var[:, :], ACT.Sqrt).then_inc(ready, 1)
                else:
                    @block.sync
                    def _(sp):
                        sp.wait_ge(made, 1)
                        sp.dma_start(node_rows(K.tab64), scaled[:, :, :]).then_inc(stored, 16)
                        sp.wait_ge(stored, 16)

        prepare()
        with ExitStack() as c:
            gather_sum(nc, K, K.tab64, K.src_idx, "hop1", FirstVariance(nc, K, c, enc))
        between(0)
        reciprocal_roots(nc, K, enc.var[:, :], "v1", rows=True)
        with ExitStack() as c:
            gather_sum(nc, K, K.tab64, K.src_idx, "hop2", SecondProduct(nc, K, c, enc))
        between(1)


def store_out(nc, K, out):
    with semaphore(nc, "out_stored") as stored, nc.Block() as block:
        @block.sync
        def _(sp):
            sp.dma_start(node_rows(out[0:NFULL * P, :]), K.x[:, 0:NFULL, :]).then_inc(stored, 16)
            sp.dma_start(out[NFULL * P:N, :], K.x[0:NREM, NFULL, :]).then_inc(stored, 16)
            sp.wait_ge(stored, 32)



def transpose_nodes(nc, K, nodes, out, tag):
    with semaphore(nc, f"{tag}_turned") as turned, semaphore(nc, f"{tag}_taken") as taken, nc.Block() as block:
        groups = [(q, min(q + 4, NB)) for q in range(0, NB, 4)]

        @block.tensor
        def _(pe):
            for i, (lo, hi) in enumerate(groups):
                for b in range(lo, hi):
                    o = i * BANK + (b - lo) * P
                    ins = pe.transpose(K.ps[0:F, o:o + P], nodes[:, b, :], K.ident[:, :])
                ins.then_inc(turned, 1)

        @block.vector
        def _(v):
            for i, (lo, hi) in enumerate(groups):
                v.wait_ge(turned, i + 1)
                v.tensor_copy(out[:, lo * P:hi * P], K.ps[0:F, i * BANK:i * BANK + (hi - lo) * P]).then_inc(taken, 1)
            v.wait_ge(taken, len(groups))


def project(nc, K, xT, w, cols, out, tag):
    per = BANK // cols
    groups = [(q, min(q + per, NB)) for q in range(0, NB, per)]
    with semaphore(nc, f"{tag}_made") as made, semaphore(nc, f"{tag}_copied") as copied, nc.Block() as block:
        @block.tensor
        def _(pe):
            for i, (lo, hi) in enumerate(groups):
                if i >= 8:
                    pe.wait_ge(copied, i - 7)
                for b in range(lo, hi):
                    o = (i % 8) * BANK + (b - lo) * cols
                    ins = pe.matmul(K.ps[:, o:o + cols], xT[:, b * P:(b + 1) * P], w, start=True, stop=True,
                                    skip_group_check=True)
                ins.then_inc(made, 1)

        @block.vector
        def _(v):
            for i, (lo, hi) in enumerate(groups):
                v.wait_ge(made, i + 1)
                o = (i % 8) * BANK
                v.tensor_copy(out[:, lo:hi, :], K.ps[:, o:o + (hi - lo) * cols].rearrange("p (b c) -> p b c", c=cols)
                              ).then_inc(copied, 1)
            v.wait_ge(copied, len(groups))


def store_table(nc, K, table, pieces, tag):
    with semaphore(nc, f"{tag}_stored") as stored, nc.Block() as block:
        @block.sync
        def _(sp):
            for col, width, ap in pieces:
                sp.dma_start(node_rows(table)[:, :, col:col + width], ap).then_inc(stored, 16)
            sp.wait_ge(stored, 16 * len(pieces))


def attention(nc, K, H, table, x, als, ald, z, tag):
    ctx = ExitStack()
    with ctx:
        GW = F + H
        HP = min(H, 2)
        MW = F + 1 if H == 1 else HP * F

        def sb(name, shape, dt=FP32):
            return ctx.enter_context(nc.sbuf_tensor(f"{tag}_{name}", shape, dt))

        kept = sb("kept", [P, SLOTS, GW])
        hot = [sb(f"hot{k}", [P, CH, P]) for k in range(2)]
        spread = sb("spread", [P, NB, 2, H, 3], BF16)
        selfw = sb("selfw", [P, NB, H])
        t0, t1 = sb("t0", [P, NB, H]), sb("t1", [P, NB, H])
        weight = sb("weight", [P, SLOTS, H])

        def gather_and_max():
            c = ExitStack()
            with c:
                def sb2(name, shape, dt=FP32):
                    return c.enter_context(nc.sbuf_tensor(f"{tag}_{name}", shape, dt))

                def sem(name):
                    return c.enter_context(semaphore(nc, f"{tag}_{name}"))

                ring = [sb2(f"ring{k}", [P, CH, GW]) for k in range(4)]
                idx = [sb2(f"idx{k}", [P, CH], I32) for k in range(4)]
                pen = [sb2(f"pen{k}", [H, CW]) for k in range(2)]
                run = [sb2(f"run{k}", [H, CW]) for k in range(2)]
                mx = [sb2(f"mx{k}", [P, CH * H]) for k in range(2)]
                idx_ready, hot_ready, added = sem("idx_ready"), sem("hot_ready"), sem("added")
                rows_in = [sem(f"rows_in{k}") for k in range(4)]
                pen_in = [sem(f"pen_in{k}") for k in range(2)]
                rows_kept, turned, scanned, back, mx_ready, start = (sem(n) for n in (
                    "rows_kept", "turned", "scanned", "back", "mx_ready", "start"))
                block = c.enter_context(nc.Block())

                @block.gpsimd
                def _(pool):
                    def rows(c, k, turn):
                        pool.wait_ge(idx_ready, c + 1)
                        pool.nop(nofuse=True)
                        gather(pool, ring[k], idx[k], table, rows_in[k])
                    pipeline(pool, [(0, rows, 4)])

                @block.sync
                def _(sp):
                    def penalties(c, k, turn):
                        sp.wait_ge(scanned, c + 1)
                        sp.dma_start(pen[k][:, :], bcast_chunk(K.pen_rows[bass.ds(c * CH, CH), :], H)).then_inc(pen_in[k], 16)
                    pipeline(sp, [(0, penalties)])

                @block.scalar
                def _(act):
                    act.sem_inc(rows_kept, 4)

                    def keep(c, k, turn):
                        act.wait_ge(rows_in[k], turn * (16 * CH) + 16 * CH)
                        act.copy(kept[:, bass.ds(c * CH, CH), :], ring[k][:, :, :]).then_inc(rows_kept, 1)

                    def maxima(c, k, turn):
                        act.wait_ge(back, c + 1)
                        act.wait_ge(added, c + 1)
                        act.copy(mx[k][:, :], K.ps[:, (3 + k) * BANK:(3 + k) * BANK + CH * H]).then_inc(mx_ready, 1)
                    pipeline(act, [(0, keep, 4), (2, maxima)])

                @block.vector
                def _(v):
                    v.memset(run[1][:, :], -BIG).then_inc(start, 1)
                    v.wait_ge(start, 1)
                    v.sem_inc(scanned, 2)

                    def indices(c, k, turn):
                        v.wait_ge(rows_kept, c + 1)
                        if not (isinstance(c, int) and c < 2):
                            v.wait_ge(turned, c - 1)
                        v.tensor_copy(idx[k][:, :], K.src_idx[:, bass.ds(c * CH, CH)]).then_inc(idx_ready, 1)

                    def scan(c, k, turn):
                        v.wait_ge(pen_in[k], turn * 16 + 16)
                        v.wait_ge(turned, c + 3)
                        if not (isinstance(c, int) and c < 2):
                            v.wait_ge(back, c - 1)
                        v.wait_ge(scanned, c + 2)
                        v.tensor_tensor_scan(run[k][:, :], pen[k][:, :], K.ps[0:H, (1 + k) * BANK:(2 + k) * BANK],
                                             run[1 - k][:, CW - 1:CW], ALU.add, ALU.max).then_inc(scanned, 1)

                    def ends(c, k, turn):
                        v.wait_ge(added, c + 1)
                        onehot(v, hot[k][:, :, :], K.iota_row[:, :], K.dl_end[:, bass.ds(c * CH, CH)]).then_inc(hot_ready, 1)
                    pipeline(v, [(0, indices, 4), (2, scan), (3, ends)])

                @block.tensor
                def _(pe):
                    clear_banks(pe, K, 0, 1).then_inc(added, 2)
                    pe.sem_inc(turned, 2)
                    blocks = SlotBlocks(nc, K, pe, back=3)

                    def turn_scores(c, k, turn):
                        pe.wait_ge(rows_in[k], turn * (16 * CH) + 16 * CH)
                        pe.wait_ge(scanned, c + 1)
                        pe.nop(nofuse=True)
                        for j in range(CH):
                            o = (1 + k % 2) * BANK + j * P
                            ins = pe.transpose(K.ps[0:H, o:o + P], ring[k][:, j, F:GW], K.ident[:, :])
                        ins.then_inc(turned, 1)

                    def turn_back(c, k, turn):
                        pe.wait_ge(scanned, c + 3)
                        if not (isinstance(c, int) and c < 2):
                            pe.wait_ge(mx_ready, c - 1)
                        pe.nop(nofuse=True)
                        for j in range(CH):
                            o = (3 + k) * BANK + j * H
                            ins = pe.transpose(K.ps[:, o:o + H], run[k][:, j * P:(j + 1) * P], K.ident[0:H, 0:H])
                        ins.then_inc(back, 1)

                    def pick_ends(c, k, turn):
                        at = blocks.now()
                        pe.wait_ge(mx_ready, c + 1)
                        pe.wait_ge(hot_ready, c + 1)
                        pe.nop(nofuse=True)
                        for j in range(CH):
                            ins = pe.matmul(K.ps[:, bass.ds(at[j] * H, H)], hot[k][:, j, :], mx[k][:, j * H:(j + 1) * H],
                                            start=False, stop=False, skip_group_check=True)
                        ins.then_inc(added, 1)
                    pipeline(pe, [(0, turn_scores, 4), (2, turn_back), (3, pick_ends)], blocks=blocks)

        def node_maxima():
            with semaphore(nc, f"{tag}_nm") as steps, semaphore(nc, f"{tag}_nmw") as wanted, \
                    semaphore(nc, f"{tag}_nmr") as ready, \
                    nc.sbuf_tensor(f"{tag}_top", [P, NB, H], FP32) as top, nc.Block() as block:
                mxs = K.ps[:, 0:NB * H].rearrange("p (b h) -> p b h", h=H)

                @block.vector
                def _(v):
                    link = Link(v, steps)
                    link(v.tensor_scalar(K.deg1[:, :], K.has[:, :], -1.0, BIG, ALU.add, ALU.mult))
                    link(v.tensor_tensor(t0[:, :, :], mxs, per_node(K.deg1[:, :], H), ALU.add))
                    link(v.tensor_tensor(t0[:, :, :], t0[:, :, :], als, ALU.max))
                    link(v.tensor_tensor(t0[:, :, :], t0[:, :, :], ald, ALU.add))
                    link(v.scalar_tensor_tensor(out=top[:, :, :], in0=t0[:, :, :], scalar=0.2, in1=t0[:, :, :],
                                                op0=ALU.mult, op1=ALU.max))
                    link(v.tensor_tensor(t0[:, :, :], als, ald, ALU.add))
                    link(v.scalar_tensor_tensor(out=t1[:, :, :], in0=t0[:, :, :], scalar=0.2, in1=t0[:, :, :],
                                                op0=ALU.mult, op1=ALU.max))
                    link(v.tensor_tensor(t1[:, :, :], t1[:, :, :], top[:, :, :], ALU.subtract))
                    v.sem_inc(wanted, 1)
                    link(v.tensor_copy(t0[:, :, :], ald))
                    split3(v, link, [spread[:, :, 0, :, q] for q in range(3)], t0[:, :, :])
                    split3(v, link, [spread[:, :, 1, :, q] for q in range(3)], top[:, :, :])

                @block.scalar
                def _(act):
                    act.wait_ge(wanted, 1)
                    act.activation(selfw[:, :, :], t1[:, :, :], ACT.Exp).then_inc(ready, 1)
                    act.wait_ge(ready, 1)

        def weigh_and_sum():
            c = ExitStack()
            with c:
                def sem(name):
                    return c.enter_context(semaphore(nc, f"{tag}_{name}"))

                def tiles(name, shape, count, dt=FP32):
                    return [c.enter_context(nc.sbuf_tensor(f"{tag}_{name}{k}", shape, dt)) for k in range(count)]

                dlb = tiles("dlb", [P, CW], 4)
                cold = tiles("cold", [P, CW], 2, BF16)
                got = tiles("got", [P, CH, 2, H], 2)
                score = tiles("score", [P, CH, H], 2)
                msg = tiles("msg", [P, CH, MW], 2)
                dl_in = [sem(f"dl_in{k}") for k in range(4)]
                cold_ready, spread_done, fetched, added, kinked, scored, weighed, msg_ready, chunk_free, steps = (
                    sem(n) for n in ("cold_ready", "spread_done", "fetched", "sc_added", "sc_kinked", "scored", "weighed",
                                     "msg_ready", "msg_free", "norm"))
                MSGS = 3 if H == 1 else 2
                block = c.enter_context(nc.Block())

                @block.sync
                def _(sp):
                    def targets(c, k, turn):
                        sp.wait_ge(cold_ready, c + 1)
                        sp.dma_start(dlb[k][:, :], bcast_chunk(K.dl_rows[bass.ds(c * CH, CH), :], P)).then_inc(dl_in[k], 16)
                    pipeline(sp, [(0, targets, 4)])

                @block.vector
                def _(v):
                    v.sem_inc(cold_ready, 4)

                    def fetch(c, k, turn):
                        v.wait_ge(spread_done, c + 1)
                        v.tensor_reduce(got[k][:, :, :, :],
                                        K.ps[:, 7 * BANK:7 * BANK + CH * 6 * H].rearrange(
                                            "p (s t h q) -> p s t h q", t=2, h=H, q=3), AX.X, ALU.add).then_inc(fetched, 1)

                    def build(c, k, turn):
                        v.wait_ge(dl_in[k], turn * 16 + 16)
                        if not (isinstance(c, int) and c < 2):
                            v.wait_ge(spread_done, c - 1)
                        v.tensor_scalar(cold[k % 2][:, :], dlb[k][:, :], K.iota_part[:, 0:1], None, ALU.is_equal
                                        ).then_inc(cold_ready, 1)

                    def add(c, k, turn):
                        v.wait_ge(fetched, c + 1)
                        v.wait_ge(weighed, c + 1)
                        v.tensor_tensor(score[k][:, :, :], kept[:, bass.ds(c * CH, CH), F:GW], got[k][:, :, 0, :], ALU.add
                                        ).then_inc(added, 1)

                    def kink(c, k, turn):
                        v.wait_ge(added, c + 1)
                        sc = score[k][:, :, :]
                        v.scalar_tensor_tensor(out=sc, in0=sc, scalar=0.2, in1=sc, op0=ALU.mult, op1=ALU.max
                                               ).then_inc(kinked, 1)

                    def below_max(c, k, turn):
                        v.wait_ge(kinked, c + 1)
                        v.tensor_tensor(score[k][:, :, :], score[k][:, :, :], got[k][:, :, 1, :], ALU.subtract
                                        ).then_inc(scored, 1)

                    def targets(c, k, turn):
                        v.wait_ge(chunk_free, c + 1)
                        onehot(v, hot[k][:, :, :], K.iota_row[:, :], K.dl[:, bass.ds(c * CH, CH)]).then_inc(msg_ready, 1)

                    def messages(c, k, turn):
                        v.wait_ge(weighed, c + 3)
                        message(v, msg[k][:, :, 0:HP * F], c, 0).then_inc(msg_ready, 1)
                        if H == 1:
                            v.tensor_scalar(msg[k][:, :, F:F + 1], weight[:, bass.ds(c * CH, CH), :], 1.0, None, ALU.min
                                            ).then_inc(msg_ready, 1)
                    pipeline(v, [(0, build, 4), (1, fetch), (2, targets), (1, add), (2, messages), (1, kink), (1, below_max)])
                    v.wait_ge(chunk_free, 2 + CHUNKS)
                    link = Link(v, steps)
                    with_self_loop(v, link, 0)
                    if H == 1:
                        divide(v, link, K.ps[:, 0:NB * P].rearrange("p (b c) -> p b c", c=P)[:, :, F:F + 1])

                @block.scalar
                def _(act):
                    act.sem_inc(weighed, 2)

                    def weigh(c, k, turn):
                        act.wait_ge(scored, c + 1)
                        act.activation(weight[:, bass.ds(c * CH, CH), :], score[k][:, :, :], ACT.Exp).then_inc(weighed, 1)
                    pipeline(act, [(0, weigh)])

                @block.tensor
                def _(pe):
                    clear_banks(pe, K, 0, 7).then_inc(chunk_free, 2)
                    blocks = SlotBlocks(nc, K, pe, back=2)
                    flat = spread[:, :, :, :, :].rearrange("p b t h q -> p (b t h q)")

                    def spread_out(c, k, turn):
                        at = blocks.now()
                        pe.wait_ge(cold_ready, c + 5)
                        if not (isinstance(c, int) and c < 1):
                            pe.wait_ge(fetched, c)
                        pe.nop(nofuse=True)
                        for j in range(CH):
                            o = 7 * BANK + j * 6 * H
                            ins = pe.matmul(K.ps[:, o:o + 6 * H], cold[k][:, j * P:(j + 1) * P],
                                            flat[:, bass.ds(at[j] * (6 * H), 6 * H)], start=True, stop=True,
                                            skip_group_check=True)
                        ins.then_inc(spread_done, 1)

                    def add_up(c, k, turn):
                        at = blocks.now()
                        pe.wait_ge(msg_ready, c * MSGS + MSGS)
                        pe.nop(nofuse=True)
                        for j in range(CH):
                            ins = pe.matmul(K.ps[:, bass.ds(at[j] * P, MW)], hot[k][:, j, :], msg[k][:, j, :],
                                            start=False, stop=False, skip_group_check=True)
                        ins.then_inc(chunk_free, 1)
                    pipeline(pe, [(0, spread_out), (2, add_up)], blocks=blocks)

        def message(v, out, c, h0):
            for i in range(HP):
                ins = v.scalar_tensor_tensor(
                    out=out[:, :, i * F:(i + 1) * F],
                    in0=weight[:, bass.ds(c * CH, CH), h0 + i:h0 + i + 1].broadcast_to([P, CH, F]), scalar=1.0,
                    in1=kept[:, bass.ds(c * CH, CH), 0:F], op0=ALU.min, op1=ALU.mult)
            return ins

        def with_self_loop(v, link, h0):
            zz = z[:, :, h0:h0 + HP, :]
            full = [P, NB, HP, F]
            link(v.tensor_tensor(zz, x.unsqueeze(2).broadcast_to(full),
                                 selfw[:, :, h0:h0 + HP].unsqueeze(3).broadcast_to(full), ALU.mult))
            sums_of = K.ps[:, 0:NB * P].rearrange("p (b c) -> p b c", c=P)[:, :, 0:HP * F]
            link(v.tensor_tensor(zz, zz, sums_of.rearrange("p b (h c) -> p b h c", c=F), ALU.add))

        def divide(v, link, den):
            link(v.tensor_tensor(t0[:, :, :], den, selfw[:, :, :], ALU.add))
            link(v.tensor_scalar(t0[:, :, :], t0[:, :, :], 1.0e-16, None, ALU.add))
            link(v.reciprocal(t0[:, :, :], t0[:, :, :]))
            link(v.tensor_tensor(z[:, :, :, :], z[:, :, :, :], t0[:, :, :].unsqueeze(3).broadcast_to([P, NB, H, F]),
                                 ALU.mult))

        def sum_second_pair():
            c = ExitStack()
            with c:
                def sem(name):
                    return c.enter_context(semaphore(nc, f"{tag}_{name}"))

                parts = c.enter_context(nc.sbuf_tensor(f"{tag}_parts", [P, SLOTS, 3, H], BF16))
                hotb = [c.enter_context(nc.sbuf_tensor(f"{tag}_hotb{k}", [P, CH, P], BF16)) for k in range(2)]
                here = [c.enter_context(nc.sbuf_tensor(f"{tag}_here{k}", [P, CH, 3 * H], BF16)) for k in range(2)]
                msg = [c.enter_context(nc.sbuf_tensor(f"{tag}_msgb{k}", [P, CH, HP * F], FP32)) for k in range(2)]
                msg_ready, hotb_ready, chunk_free, steps = (sem(n) for n in ("msgb_ready", "hotb_ready", "msgb_free", "normb"))
                block = c.enter_context(nc.Block())

                @block.vector
                def _(v):
                    link = Link(v, steps)
                    with nc.sbuf_tensor(f"{tag}_rest", [P, SLOTS, H], FP32) as rest:
                        link(v.tensor_scalar(rest[:, :, :], weight[:, :, :], 1.0, None, ALU.min))
                        split3(v, link, [parts[:, :, q, :] for q in range(3)], rest[:, :, :])

                    def targets(c, k, turn):
                        v.wait_ge(chunk_free, c + 1)
                        onehot(v, hot[k][:, :, :], K.iota_row[:, :], K.dl[:, bass.ds(c * CH, CH)]).then_inc(msg_ready, 1)
                        message(v, msg[k][:, :, :], c, 2).then_inc(msg_ready, 1)
                    pipeline(v, [(0, targets)])
                    v.wait_ge(chunk_free, 2 + CHUNKS)
                    with_self_loop(v, link, 2)
                    link(v.tensor_reduce(t1[:, :, :], K.ps[:, 7 * BANK:7 * BANK + NB * 3 * H].rearrange(
                        "p (b q h) -> p b h q", q=3, h=H), AX.X, ALU.add))
                    divide(v, link, t1[:, :, :])

                @block.scalar
                def _(act):
                    def short(c, k, turn):
                        act.wait_ge(msg_ready, c * 2 + 1)
                        act.copy(hotb[k][:, :, :], hot[k][:, :, :])
                        act.copy(here[k][:, :, :], parts[:, bass.ds(c * CH, CH), :, :].rearrange("p s q h -> p s (q h)")
                                 ).then_inc(hotb_ready, 1)
                    pipeline(act, [(0, short)])

                @block.tensor
                def _(pe):
                    clear_banks(pe, K, 0, 8).then_inc(chunk_free, 2)
                    blocks = SlotBlocks(nc, K, pe)

                    def add_up(c, k, turn):
                        at = blocks.now()
                        pe.wait_ge(msg_ready, c * 2 + 2)
                        pe.wait_ge(hotb_ready, c + 1)
                        pe.nop(nofuse=True)
                        for j in range(CH):
                            pe.matmul(K.ps[:, bass.ds(at[j] * (3 * H) + 7 * BANK, 3 * H)], hotb[k][:, j, :],
                                      here[k][:, j, :], start=False, stop=False, skip_group_check=True)
                        for j in range(CH):
                            ins = pe.matmul(K.ps[:, bass.ds(at[j] * P, P)], hot[k][:, j, :], msg[k][:, j, :],
                                            start=False, stop=False, skip_group_check=True)
                        ins.then_inc(chunk_free, 1)
                    pipeline(pe, [(0, add_up)], blocks=blocks)

        gather_and_max()
        node_maxima()
        weigh_and_sum()
        if H > HP:
            sum_second_pair()


def bcast_chunk(rows, parts):
    return rows.rearrange("(o s) e -> o (s e)", o=1).broadcast_to([parts, CW])


def residual_norm(nc, K, add, tag):
    ctx = ExitStack()
    with ctx:
        y = ctx.enter_context(nc.sbuf_tensor(f"{tag}_y", [P, NB, F], FP32))
        sq = ctx.enter_context(nc.sbuf_tensor(f"{tag}_sq", [P, NB, F], FP32))
        mean = ctx.enter_context(nc.sbuf_tensor(f"{tag}_mean", [P, NB], FP32))
        var = ctx.enter_context(nc.sbuf_tensor(f"{tag}_var", [P, NB], FP32))
        steps = ctx.enter_context(semaphore(nc, f"{tag}_rn"))
        wanted = ctx.enter_context(semaphore(nc, f"{tag}_rnw"))
        ready = ctx.enter_context(semaphore(nc, f"{tag}_rnr"))
        block = ctx.enter_context(nc.Block())

        @block.vector
        def _(v):
            link = Link(v, steps)
            add(v, link, y)
            link(v.tensor_tensor(y[:, :, :], y[:, :, :], K.x[:, :, :], ALU.add))
            layernorm_steps(v, link, K, y[:, :, :], K.x[:, :, :], sq[:, :, :], mean[:, :], var[:, :], wanted, ready)

        @block.scalar
        def _(act):
            act.wait_ge(wanted, 1)
            act.activation(var[:, :], var[:, :], ACT.Sqrt).then_inc(ready, 1)


def gat(nc, K, A):
    H = HEADS
    ctx = ExitStack()
    with ctx:
        def sb(name, shape, dt=FP32):
            return ctx.enter_context(nc.sbuf_tensor(name, shape, dt))

        w1 = sb("w1", [F, H, F])
        w2a = sb("w2a", [F, H, F + 2])
        b1 = sb("b1c", [F, H])
        b2 = sb("b2r", [P, F])
        va = sb("va", [F, 2 * H])
        h2 = sb("h2", [P, NB, F + 2])
        prep = ExitStack()
        with prep:
            rows = prep.enter_context(nc.sbuf_tensor("att_rows", [F, 2, H, F], FP32))
            rows2 = prep.enter_context(nc.sbuf_tensor("att_rows2", [F, 2, F], FP32))
            prod = prep.enter_context(nc.sbuf_tensor("att_prod", [F, H, F], FP32))
            loaded = prep.enter_context(semaphore(nc, "gat_loaded"))
            steps = prep.enter_context(semaphore(nc, "gat_steps"))
            block = prep.enter_context(nc.Block())

            @block.sync
            def _(sp):
                sp.dma_start(w1[:, :, :], A["L1_gnn_W1"].rearrange("k (h o) -> k h o", h=H)).then_inc(loaded, 16)
                sp.dma_start(w2a[:, :, 0:F], A["L1_gnn_W2"].rearrange("(h k) o -> k h o", h=H)).then_inc(loaded, 16)
                with nc.allow_non_contiguous_dma(reason="a column of 256 biases"):
                    sp.dma_start(b1[:, :], A["L1_gnn_b1"].rearrange("(h k) -> k h", h=H)).then_inc(loaded, 16)
                sp.dma_start(b2[:, :], bcast_rows(A["L1_gnn_b2"], P)).then_inc(loaded, 16)
                for i, n in enumerate(("L1_gnn_a_src1", "L1_gnn_a_dst1")):
                    sp.dma_start(rows[:, i, :, :].rearrange("p h o -> p (h o)"),
                                 bcast_rows(A[n].rearrange("h o -> (h o)"), F)).then_inc(loaded, 16)
                for i, n in enumerate(("L1_gnn_a_src2", "L1_gnn_a_dst2")):
                    sp.dma_start(rows2[:, i, :], bcast_rows(A[n].rearrange("h o -> (h o)"), F)).then_inc(loaded, 16)

            @block.vector
            def _(v):
                link = Link(v, steps)
                v.wait_ge(loaded, 16 * 8)
                for i in range(2):
                    link(v.tensor_tensor(prod[:, :, :], w1[:, :, :], rows[:, i, :, :], ALU.mult))
                    link(v.tensor_reduce(va[:, i * H:(i + 1) * H], prod[:, :, :], AX.X, ALU.add))
                    link(v.tensor_tensor(prod[:, :, :], w2a[:, :, 0:F],
                                         rows2[:, i, :].unsqueeze(1).broadcast_to([F, H, F]), ALU.mult))
                    link(v.tensor_reduce(w2a[:, :, F + i], prod[:, :, :], AX.X, ALU.add))

        first = ExitStack()
        with first:
            al = first.enter_context(nc.sbuf_tensor("al1", [P, NB, 2 * H], FP32))
            z = first.enter_context(nc.sbuf_tensor("z1", [P, NB, H, F], FP32))
            with nc.sbuf_tensor("xT1", [F, NB * P], FP32) as xT:
                transpose_nodes(nc, K, K.x, xT, "g1t")
                project(nc, K, xT, va[:, :], 2 * H, al, "g1p")
            store_table(nc, K, K.tab_gat1, [(0, F, K.x[:, :, :]), (F, H, al[:, :, 0:H])], "g1s")
            attention(nc, K, H, K.tab_gat1, K.x[:, :, :], al[:, :, 0:H], al[:, :, H:2 * H], z, "g1")
            dense_heads(nc, K, z, w1, b1, w2a, h2)
        store_table(nc, K, K.tab_gat2, [(0, F + 1, h2[:, :, 0:F + 1])], "g2s")
        z2 = sb("z2", [P, NB, 1, F])
        attention(nc, K, 1, K.tab_gat2, h2[:, :, 0:F], h2[:, :, F:F + 1], h2[:, :, F + 1:F + 2], z2, "g2")

        def add(v, link, y):
            link(v.tensor_tensor(y[:, :, :], z2[:, :, 0, :], per_feature(b2[:, :]), ALU.add))
        residual_norm(nc, K, add, "g")


def dense_heads(nc, K, z, w1, b1, w2a, h2):
    H, C = HEADS, F + 2
    ctx = ExitStack()
    with ctx:
        def sem(name):
            return ctx.enter_context(semaphore(nc, name))

        def pair(name, shape):
            return [ctx.enter_context(nc.sbuf_tensor(f"{name}{k}", shape, FP32)) for k in range(2)]

        zb, zt, ht = pair("zb", [P, H, F]), pair("zt", [F, H, P]), pair("ht", [F, H, P])
        staged, turned, zt_ready, hidden, ht_ready, made, copied = (sem(n) for n in (
            "d_staged", "d_turned", "d_zt_ready", "d_hidden", "d_ht_ready", "d_made", "d_copied"))
        block = ctx.enter_context(nc.Block())


        @block.scalar
        def _(act):
            act.sem_inc(ht_ready, 2)

            def stage(b, k, turn):
                act.wait_ge(turned, b + 1)
                at = slice(b, b + 1) if isinstance(b, int) else bass.ds(b, 1)
                act.copy(zb[k][:, :, :], z[:, at, :, :].rearrange("p b h c -> p (b h) c")).then_inc(staged, 1)

            def rectify(b, k, turn):
                act.wait_ge(hidden, b + 3)
                act.wait_ge(made, b + 1)
                for h in range(H):
                    o = (2 + k) * BANK + h * P
                    ins = act.activation(ht[k][:, h, :], K.ps[0:F, o:o + P], ACT.Relu, bias=b1[:, h:h + 1])
                ins.then_inc(ht_ready, 1)
            pipeline(act, [(0, stage), (1, rectify)], chunks=NB)

        @block.vector
        def _(v):
            v.sem_inc(zt_ready, 2)
            v.sem_inc(copied, 2)

            def keep_turned(b, k, turn):
                v.wait_ge(turned, b + 3)
                v.wait_ge(hidden, b + 1)
                v.tensor_copy(zt[k][:, :, :], K.ps[0:F, k * BANK:(k + 1) * BANK].rearrange("p (h e) -> p h e", h=H)
                              ).then_inc(zt_ready, 1)

            def keep_made(b, k, turn):
                v.wait_ge(made, b + 3)
                at = slice(b, b + 1) if isinstance(b, int) else bass.ds(b, 1)
                v.tensor_copy(h2[:, at, :].rearrange("p b c -> p (b c)"), K.ps[:, (4 + k) * BANK:(4 + k) * BANK + C]
                              ).then_inc(copied, 1)
            pipeline(v, [(0, keep_turned), (2, keep_made)], chunks=NB)

        @block.tensor
        def _(pe):
            for s in (turned, hidden, made):
                pe.sem_inc(s, 2)

            def turn_heads(b, k, turn):
                pe.wait_ge(staged, b + 1)
                pe.wait_ge(zt_ready, b + 1)
                pe.nop(nofuse=True)
                for h in range(H):
                    o = k * BANK + h * P
                    ins = pe.transpose(K.ps[0:F, o:o + P], zb[k][:, h, :], K.ident[:, :])
                ins.then_inc(turned, 1)

            def first_weights(b, k, turn):
                pe.wait_ge(zt_ready, b + 3)
                pe.wait_ge(ht_ready, b + 1)
                pe.nop(nofuse=True)
                for h in range(H):
                    o = (2 + k) * BANK + h * P
                    ins = pe.matmul(K.ps[0:F, o:o + P], w1[:, h, :], zt[k][:, h, :], start=True, stop=True,
                                    skip_group_check=True)
                ins.then_inc(hidden, 1)

            def second_weights(b, k, turn):
                pe.wait_ge(ht_ready, b + 3)
                pe.wait_ge(copied, b + 1)
                pe.nop(nofuse=True)
                for h in range(H):
                    ins = pe.matmul(K.ps[:, (4 + k) * BANK:(4 + k) * BANK + C], ht[k][:, h, :], w2a[:, h, :],
                                    start=h == 0, stop=h == H - 1)
                ins.then_inc(made, 1)
            pipeline(pe, [(0, turn_heads), (1, first_weights), (2, second_weights)], chunks=NB)


def relational(nc, K, A):
    ctx = ExitStack()
    with ctx:
        def sb(name, shape, dt=FP32):
            return ctx.enter_context(nc.sbuf_tensor(name, shape, dt))

        rel = sb("rel", [F, REL, F])
        wself = sb("wself", [F, F])
        bias = sb("rel_bias", [P, F])
        own = sb("rel_own", [P, NB, F])
        xT = sb("xT2", [F, NB * P])
        prep = ExitStack()
        with prep:
            basis = prep.enter_context(nc.sbuf_tensor("basis", [NBASE, F, F], FP32))
            coeff = prep.enter_context(nc.sbuf_tensor("coeff", [REL, NBASE], FP32))
            coefT = prep.enter_context(nc.sbuf_tensor("coefT", [NBASE, REL], FP32))
            loaded = prep.enter_context(semaphore(nc, "rel_loaded"))
            turned = prep.enter_context(semaphore(nc, "rel_turned"))
            ready = prep.enter_context(semaphore(nc, "rel_coef"))
            made = prep.enter_context(semaphore(nc, "rel_made"))
            block = prep.enter_context(nc.Block())

            @block.sync
            def _(sp):
                sp.dma_start(basis[:, :, :], A["L2_gnn_basis"]).then_inc(loaded, 16)
                sp.dma_start(coeff[:, :], A["L2_gnn_coeff"]).then_inc(loaded, 16)
                sp.dma_start(wself[:, :], A["L2_gnn_self_weight"]).then_inc(loaded, 16)
                sp.dma_start(bias[:, :], bcast_rows(A["L2_gnn_bias"], P)).then_inc(loaded, 16)

            @block.tensor
            def _(pe):
                pe.wait_ge(loaded, 64)
                pe.transpose(K.ps[0:NBASE, 7 * BANK:7 * BANK + REL], coeff[:, :], K.ident[0:REL, 0:REL]).then_inc(turned, 1)
                pe.wait_ge(ready, 1)
                for o in range(F):
                    ins = pe.matmul(K.ps[0:F, o * REL:(o + 1) * REL], basis[:, :, o], coefT[:, :], start=True, stop=True,
                                    skip_group_check=True)
                ins.then_inc(made, 1)

            @block.vector
            def _(v):
                v.wait_ge(turned, 1)
                v.tensor_copy(coefT[:, :], K.ps[0:NBASE, 7 * BANK:7 * BANK + REL]).then_inc(ready, 1)
                v.wait_ge(made, 1)
                v.tensor_copy(rel[:, :, :], K.ps[0:F, 0:F * REL].rearrange("p (o r) -> p r o", r=REL)).then_inc(ready, 1)
                v.wait_ge(ready, 2)
        transpose_nodes(nc, K, K.x, xT, "r1t")
        project(nc, K, xT, wself[:, :], F, own, "r1p")
        reciprocal_roots(nc, K, K.sq_var[:, :], "v2")
        relation_table(nc, K, rel, xT)
        with ExitStack() as c:
            gather_sum(nc, K, K.tab_rel.rearrange("n (r o) -> (n r) o", r=REL), K.rel_idx, "relg", FinishEncoding(nc, K, c))

        def add(v, link, y):
            link(v.tensor_tensor(y[:, :, :], sums(K), per_node(K.rdeg[:, :]), ALU.mult))
            link(v.tensor_tensor(y[:, :, :], y[:, :, :], own[:, :, :], ALU.add))
            link(v.tensor_tensor(y[:, :, :], y[:, :, :], per_feature(bias[:, :]), ALU.add))
        residual_norm(nc, K, add, "r")


def relation_table(nc, K, rel, xT):
    ctx = ExitStack()
    with ctx:
        W = REL * F
        Q = W // BANK
        y = [ctx.enter_context(nc.sbuf_tensor(f"ytab{k}", [P, W], FP32)) for k in range(2)]
        xb = [ctx.enter_context(nc.sbuf_tensor(f"xtb{k}", [F, P], FP32)) for k in range(2)]
        staged, made, copied_v, copied_a = (ctx.enter_context(semaphore(nc, n)) for n in (
            "y_staged", "y_made", "y_copied_v", "y_copied_a"))
        stored = [ctx.enter_context(semaphore(nc, f"y_stored{k}")) for k in range(2)]
        block = ctx.enter_context(nc.Block())
        flat = rel[:, :, :].rearrange("p r o -> p (r o)")
        rows = node_rows(K.tab_rel)

        @block.tensor
        def _(pe):
            def one(b, k):
                pe.wait_ge(staged, b + 1)
                pe.wait_ge(copied_v, b * (Q // 2) + Q // 2)
                pe.wait_ge(copied_a, b * (Q // 2) + Q // 2)
                pe.nop(nofuse=True)
                for q in range(Q):
                    pe.matmul(K.ps[:, (4 * k + q) * BANK:(4 * k + q + 1) * BANK], xb[k][:, :],
                              flat[:, q * BANK:(q + 1) * BANK], start=True, stop=True).then_inc(made, 1)
            with pe.Fori(0, NB // 2) as it:
                for k in range(2):
                    one(it * 2 + k, k)
            one(NB - 1, 0)

        @block.scalar
        def _(act):
            def half(b, k, n):
                act.wait_ge(stored[k], n)
                for q in range(Q // 2, Q):
                    act.wait_ge(made, b * Q + q + 1)
                    act.copy(y[k][:, q * BANK:(q + 1) * BANK], K.ps[:, (4 * k + q) * BANK:(4 * k + q + 1) * BANK]
                             ).then_inc(copied_a, 1)
            act.sem_inc(copied_a, Q)
            with act.Fori(0, NB // 2) as it:
                for k in range(2):
                    half(it * 2 + k, k, it * 16 + 16)
            half(NB - 1, 0, (NB // 2) * 16 + 16)

        @block.vector
        def _(v):
            def half(b, k, n):
                v.wait_ge(copied_a, b * (Q // 2) + Q // 2)
                v.tensor_copy(xb[k][:, :], xT[:, bass.ds(b * P, P)] if not isinstance(b, int)
                              else xT[:, b * P:(b + 1) * P]).then_inc(staged, 1)
                v.wait_ge(stored[k], n)
                for q in range(Q // 2):
                    v.wait_ge(made, b * Q + q + 1)
                    v.tensor_copy(y[k][:, q * BANK:(q + 1) * BANK], K.ps[:, (4 * k + q) * BANK:(4 * k + q + 1) * BANK]
                                  ).then_inc(copied_v, 1)
            v.sem_inc(copied_v, Q)
            with v.Fori(0, NB // 2) as it:
                for k in range(2):
                    half(it * 2 + k, k, it * 16 + 16)
            half(NB - 1, 0, (NB // 2) * 16 + 16)

        @block.sync
        def _(sp):
            def one(b, k):
                sp.wait_ge(copied_v, b * (Q // 2) + Q + Q // 2)
                sp.wait_ge(copied_a, b * (Q // 2) + Q + Q // 2)
                out = rows[:, bass.ds(b, 1), :] if not isinstance(b, int) else rows[:, b:b + 1, :]
                sp.dma_start(out, y[k][:, :].unsqueeze(1)).then_inc(stored[k], 16)
            sp.sem_inc(stored[0], 16)
            sp.sem_inc(stored[1], 16)
            with sp.Fori(0, NB // 2) as it:
                for k in range(2):
                    one(it * 2 + k, k)
            one(NB - 1, 0)
            sp.wait_ge(stored[0], 16 + 16 * (NB // 2 + 1))
            sp.wait_ge(stored[1], 16 + 16 * (NB // 2))


def reciprocal_roots(nc, K, var, tag, rows=False):
    ctx = ExitStack()
    with ctx:
        rr = ctx.enter_context(nc.sbuf_tensor(f"{tag}_rr", [P, 4, P], FP32))
        steps, wanted, ready, turned, stored = (ctx.enter_context(semaphore(nc, f"{tag}_{n}")) for n in (
            "steps", "wanted", "ready", "turned", "stored"))
        block = ctx.enter_context(nc.Block())

        @block.vector
        def _(v):
            link = Link(v, steps)
            link(v.tensor_scalar(var, var, 1.0 / F, EPS, ALU.mult, ALU.add))
            v.sem_inc(wanted, 1)
            v.wait_ge(ready, 1)
            link(v.reciprocal(var, var))
            if rows:
                v.wait_ge(turned, 1)
                link(v.tensor_copy(rr[0:SG, :, :], K.ps[0:SG, 0:4 * P].rearrange("p (g e) -> p g e", g=4)))

        @block.scalar
        def _(act):
            act.wait_ge(wanted, 1)
            act.activation(var, var, ACT.Sqrt).then_inc(ready, 1)

        if rows:
            @block.tensor
            def _(pe):
                pe.wait_ge(steps, 2)
                for g in range(4):
                    ins = pe.transpose(K.ps[0:SG, g * P:(g + 1) * P], var[:, g * SG:(g + 1) * SG], K.ident[:, :])
                ins.then_inc(turned, 1)

            @block.sync
            def _(sp):
                sp.wait_ge(steps, 3)
                sp.dma_start(K.rstd_rows.rearrange("(g s) e -> s g e", g=4), rr[0:SG, :, :]).then_inc(stored, 16)
                sp.wait_ge(stored, 16)


class EdgeWeights:

    def __init__(self, nc, K, A, ctx):
        def sb(name, shape, dt=FP32):
            return ctx.enter_context(nc.sbuf_tensor(name, shape, dt))

        wd1 = self.wd1 = sb("wd1", [4, F])
        wd2 = self.wd2 = sb("wd2", [F + 1, F])
        mean = sb("wmean", [F + 1, 2])
        gb = self.gb = sb("gb1", [F, 2])
        self.var = K.sq_var
        at = self.at = [sb(f"at{k}", [4, CW]) for k in range(2)]
        with semaphore(nc, "w_loaded") as loaded, semaphore(nc, "w_steps") as steps, nc.Block() as block:
            @block.sync
            def _(sp):
                sp.dma_start(wd1[0:3, :], A["L3_gnn_Wd1"]).then_inc(loaded, 16)
                sp.dma_start(wd1[3:4, :], bcast_rows(A["L3_gnn_bd1"], 1)).then_inc(loaded, 16)
                sp.dma_start(wd2[0:F, :], A["L3_gnn_Wd2"]).then_inc(loaded, 16)
                sp.dma_start(wd2[F:F + 1, :], bcast_rows(A["L3_gnn_bd2"], 1)).then_inc(loaded, 16)
                with nc.allow_non_contiguous_dma(reason="columns of 64"):
                    for i, n in enumerate(("L3_gnn_g1", "L3_gnn_b1")):
                        sp.dma_start(gb[:, i:i + 1], A[n].rearrange("(c o) -> c o", o=1)).then_inc(loaded, 16)
                for i, n in enumerate(("L3_gnn_g2", "L3_gnn_b2")):
                    sp.dma_start(K.gb2[:, i, :], bcast_rows(A[n], P)).then_inc(loaded, 16)

            @block.vector
            def _(v):
                link = Link(v, steps)
                for k in range(2):
                    link(v.memset(at[k][:, :], 1.0))
                v.wait_ge(loaded, 16 * 8)
                for i, (w, n) in enumerate(((wd1, 4), (wd2, F + 1))):
                    link(v.tensor_reduce(mean[0:n, i:i + 1], w[:, :], AX.X, ALU.add))
                    link(v.tensor_scalar(mean[0:n, i:i + 1], mean[0:n, i:i + 1], -1.0 / F, None, ALU.mult))
                    link(v.tensor_scalar(w[:, :], w[:, :], mean[0:n, i:i + 1], None, ALU.add))


def attr_chunk(K, c):
    return K.attr_rows[:, bass.ds(c * CH, CH), :].rearrange("a s e -> a (s e)")


class FirstVariance:

    def __init__(self, nc, K, ctx, enc):
        def sem(name):
            return ctx.enter_context(semaphore(nc, name))

        self.K, self.enc = K, enc
        self.sq = [ctx.enter_context(nc.sbuf_tensor(f"esq{k}", [P, CH, F], FP32)) for k in range(2)]
        self.at_in = [sem(f"e_at_in{k}") for k in range(2)]
        self.made, self.squared, self.summed = sem("e_made"), sem("e_squared"), sem("e_summed")

    def sync(self, sp):
        def load(c, k, turn):
            sp.wait_ge(self.made, c + 1)
            sp.dma_start(self.enc.at[k][0:3, :], attr_chunk(self.K, c)).then_inc(self.at_in[k], 16)
        return [(0, load)]

    def finish(self, sp):
        pass

    def tensor(self, pe):
        pe.sem_inc(self.made, 2)

        def product(c, k, turn):
            pe.wait_ge(self.at_in[k], turn * 16 + 16)
            pe.wait_ge(self.squared, c + 1)
            pe.nop(nofuse=True)
            for j in range(CH):
                o = (4 + k) * BANK + j * F
                ins = pe.matmul(self.K.ps[:, o:o + F], self.enc.at[k][:, j * P:(j + 1) * P], self.enc.wd1[:, :],
                                start=True, stop=True, skip_group_check=True)
            ins.then_inc(self.made, 1)
        return [(0, product)]

    def scalar(self, act):
        act.sem_inc(self.squared, 2)

        def square(c, k, turn):
            act.wait_ge(self.made, c + 3)
            act.wait_ge(self.summed, c + 1)
            act.activation(self.sq[k][:, :, :], self.K.ps[:, (4 + k) * BANK:(4 + k) * BANK + CH * F].rearrange(
                "p (s c) -> p s c", c=F), ACT.Square).then_inc(self.squared, 1)
        return [(0, square)]

    def vector(self, v):
        v.sem_inc(self.summed, 2)

        def total(c, k, turn):
            v.wait_ge(self.squared, c + 3)
            v.tensor_reduce(self.enc.var[:, bass.ds(c * CH, CH)], self.sq[k][:, :, :], AX.X, ALU.add).then_inc(self.summed, 1)
        return [(1, total)]


def enc_chunk(K, c):
    return K.enc[:, bass.ds(c * (CH * F), CH * F)].rearrange("p (s c) -> p s c", c=F)


class SecondProduct:

    def __init__(self, nc, K, ctx, enc):
        def tiles(name, shape, count=2):
            return [ctx.enter_context(nc.sbuf_tensor(f"{name}{k}", shape, FP32)) for k in range(count)]

        def sem(name):
            return ctx.enter_context(semaphore(nc, name))

        self.K, self.enc = K, enc
        self.ats, self.rs = tiles("ats", [4, CW]), tiles("ers", [4, CW])
        self.d1 = tiles("ed1", [F + 1, CW])
        self.sq, self.hh = tiles("ehs", [P, CH, F]), tiles("ehh", [P, CH, F], 4)
        self.at_in = [sem(f"m_in{k}") for k in range(2)]
        self.stored = [sem(f"m_stored{k}") for k in range(4)]
        self.scaled, self.first, self.ones_set, self.gelued, self.second, self.moved, self.squared, self.summed = (
            sem(f"m_{n}") for n in ("scaled", "first", "ones_set", "gelued", "second", "moved", "squared", "summed"))

    def sync(self, sp):
        K = self.K
        for k in range(4):
            sp.sem_inc(self.stored[k], 16)

        def load(c, k, turn):
            sp.wait_ge(self.scaled, c + 1)
            sp.dma_start(self.enc.at[k][0:3, :], attr_chunk(K, c)).then_inc(self.at_in[k], 16)
            sp.dma_start(self.rs[k][:, :], bcast_chunk(K.rstd_rows[bass.ds(c * CH, CH), :], 4)).then_inc(self.at_in[k], 16)

        def store(c, k, turn):
            sp.wait_ge(self.moved, c + 1)
            sp.dma_start(enc_chunk(K, c), self.hh[k][:, :, :]).then_inc(self.stored[k], 16)
        return [(0, load), (3, store, 4)]

    def finish(self, sp):
        for k in range(4):
            sp.wait_ge(self.stored[k], 16 + 16 * (CHUNKS // 4))

    def vector(self, v):
        for k in range(2):
            v.memset(self.d1[k][:, :], 1.0).then_inc(self.ones_set, 1)
        v.sem_inc(self.scaled, 2)
        v.sem_inc(self.summed, 2)

        def scale(c, k, turn):
            v.wait_ge(self.at_in[k], turn * 32 + 32)
            v.wait_ge(self.first, c + 1)
            v.tensor_tensor(self.ats[k][:, :], self.enc.at[k][:, :], self.rs[k][:, :], ALU.mult).then_inc(self.scaled, 1)

        def total(c, k, turn):
            v.wait_ge(self.squared, c + 3)
            v.tensor_reduce(self.enc.var[:, bass.ds(c * CH, CH)], self.sq[k][:, :, :], AX.X, ALU.add).then_inc(self.summed, 1)
        return [(0, scale), (3, total)]

    def scalar(self, act):
        K, gb = self.K, self.enc.gb
        act.sem_inc(self.gelued, 2)
        act.sem_inc(self.squared, 2)
        act.wait_ge(self.ones_set, 2)

        def gelu(c, k, turn):
            act.wait_ge(self.first, c + 3)
            act.wait_ge(self.second, c + 1)
            act.activation(self.d1[k][0:F, :], K.ps[0:F, (4 + k) * BANK:(5 + k) * BANK], ACT.Gelu, bias=gb[:, 1:2],
                           scale=gb[:, 0:1]).then_inc(self.gelued, 1)

        def move(c, k, turn):
            act.wait_ge(self.second, c + 3)
            act.wait_ge(self.stored[k], turn * 16 + 16)
            made = K.ps[:, (6 + k % 2) * BANK:(6 + k % 2) * BANK + CH * F].rearrange("p (s c) -> p s c", c=F)
            act.copy(self.hh[k][:, :, :], made).then_inc(self.moved, 1)
            act.wait_ge(self.summed, c + 1)
            act.activation(self.sq[k % 2][:, :, :], made, ACT.Square).then_inc(self.squared, 1)
        return [(0, gelu), (1, move, 4)]

    def tensor(self, pe):
        K, enc = self.K, self.enc
        pe.sem_inc(self.first, 2)
        pe.sem_inc(self.second, 2)

        def first(c, k, turn):
            pe.wait_ge(self.scaled, c + 3)
            pe.wait_ge(self.gelued, c + 1)
            pe.nop(nofuse=True)
            pe.matmul(K.ps[0:F, (4 + k) * BANK:(5 + k) * BANK], enc.wd1[:, :], self.ats[k][:, :], start=True, stop=True
                      ).then_inc(self.first, 1)

        def second(c, k, turn):
            pe.wait_ge(self.gelued, c + 3)
            pe.wait_ge(self.squared, c + 1)
            pe.nop(nofuse=True)
            for j in range(CH):
                o = (6 + k) * BANK + j * F
                ins = pe.matmul(K.ps[:, o:o + F], self.d1[k][:, j * P:(j + 1) * P], enc.wd2[:, :], start=True, stop=True,
                                skip_group_check=True)
            ins.then_inc(self.second, 1)
        return [(0, first), (1, second)]


class FinishEncoding:

    def __init__(self, nc, K, ctx):
        def pair(name):
            return [ctx.enter_context(nc.sbuf_tensor(f"{name}{k}", [P, CH, F], FP32)) for k in range(2)]

        def sem(name):
            return ctx.enter_context(semaphore(nc, name))

        self.K = K
        self.hin, self.prod, self.dd = (pair(n) for n in ("fh", "fp", "fd"))
        self.h_in = [sem(f"f_in{k}") for k in range(2)]
        self.stored = [sem(f"f_stored{k}") for k in range(2)]
        self.steps, self.scaled, self.gelued = sem("f_steps"), sem("f_scaled"), sem("f_gelued")

    def sync(self, sp):
        K = self.K
        for k in range(2):
            sp.sem_inc(self.stored[k], 16)

        def load(c, k, turn):
            sp.wait_ge(self.scaled, c + 1)
            sp.dma_start(self.hin[k][:, :, :], enc_chunk(K, c)).then_inc(self.h_in[k], 16)

        def store(c, k, turn):
            sp.wait_ge(self.gelued, c + 3)
            sp.dma_start(enc_chunk(K, c), self.dd[k][:, :, :]).then_inc(self.stored[k], 16)
        return [(0, load), (2, store)]

    def finish(self, sp):
        for k in range(2):
            sp.wait_ge(self.stored[k], 16 + 16 * ITERS)

    def vector(self, v):
        K = self.K
        v.sem_inc(self.scaled, 2)
        link = Link(v, self.steps, 2)
        full = [P, CH, F]

        def scale(c, k, turn):
            link.turn(c)
            v.wait_ge(self.h_in[k], turn * 16 + 16)
            v.wait_ge(self.gelued, c + 1)
            prod = self.prod[k][:, :, :]
            link(v.tensor_tensor(prod, self.hin[k][:, :, :], K.sq_var[:, bass.ds(c * CH, CH)].unsqueeze(2).broadcast_to(full),
                                 ALU.mult))
            link(v.tensor_tensor(prod, prod, K.gb2[:, 0:1, :].broadcast_to(full), ALU.mult))
            v.tensor_tensor(prod, prod, K.gb2[:, 1:2, :].broadcast_to(full), ALU.add).then_inc(self.scaled, 1)
        return [(0, scale)]

    def scalar(self, act):
        act.sem_inc(self.gelued, 2)

        def gelu(c, k, turn):
            act.wait_ge(self.scaled, c + 3)
            act.wait_ge(self.stored[k], turn * 16 + 16)
            act.activation(self.dd[k][:, :, :], self.prod[k][:, :, :], ACT.Gelu).then_inc(self.gelued, 1)
        return [(0, gelu)]

    def tensor(self, pe):
        return []


def vector_attention(nc, K, A):
    ctx = ExitStack()
    with ctx:
        def sb(name, shape, dt=FP32):
            return ctx.enter_context(nc.sbuf_tensor(name, shape, dt))

        proj = sb("proj", [P, NB, 3, F])
        with nc.sbuf_tensor("wv", [F, 3, F], FP32) as wv, nc.sbuf_tensor("xT3", [F, NB * P], FP32) as xT:
            with semaphore(nc, "wv_in") as wv_in, semaphore(nc, "wv_neg") as wv_neg, nc.Block() as block:
                @block.sync
                def _(sp):
                    for i, n in enumerate(("L3_gnn_W2", "L3_gnn_W3", "L3_gnn_W1")):
                        sp.dma_start(wv[:, i, :], A[n]).then_inc(wv_in, 16)

                @block.vector
                def _(v):
                    v.wait_ge(wv_in, 48)
                    v.tensor_scalar(wv[:, 0, :], wv[:, 0, :], -1.0, None, ALU.mult).then_inc(wv_neg, 1)
                    v.wait_ge(wv_neg, 1)
            transpose_nodes(nc, K, K.x, xT, "v1t")
            project(nc, K, xT, wv[:, :, :].rearrange("p i o -> p (i o)"), 3 * F,
                    proj[:, :, :, :].rearrange("p b i o -> p b (i o)"), "v1p")
        store_table(nc, K, K.tab_vec, [(0, 2 * F, proj[:, :, 0:2, :].rearrange("p b i o -> p b (i o)"))], "v1s")
        scan_edges(nc, K, proj)

        def add(v, link, y):
            link(v.tensor_copy(y[:, :, :], sums(K)))
        residual_norm(nc, K, add, "vec")


def scan_edges(nc, K, proj):
    ctx = ExitStack()
    with ctx:
        def pair(name, shape, dt=FP32):
            return [ctx.enter_context(nc.sbuf_tensor(f"s_{name}{k}", shape, dt)) for k in range(2)]

        def sem(name):
            return ctx.enter_context(semaphore(nc, f"s_{name}"))

        ring = [ctx.enter_context(nc.sbuf_tensor(f"s_ring{k}", [P, CH, 2 * F], FP32)) for k in range(4)]
        idx = [ctx.enter_context(nc.sbuf_tensor(f"s_idx{k}", [P, CH], I32)) for k in range(4)]
        dlb, pen, enc = ([ctx.enter_context(nc.sbuf_tensor(f"s_{name}{k}", [parts, CW if name != "enc" else CH * F], FP32)) for k in range(4)]
                         for name, parts in (("dlb", P), ("pen", F), ("enc", P)))
        cold, hot = pair("cold", [P, CW]), pair("hot", [P, CH, P])
        w1 = pair("w1", [P, CH, F])
        mrun = pair("mrun", [F, CW + 1])
        arg = pair("arg", [F, 2, CW])
        ex = pair("ex", [P, 2, CW])
        sums2 = pair("sums", [P, CW])
        rt = pair("rt", [P, CH, 2, F])
        quo = pair("quo", [P, CH, F])
        inv = pair("inv", [P, CH, F])
        rows_in = [sem(f"rows_in{k}") for k in range(4)]
        side_in = [sem(f"side_in{k}") for k in range(4)]
        (idx_ready, started, encoded, cold_ready, hot_ready, w1_ready, logits, max_made, edge_copied, kept_args, args, exps,
         values, summed, back, rt_ready, inverted, divided, done) = (
            sem(n) for n in ("idx_ready", "started", "encoded", "cold_ready", "hot_ready", "w1_ready", "logits", "max_made",
                             "edge_copied", "kept_args", "args", "exps", "values", "summed", "back", "rt_ready", "inverted",
                             "divided", "done"))
        block = ctx.enter_context(nc.Block())

        def bank(k):
            return K.ps[:, (4 + k) * BANK:(5 + k) * BANK]

        @block.gpsimd
        def _(pool):
            def rows(c, k, turn):
                pool.wait_ge(idx_ready, c + 1)
                pool.nop(nofuse=True)
                gather(pool, ring[k], idx[k], K.tab_vec, rows_in[k])

            def encode(c, k, turn):
                pool.wait_ge(side_in[k], turn * 48 + 48)
                pool.wait_ge(rows_in[k], turn * (16 * CH) + 16 * CH)
                both = ring[k][:, :, :].rearrange("p s (t c) -> p s t c", t=2)
                pool.tensor_tensor(both, both, enc[k][:, :].rearrange("p (s c) -> p s c", c=F).unsqueeze(2).broadcast_to(
                    [P, CH, 2, F]), ALU.add).then_inc(encoded, 1)
            pipeline(pool, [(2, encode, 4), (0, rows, 4)])

        @block.sync
        def _(sp):
            def load(c, k, turn):
                sp.wait_ge(args, c + 1)
                sp.dma_start(dlb[k][:, :], bcast_chunk(K.dl_rows[bass.ds(c * CH, CH), :], P)).then_inc(side_in[k], 16)
                sp.dma_start(pen[k][:, :], bcast_chunk(K.pen_rows[bass.ds(c * CH, CH), :], F)).then_inc(side_in[k], 16)
                sp.dma_start(enc[k][:, :].rearrange("p (s c) -> p s c", c=F), enc_chunk(K, c)).then_inc(side_in[k], 16)
            pipeline(sp, [(0, load, 4)])

        @block.vector
        def _(v):
            v.memset(mrun[1][:, :], -BIG).then_inc(started, 1)
            v.memset(sums2[1][:, :], 0.0).then_inc(started, 1)
            v.wait_ge(started, 2)
            v.sem_inc(args, 4)
            v.sem_inc(summed, 2)
            def indices(c, k, turn):
                if not (isinstance(c, int) and c < 4):
                    v.wait_ge(logits, c - 1)
                v.tensor_copy(idx[k][:, :], K.src_idx[:, bass.ds(c * CH, CH)]).then_inc(idx_ready, 1)

            def targets(c, k, turn):
                v.wait_ge(logits, c + 1)
                v.wait_ge(side_in[k], turn * 48 + 48)
                v.tensor_scalar(cold[k % 2][:, :], dlb[k][:, :], K.iota_part[:, 0:1], None, ALU.is_equal).then_inc(cold_ready, 1)

            def maxima(c, k, turn):
                v.wait_ge(logits, c + 3)
                if not (isinstance(c, int) and c < 1):
                    v.wait_ge(edge_copied, c)
                v.tensor_tensor_scan(mrun[k % 2][:, 1:CW + 1], pen[k][:, :], bank(k % 2)[0:F, :],
                                     mrun[1 - k % 2][:, CW:CW + 1], ALU.add, ALU.max).then_inc(max_made, 1)

            def first_column(c, k, turn):
                v.tensor_copy(mrun[k][:, 0:1], mrun[1 - k][:, CW:CW + 1]).then_inc(edge_copied, 1)

            def keep_or_restart(c, k, turn):
                v.wait_ge(max_made, c + 1)
                v.wait_ge(edge_copied, c + 1)
                if not (isinstance(c, int) and c < 2):
                    v.wait_ge(exps, c - 1)
                v.tensor_tensor(arg[k % 2][:, 0, :], mrun[k % 2][:, 0:CW], pen[k][:, :], ALU.add).then_inc(kept_args, 1)

            def logit_args(c, k, turn):
                v.tensor_tensor(arg[k][:, 1, :], bank(k)[0:F, :], mrun[k][:, 1:CW + 1], ALU.subtract)

            def keep_args(c, k, turn):
                v.wait_ge(kept_args, c + 1)
                v.tensor_tensor(arg[k][:, 0, :], arg[k][:, 0, :], mrun[k][:, 1:CW + 1], ALU.subtract).then_inc(args, 1)

            def weigh(c, k, turn):
                v.wait_ge(exps, c + 1)
                v.tensor_tensor(ex[k][F:P, 1, :], ex[k][F:P, 1, :], bank(k)[F:P, :], ALU.mult).then_inc(values, 1)

            def add_up(c, k, turn):
                v.wait_ge(values, c + 1)
                v.wait_ge(back, c + 1)
                v.wait_ge(summed, c + 2)
                v.tensor_tensor_scan(sums2[k][:, :], ex[k][:, 0, :], ex[k][:, 1, :], sums2[1 - k][:, CW - 1:CW],
                                     ALU.mult, ALU.add).then_inc(summed, 1)

            def ends(c, k, turn):
                v.wait_ge(done, c + 1)
                onehot(v, hot[k][:, :, :], K.iota_row[:, :], K.dl_end[:, bass.ds(c * CH, CH)]).then_inc(hot_ready, 1)

            def invert(c, k, turn):
                v.wait_ge(rt_ready, c + 1)
                if not (isinstance(c, int) and c < 2):
                    v.wait_ge(divided, c - 1)
                v.reciprocal(inv[k][:, :, :], rt[k][:, :, 0, :]).then_inc(inverted, 1)

            def divide(c, k, turn):
                v.wait_ge(inverted, c + 1)
                v.wait_ge(done, c + 1)
                v.tensor_tensor(quo[k][:, :, :], inv[k][:, :, :], rt[k][:, :, 1, :], ALU.mult).then_inc(divided, 1)
            pipeline(v, [(0, indices, 4), (2, targets, 4), (7, divide), (4, weigh), (3, maxima, 4), (3, first_column), (4, add_up),
                         (3, keep_or_restart, 4), (3, logit_args), (3, keep_args), (6, ends), (6, invert)])

        @block.scalar
        def _(act):
            blocks = SlotBlocks(nc, K, act)

            def targets(c, k, turn):
                at = blocks.now()
                act.wait_ge(logits, c + 1)
                for j in range(CH):
                    act.copy(w1[k][:, j, :], proj[:, bass.ds(at[j], 1), 2, :].rearrange("p b o -> p (b o)")
                             ).then_inc(w1_ready, 1)

            def exponentials(c, k, turn):
                act.wait_ge(args, c + 5)
                act.wait_ge(summed, c + 1)
                for half in range(2):
                    ins = act.activation(ex[k][half * F:(half + 1) * F, :, :], arg[k][:, :, :], ACT.Exp)
                ins.then_inc(exps, 1)

            def by_edge(c, k, turn):
                act.wait_ge(back, c + 3)
                if not (isinstance(c, int) and c < 2):
                    act.wait_ge(divided, c - 1)
                act.copy(rt[k][:, :, :, :].rearrange("p s t c -> p (s t c)"), K.ps[:, (6 + k) * BANK:(7 + k) * BANK]
                         ).then_inc(rt_ready, 1)
            pipeline(act, [(0, targets), (1, exponentials), (3, by_edge)], blocks=blocks)

        @block.tensor
        def _(pe):
            clear_banks(pe, K, 0, 4).then_inc(done, 2)
            pe.sem_inc(logits, 2)
            pe.sem_inc(back, 2)
            blocks = SlotBlocks(nc, K, pe, back=5)

            def products(c, r, turn):
                k = r % 2
                pe.wait_ge(encoded, c + 1)
                if not (isinstance(c, int) and c < 2):
                    pe.wait_ge(values, c - 1)
                pe.wait_ge(cold_ready, c + 1)
                pe.wait_ge(w1_ready, c * CH + CH)
                pe.nop(nofuse=True)
                for j in range(CH):
                    cols = bank(k)[:, j * P:(j + 1) * P]
                    pe.matmul(cols, ring[r][:, j, :], K.ident[:, :], start=True, stop=False, skip_group_check=True)
                    ins = pe.matmul(cols[0:F, :], w1[k][:, j, :], cold[k][:, j * P:(j + 1) * P], start=False, stop=True,
                                    skip_group_check=True)
                ins.then_inc(logits, 1)

            def turn_back(c, k, turn):
                pe.wait_ge(summed, c + 3)
                if not (isinstance(c, int) and c < 2):
                    pe.wait_ge(rt_ready, c - 1)
                pe.nop(nofuse=True)
                for j in range(CH):
                    o = (6 + k) * BANK + j * P
                    ins = pe.transpose(K.ps[:, o:o + P], sums2[k][:, j * P:(j + 1) * P], K.ident[:, :])
                ins.then_inc(back, 1)

            def pick_ends(c, k, turn):
                at = blocks.now()
                pe.wait_ge(divided, c + 1)
                pe.wait_ge(hot_ready, c + 1)
                pe.nop(nofuse=True)
                for j in range(CH):
                    ins = pe.matmul(K.ps[:, bass.ds(at[j] * F, F)], hot[k][:, j, :], quo[k][:, j, :], start=False,
                                    stop=False, skip_group_check=True)
                ins.then_inc(done, 1)
            pipeline(pe, [(0, products, 4), (3, turn_back), (5, pick_ends)], blocks=blocks)



def build(nc, A, out):
    K = Space()
    ctx = ExitStack()
    with ctx:
        def sb(name, shape, dt=FP32):
            return ctx.enter_context(nc.sbuf_tensor(name, shape, dt))

        def dram(name, shape, dt=FP32):
            return nc.dram_tensor(name, shape, dt, kind="Internal").ap()

        K.ps = ctx.enter_context(nc.psum_tensor("ps", [P, 8 * BANK], FP32))
        K.ident = sb("ident", [P, P])
        K.iota_row = sb("iota_row", [P, P])
        K.iota_part = sb("iota_part", [P, 1])
        K.ones = sb("ones", [P, P])
        K.zeros = sb("zeros", [P, BANK])
        K.dl = sb("dl", [P, SLOTS])
        K.dl_end = sb("dl_end", [P, SLOTS])
        K.src_idx = sb("src_idx", [P, SLOTS], I32)
        K.rel_idx = sb("rel_idx", [P, SLOTS], I32)
        K.blk_i = sb("blk_i", [P, SLOTS], I32)
        K.x = sb("x_nodes", [P, NB, F])
        K.deg, K.deg1, K.has, K.rdeg, K.dis = (sb(n, [P, NB]) for n in ("deg", "deg1", "has", "rdeg", "dis"))
        K.dl_rows = dram("dl_rows", [SLOTS, P])
        K.pen_rows = dram("pen_rows", [SLOTS, P])
        K.attr_rows = dram("attr_rows", [3, SLOTS, P])
        K.tab64 = dram("tab64", [NB * P, F])
        K.tab_gat1 = dram("tab_gat1", [NB * P, F + HEADS])
        K.tab_gat2 = dram("tab_gat2", [NB * P, F + 1])
        K.tab_rel = dram("tab_rel", [NB * P, REL * F])
        K.tab_vec = dram("tab_vec", [NB * P, 2 * F])
        K.rstd_rows = dram("rstd_rows", [SLOTS, P])
        K.enc = dram("enc", [P, SLOTS * F])
        with nc.cleanup_on_exit():
            build_slots(nc, K, A["dst"], A["src"], A["edge_type_32"], A["edge_attr_3"])
            count_degrees(nc, K)
        K.sq_var = sb("sq_var", [P, SLOTS])
        K.gb2 = sb("gb2", [P, 2, F])
        with nc.cleanup_on_exit(), ExitStack() as c:
            enc = EdgeWeights(nc, K, A, c)
            appnp(nc, K, A["x"], A["L0_gnn_alpha"], enc)
        with nc.cleanup_on_exit():
            gat(nc, K, A)
        with nc.cleanup_on_exit():
            relational(nc, K, A)
        with nc.cleanup_on_exit():
            vector_attention(nc, K, A)
        store_out(nc, K, out)


_INS = ['x', 'src', 'dst', 'edge_attr_3', 'edge_type_32', 'L0_gnn_alpha', 'L1_gnn_W1', 'L1_gnn_a_src1', 'L1_gnn_a_dst1',
        'L1_gnn_b1', 'L1_gnn_W2', 'L1_gnn_a_src2', 'L1_gnn_a_dst2', 'L1_gnn_b2', 'L2_gnn_basis', 'L2_gnn_coeff',
        'L2_gnn_self_weight', 'L2_gnn_bias', 'L3_gnn_Wd1', 'L3_gnn_bd1', 'L3_gnn_g1', 'L3_gnn_b1', 'L3_gnn_Wd2',
        'L3_gnn_bd2', 'L3_gnn_g2', 'L3_gnn_b2', 'L3_gnn_W1', 'L3_gnn_W2', 'L3_gnn_W3']


def kernel(**inputs):
    import numpy as _np
    import concourse.bacc as _bacc
    from concourse import mybir as _mybir
    from concourse.bass_utils import run_bass_kernel_spmd as _run

    nc = _bacc.Bacc("TRN2", target_bir_lowering=False, num_devices=1)
    arrays, args = {}, {}
    for name in _INS:
        a = _np.ascontiguousarray(inputs[name])
        arrays[f"in_{name}_dram"] = a
        args[name] = nc.dram_tensor(f"in_{name}_dram", a.shape, _mybir.dt.from_np(a.dtype), kind="ExternalInput").ap()
    out = nc.dram_tensor("out_0_dram", (N, F), FP32, kind="ExternalOutput").ap()
    build(nc, args, out)
    r = _run(nc, [arrays], core_ids=[0])
    return r.results[0]["out_0_dram"]
```
